# Optimizing a Trainium2 kernel written in Bass

```python
import numpy as np
import jax
import jax.numpy as jnp

def _softmax(x, axis=-1):
    return jax.nn.softmax(x, axis=axis)

def _gelu(x):
    return jax.nn.gelu(x, approximate=True)

def _silu(x):
    return jax.nn.silu(x)

def _sigmoid(x):
    return jax.nn.sigmoid(x)

def _layernorm(x, axis=-1, eps=1e-05):
    m = jnp.mean(x, axis=axis, keepdims=True)
    v = jnp.var(x, axis=axis, keepdims=True)
    return (x - m) / jnp.sqrt(v + eps)

def _scatter_add(tgt, idx, src, axis=0):
    return tgt.at[idx].add(src)

def _segment_sum(src, seg, n):
    return jax.ops.segment_sum(src, seg, n)
kernel_name = 'mk_adaln_d1_jaxref_r4_bcd5c7'

def setup_inputs(seed: int=0):
    np.random.seed(seed)
    _w = jnp.asarray

    def _L0_attn_setup():
        import jax, jax.numpy as jnp
        import numpy as np
        import math
        D_MODEL = 256
        N_HEADS = 16
        D_K = D_MODEL // N_HEADS
        MAX_REL = 32
        key = jax.random.key(seed)
        ks = jax.random.split(key, 8)
        B, S = (8, 256)
        x = jax.random.normal(ks[0], (B, S, D_MODEL), dtype=jnp.float32)
        scale = 1.0 / math.sqrt(D_MODEL)
        Wq = jax.random.normal(ks[1], (D_MODEL, D_MODEL), dtype=jnp.float32) * scale
        Wk = jax.random.normal(ks[2], (D_MODEL, D_MODEL), dtype=jnp.float32) * scale
        Wv = jax.random.normal(ks[3], (D_MODEL, D_MODEL), dtype=jnp.float32) * scale
        Wo = jax.random.normal(ks[4], (D_MODEL, D_MODEL), dtype=jnp.float32) * scale
        b_o = jnp.zeros((D_MODEL,), dtype=jnp.float32)
        rel_k_emb = jax.random.normal(ks[5], (2 * MAX_REL + 1, D_K), dtype=jnp.float32) * 0.02
        rel_v_emb = jax.random.normal(ks[6], (2 * MAX_REL + 1, D_K), dtype=jnp.float32) * 0.02
        return {'x': x, 'Wq': Wq, 'Wk': Wk, 'Wv': Wv, 'Wo': Wo, 'b_o': b_o, 'rel_k_emb': rel_k_emb, 'rel_v_emb': rel_v_emb}
    _L0_attn_in = _L0_attn_setup()

    def _L0_ffn_setup():
        import jax, jax.numpy as jnp
        import numpy as np
        CAPACITY_FACTOR = 0.5
        key = jax.random.key(seed)
        ks = jax.random.split(key, 5)
        B, S, D, F = (4, 1024, 256, 1024)
        scale_in = 1.0 / np.sqrt(D)
        scale_ff = 1.0 / np.sqrt(F)
        return {'hidden_states': jax.random.normal(ks[0], (B, S, D), dtype=jnp.float32), 'w_router': jax.random.normal(ks[1], (D,), dtype=jnp.float32) * scale_in, 'W1': jax.random.normal(ks[2], (D, F), dtype=jnp.float32) * scale_in, 'b1': jnp.zeros((F,), dtype=jnp.float32), 'W2': jax.random.normal(ks[3], (F, D), dtype=jnp.float32) * scale_ff, 'b2': jnp.zeros((D,), dtype=jnp.float32)}
    _L0_ffn_in = _L0_ffn_setup()
    _L0_c = _w((lambda *s: np.random.randn(*s).astype(np.float32) * 0.05)(16, 256))
    _L0_wmod = _w((lambda *s: np.random.randn(*s).astype(np.float32) * 0.05)(256, 6 * 256) * 256 ** (-0.5))
    _d = {'L0_attn_x': _L0_attn_in['x'], 'L0_attn_Wq': _L0_attn_in['Wq'], 'L0_attn_Wk': _L0_attn_in['Wk'], 'L0_attn_Wv': _L0_attn_in['Wv'], 'L0_attn_Wo': _L0_attn_in['Wo'], 'L0_attn_b_o': _L0_attn_in['b_o'], 'L0_attn_rel_k_emb': _L0_attn_in['rel_k_emb'], 'L0_attn_rel_v_emb': _L0_attn_in['rel_v_emb'], 'L0_ffn_w_router': _L0_ffn_in['w_router'], 'L0_ffn_W1': _L0_ffn_in['W1'], 'L0_ffn_b1': _L0_ffn_in['b1'], 'L0_ffn_W2': _L0_ffn_in['W2'], 'L0_ffn_b2': _L0_ffn_in['b2'], 'L0_c': _L0_c, 'L0_wmod': _L0_wmod}
    _x0 = _d['L0_attn_x']
    _d['L0_attn_x'] = jax.random.normal(jax.random.fold_in(jax.random.key(seed), 1), (16, 1024, 256), dtype=_x0.dtype)
    del _x0
    return _d

def reference(L0_attn_x, L0_attn_Wq, L0_attn_Wk, L0_attn_Wv, L0_attn_Wo, L0_attn_b_o, L0_attn_rel_k_emb, L0_attn_rel_v_emb, L0_ffn_w_router, L0_ffn_W1, L0_ffn_b1, L0_ffn_W2, L0_ffn_b2, L0_c, L0_wmod):

    def _L0_attn_ref(x, Wq, Wk, Wv, Wo, b_o, rel_k_emb, rel_v_emb):
        import jax, jax.numpy as jnp
        import numpy as np
        import math
        D_MODEL = 256
        N_HEADS = 16
        D_K = D_MODEL // N_HEADS
        MAX_REL = 32
        B, S, D = x.shape
        H, dk = (N_HEADS, D_K)
        inv_sqrt_dk = 1.0 / math.sqrt(dk)
        Q = (x @ Wq.T).reshape(B, S, H, dk)
        K = (x @ Wk.T).reshape(B, S, H, dk)
        V = (x @ Wv.T).reshape(B, S, H, dk)
        pos = jnp.arange(S)
        rel_idx = jnp.clip(pos[None, :] - pos[:, None], -MAX_REL, MAX_REL) + MAX_REL
        rel_k = rel_k_emb[rel_idx]
        rel_v = rel_v_emb[rel_idx]
        scores = jnp.einsum('bihd,bjhd->bhij', Q, K) * inv_sqrt_dk
        scores = scores + jnp.einsum('bihd,ijd->bhij', Q, rel_k) * inv_sqrt_dk
        attn = jax.nn.softmax(scores, axis=-1)
        ctx = jnp.einsum('bhij,bjhd->bihd', attn, V)
        ctx = ctx + jnp.einsum('bhij,ijd->bihd', attn, rel_v)
        ctx = ctx.reshape(B, S, D)
        out = ctx @ Wo.T + b_o
        return out

    def _L0_ffn_ref(hidden_states, w_router, W1, b1, W2, b2):
        import jax, jax.numpy as jnp
        import numpy as np
        CAPACITY_FACTOR = 0.5
        'Mixture-of-Depths block: route top-k tokens through an FFN inner block,\n            scatter back with sigmoid router weights; bypassed tokens pass through.'
        B, S, D = hidden_states.shape
        k = int(S * CAPACITY_FACTOR)
        scores = jnp.einsum('bsd,d->bs', hidden_states, w_router)
        top_scores, top_idx = jax.lax.top_k(scores, k)
        weights = jax.nn.sigmoid(top_scores)
        selected = jnp.take_along_axis(hidden_states, top_idx[:, :, None], axis=1)
        h = jax.nn.gelu(jnp.einsum('bkd,df->bkf', selected, W1) + b1)
        processed = jnp.einsum('bkf,fd->bkd', h, W2) + b2
        update = weights[:, :, None] * processed

        def scatter_one(xb, ib, ub):
            return xb.at[ib].add(ub)
        output = jax.vmap(scatter_one)(hidden_states, top_idx, update)
        return output
    x = L0_attn_x
    mod = (_silu(L0_c) @ L0_wmod).reshape(L0_c.shape[0], 6, 1, -1)
    sa, ca, ga, sb, cb, gb = (mod[:, 0], mod[:, 1], mod[:, 2], mod[:, 3], mod[:, 4], mod[:, 5])
    ga = (2 * (ga >= 0) - 1) * jnp.maximum(jnp.abs(ga), 0.25)
    gb = (2 * (gb >= 0) - 1) * jnp.maximum(jnp.abs(gb), 0.25)
    h = _layernorm(x, axis=-1) * (1 + ca) + sa
    x = x + ga * _L0_attn_ref(h, L0_attn_Wq, L0_attn_Wk, L0_attn_Wv, L0_attn_Wo, L0_attn_b_o, L0_attn_rel_k_emb, L0_attn_rel_v_emb)
    h = _layernorm(x, axis=-1) * (1 + cb) + sb
    x = x + gb * _L0_ffn_ref(h, L0_ffn_w_router, L0_ffn_W1, L0_ffn_b1, L0_ffn_W2, L0_ffn_b2)
    return x

_drawn_inputs = setup_inputs


def setup_inputs(seed=0):
    import zlib

    import numpy as np

    out = dict(_drawn_inputs(seed))
    spreads = {'L0_attn_b_o': (0.0, 0.317), 'L0_ffn_b1': (0.0, 0.8), 'L0_ffn_b2': (0.0, 0.706)}
    factors = {'L0_attn_Wq': 2.897,
     'L0_attn_Wk': 2.84,
     'L0_attn_rel_k_emb': 8.0,
     'L0_attn_rel_v_emb': 8.0}
    for name, (base, spread) in spreads.items():
        noise = np.random.default_rng([zlib.crc32(name.encode()), seed]).standard_normal(out[name].shape)
        drawn = base * np.exp(spread * noise) if base else spread * noise
        out[name] = jnp.asarray(drawn.astype(out[name].dtype))
    for name, factor in factors.items():
        out[name] = (out[name] * factor).astype(out[name].dtype)
    return out
```

```python
from contextlib import ExitStack

import concourse.bass as bass
from concourse import mybir

F32 = mybir.dt.float32
BF16 = mybir.dt.bfloat16
ALU = mybir.AluOpType
ACT = mybir.ActivationFunctionType
AX = mybir.AxisListType.X

P = 128
B, S, D = 16, 1024, 256
H, DK = 16, 16
R = 32
NR = 2 * R + 1
KT = D // P
NB = S // P
HB = 4
NG = H // HB
CH = 512
NC = S // CH
XW = P + 2 * R
F = 1024
FT = F // P
TOPK = S // 2
EPS = 1e-5
SCALE = 1.0 / 4.0
Q_PARTS = (0, 1, 2, 0, 1, 0)
K_PARTS = (0, 1, 0, 1, 0, 2)
ROWS = 6 * DK
M_ROWS = ROWS + 2
C_ROWS = ROWS + 5


def scratch(nc):
    def t(name, shape, dt=F32):
        return nc.dram_tensor(name, shape, dt).ap()
    return dict(
        mod_row=t("mod_row", [B, 4 * D]),
        mod_col=t("mod_col", [B, P, 2 * KT]),
        q=t("q_parts", [B * NG, 3, DK, HB * S], BF16),
        k=t("k_parts", [B * NG, 3, DK, HB * S], BF16),
        c=t("c_parts", [B * NG, 5, HB * S], BF16),
        v=t("v_both", [B * NG, NB, P, 2 * HB * 32]),
        ctx=t("ctx", [B * NG, P, S]),
        relv=t("relv_ext", [XW + P, DK]),
    )




def setup_project(nc, io, dr, w):
    with ExitStack() as ctx:
        def tmp(name, shape, dt=F32):
            return ctx.enter_context(nc.sbuf_tensor(name, shape, dt))

        wnat = tmp("wnat", [P, 3, KT, D])
        cT = tmp("cT", [P, KT, B])
        cth = tmp("cth", [P, KT, B])
        csl = tmp("csl", [P, KT, B])
        wmod = tmp("wmod", [P, KT, 6 * D])
        mod = tmp("mod", [B, 6 * D])
        sgn = tmp("sgn", [B, 2, D])
        modr = tmp("modr", [B, 4, D])
        modc = tmp("modc", [P, B, 2 * KT])
        dl = tmp("dl", [P, DK])
        wcm = tmp("wcm", [P, KT, D])
        zero = tmp("zero", [P, 2 * HB * S], BF16)
        pt = [ctx.enter_context(nc.psum_tensor(f"pt{i}", [P, CH], F32)) for i in range(8)]
        loaded = ctx.enter_context(nc.semaphore("loaded"))
        ident_z = ctx.enter_context(nc.semaphore("ident_z"))
        ident_ok = ctx.enter_context(nc.semaphore("ident_ok"))
        zero_ok = ctx.enter_context(nc.semaphore("zero_ok"))
        tanh_ok = ctx.enter_context(nc.semaphore("tanh_ok"))
        dve = ctx.enter_context(nc.semaphore("dve_step"))
        turned = ctx.enter_context(nc.semaphore("turned"))
        modded = ctx.enter_context(nc.semaphore("modded"))
        stored = ctx.enter_context(nc.semaphore("stored"))
        silu_ok = ctx.enter_context(nc.semaphore("silu_ok"))
        mod_ok = ctx.enter_context(nc.semaphore("mod_ok"))
        blk = ctx.enter_context(nc.Block())
        N_LOADS = 11

        @blk.sync
        def _(sp):
            for n, name in enumerate(("Wq", "Wk", "Wv")):
                sp.dma_start(wnat[:, n], io[name].rearrange("(t p) k -> p t k", p=P)).then_inc(loaded, 16)
            for kt in range(KT):
                sp.dma_start(cT[:, kt], io["c"].rearrange("b (t p) -> t p b", p=P)[kt],
                             allow_slow_non_contiguous=True).then_inc(loaded, 16)
            sp.dma_start(wmod[:], io["wmod"].rearrange("(t p) n -> p t n", p=P)).then_inc(loaded, 16)
            rk, rv = io["rel_k"], io["rel_v"]
            sp.dma_start(w["rk_bc"][:, 0], bass.AP(rk.tensor, 0, [[0, P], [1, DK]])).then_inc(loaded, 16)
            sp.dma_start(w["rk_bc"][:, 1], bass.AP(rk.tensor, 2 * R * DK, [[0, P], [1, DK]])).then_inc(loaded, 16)
            sp.dma_start(w["rv_bc"][:], bass.AP(rv.tensor, 0, [[0, P], [2 * R * DK, 2], [1, DK]])).then_inc(loaded, 16)
            for g in range(2):
                sp.dma_start(w["rk_col"][g * 64:(g + 1) * 64], bass.AP(rk.tensor, 0, [[1, DK], [0, HB], [1, 1]]),
                             allow_slow_non_contiguous=True).then_inc(loaded, 16)
            ext = dr["relv"]
            sp.dma_start(ext[0:P - 1], bass.AP(rv.tensor, 0, [[0, P - 1], [1, DK]])).then_inc(stored, 16)
            sp.dma_start(ext[P - 1:P - 1 + NR], rv[:, :]).then_inc(stored, 16)
            rest = XW + P - (P - 1 + NR)
            sp.dma_start(ext[P - 1 + NR:], bass.AP(rv.tensor, 2 * R * DK, [[0, rest], [1, DK]])).then_inc(stored, 16)
            sp.wait_ge(zero_ok, 2)
            sp.dma_start(dr["c"][:, 0:2, :].rearrange("g r t -> g (r t)"), zero[0:B * NG, :]).then_inc(stored, 16)
            sp.wait_ge(mod_ok, 2)
            sp.dma_start(dr["mod_row"], modr[:].rearrange("b f d -> b (f d)")).then_inc(stored, 16)
            sp.dma_start(dr["mod_col"].rearrange("b p c -> p b c"), modc[:],
                         allow_slow_non_contiguous=True).then_inc(stored, 16)
            sp.wait_ge(stored, 16 * (3 + 1 + 2))

        @blk.gpsimd
        def _(pool):
            pool.memset(w["ident"][:], 0.0).then_inc(ident_z, 1)
            pool.wait_ge(ident_z, 1)
            pool.affine_select(out=w["ident"][:], in_=w["ident"][:], compare_op=ALU.not_equal, fill=1.0,
                               base=0, pattern=[[-1, P]], channel_multiplier=1).then_inc(ident_ok, 1)
            pool.memset(zero[:], 0.0).then_inc(zero_ok, 1)
            pool.memset(w["mhalf"][:], -0.5).then_inc(zero_ok, 1)

        @blk.scalar
        def _(act):
            act.wait_ge(loaded, 16 * N_LOADS)
            act.activation(cth[:], cT[:], ACT.Tanh, scale=0.5).then_inc(tanh_ok, 1)

        @blk.tensor
        def _(pe):
            pe.wait_ge(loaded, 16 * N_LOADS)
            pe.wait_ge(ident_ok, 1)
            for n in range(3):
                for kt in range(KT):
                    for nt in range(KT):
                        mm = pe.transpose(pt[n * KT + kt][:, nt * P:(nt + 1) * P],
                                          wnat[:, n, nt, kt * P:(kt + 1) * P], w["ident"][:])
            mm.then_inc(turned, 1)
            pe.wait_ge(silu_ok, 1)
            for n in range(3):
                for kt in range(KT):
                    mm = pe.matmul(pt[(6, 7, 0)[n]][0:B, :], csl[:, kt], wmod[:, kt, n * CH:(n + 1) * CH],
                                   start=(kt == 0), stop=(kt == KT - 1))
            for n in range(2 * KT):
                for kt in range(KT):
                    mm = pe.matmul(pt[1][:, n * B:(n + 1) * B], wmod[:, kt, n * P:(n + 1) * P], csl[:, kt],
                                   start=(kt == 0), stop=(kt == KT - 1))
            mm.then_inc(modded, 1)

        @blk.vector
        def _(v):
            steps = 0

            def done(ins):
                nonlocal steps
                steps += 1
                ins.then_inc(dve, 1)
                v.wait_ge(dve, steps)

            v.wait_ge(loaded, 16 * N_LOADS)
            done(v.tensor_tensor(dl[:], w["rk_bc"][:, 1], w["rk_bc"][:, 0], ALU.subtract))
            v.wait_ge(turned, 1)
            for n, name in enumerate(("wqT", "wkT")):
                for kt in range(KT):
                    src = pt[n * KT + kt][:, 0:D].rearrange("k (g h d) -> k g d h", g=NG, h=HB)
                    for g in range(NG):
                        done(v.tensor_copy(w[name][:, kt, g * 64:(g + 1) * 64].rearrange("k (d h) -> k d h", h=HB),
                                           src[:, g]))
            for kt in range(KT):
                done(v.tensor_copy(w["wvT"][:, kt], pt[2 * KT + kt][:, 0:D]))
            for kt in range(KT):
                for h in range(H):
                    c0 = h * DK
                    done(v.tensor_tensor(wcm[:, kt, c0:c0 + DK], pt[kt][:, c0:c0 + DK], dl[:], ALU.mult))
                done(v.tensor_reduce(w["wcT"][:, kt], wcm[:, kt].rearrange("k (h d) -> k h d", d=DK), AX, ALU.add))
            v.wait_ge(tanh_ok, 1)
            done(v.tensor_scalar(cth[:], cth[:], 0.5, 0.5, ALU.mult, ALU.add))
            v.tensor_tensor(csl[:], cth[:], cT[:], ALU.mult).then_inc(silu_ok, 1)
            v.wait_ge(modded, 1)
            for n in range(3):
                done(v.tensor_copy(mod[:, n * CH:(n + 1) * CH], pt[(6, 7, 0)[n]][0:B, :]))
            for n, src, dst in ((0, 2, 0), (1, 5, 3)):
                g = mod[:, src * D:(src + 1) * D]
                done(v.tensor_scalar(sgn[:, n], g, 0.0, 2.0, ALU.is_ge, ALU.mult))
                done(v.tensor_scalar(sgn[:, n], sgn[:, n], -1.0, None, ALU.add))
                done(v.tensor_scalar(modr[:, dst], g, -1.0, None, ALU.mult))
                done(v.tensor_tensor(modr[:, dst], modr[:, dst], g, ALU.max))
                done(v.tensor_scalar(modr[:, dst], modr[:, dst], 0.25, None, ALU.max))
                done(v.tensor_tensor(modr[:, dst], modr[:, dst], sgn[:, n], ALU.mult))
            done(v.tensor_copy(modr[:, 1], mod[:, 3 * D:4 * D]))
            v.tensor_scalar(modr[:, 2], mod[:, 4 * D:5 * D], 1.0, None, ALU.add).then_inc(mod_ok, 1)
            mc = pt[1][:, 0:2 * KT * B].rearrange("p (c b) -> p b c", b=B)
            done(v.tensor_copy(modc[:, :, 0:KT], mc[:, :, 0:KT]))
            v.tensor_scalar(modc[:, :, KT:2 * KT], mc[:, :, KT:2 * KT], 1.0, None, ALU.add).then_inc(mod_ok, 1)


def project(nc, io, dr, w, nbatch=B):
    with ExitStack() as ctx:
        def sb(name, shape, dt=F32):
            return ctx.enter_context(nc.sbuf_tensor(name, shape, dt))

        def sem(name):
            return ctx.enter_context(nc.semaphore(name))

        xin = sb("xin", [P, 2, NB, D])
        mcol = sb("mcol", [P, 2, 2 * KT])
        stats = sb("stats", [P, NB, 6])
        mv = sb("mv", [P, NB, 2])
        veps = sb("veps", [P, NB])
        rstd = sb("rstd", [P, NB])
        nmr = sb("nmr", [P, NB])
        nrm = sb("nrm", [P, NB, D])
        hT = sb("hT", [P, 2, KT, S])
        part1 = sb("part1", [P, 2, 5, S], BF16)
        part2 = sb("part2", [P, 2, 5, S], BF16)
        part3 = sb("part3", [P, 2, 5, S], BF16)
        rest = sb("rest", [P, 2, CH])
        vout = sb("vout", [P, 2, 2, NG, 2, HB, 32])
        NP_ = 7
        ps = [ctx.enter_context(nc.psum_tensor(f"ps{i}", [P, CH], F32)) for i in range(NP_)]
        tp = ctx.enter_context(nc.psum_tensor("tp", [P, CH], F32))

        x_in = [sem(f"x_in{i}") for i in range(2)]
        m_in = [sem(f"m_in{i}") for i in range(2)]
        x_free, m_free = sem("x_free"), sem("m_free")
        normed, nrm_free = sem("normed"), sem("nrm_free")
        tp_full, tp_free = sem("tp_full"), sem("tp_free")
        qkc_full, v_full, ps_free, ps_v_free = sem("qkc_full"), sem("v_full"), sem("ps_free"), sem("ps_v_free")
        part1_ok, rest_ok, rest_free = sem("part1_ok"), sem("rest_ok"), sem("rest_free")
        pool_step, dve_step = sem("pool_step"), sem("dve_step2")
        parts_ok, parts_free = sem("parts_ok"), sem("parts_free")
        parts_out = [sem(f"parts_out{i}") for i in range(2)]
        v_ok = sem("v_ok")
        v_out = [sem(f"v_out{i}") for i in range(2)]
        ones_ok, var_ok, rstd_ok = sem("ones_ok"), sem("var_ok"), sem("rstd_ok")
        blk = ctx.enter_context(nc.Block())

        QK = 8
        FILLS = QK + NC + NB // 2
        bank = lambda f: ps[f % NP_]
        STORES = 3 * (QK // 2) + 3

        def load(sp, b, p):
            sp.dma_start(xin[:, p], io["x"][bass.ds(b, 1)].rearrange("o (t p) d -> p (o t) d", p=P)).then_inc(x_in[p], 16)
            sp.dma_start(mcol[:, p], dr["mod_col"][bass.ds(b, 1)].rearrange("o p c -> (o p) c")).then_inc(m_in[p], 16)

        @blk.sync
        def _(sp):
            load(sp, 0, 0)

            def step(b, p, last):
                if not last:
                    sp.wait_ge(x_free, 1)
                    sp.wait_ge(m_free, 1)
                    load(sp, b + 1, 1 - p)
                    sp.sem_inc(x_free, -1)
                    sp.sem_inc(m_free, -1)
                sp.wait_ge(parts_out[p], 16 * STORES)
                sp.sem_inc(parts_out[p], -16 * STORES)
                sp.sem_inc(parts_free, 1)
                for m in range(QK // 2):
                    sp.wait_ge(parts_ok, 2 * (m + 1))
                    dst = dr["q"] if m < KT else dr["k"]
                    for n, part in enumerate((part1, part2, part3)):
                        to = dst[bass.ds(b * NG + m % KT * 2, 2), n].rearrange("g d (h t) -> g (d h) t", h=HB)
                        sp.dma_start(to, part[:, p, m]).then_inc(parts_out[p], 16)
                sp.wait_ge(parts_ok, QK + NC)
                for n, part in enumerate((part1, part2, part3)):
                    to = dr["c"][bass.ds(b * NG, NG), 2 + n].rearrange("g (h t) -> g h t", h=HB)
                    sp.dma_start(to, part[0:H, p, 4]).then_inc(parts_out[p], 16)
                sp.sem_inc(parts_ok, -(QK + NC))
                for f in range(NB // 2):
                    sp.wait_ge(v_ok, f + 1)
                    for k in range(2):
                        to = dr["v"][bass.ds(b * NG, NG), 2 * f + k].rearrange("g p c -> p g c")
                        sp.dma_start(to, vout[:, f % 2, k].rearrange("p g r h c -> p g (r h c)")
                                     ).then_inc(v_out[f % 2], 16)
                sp.sem_inc(v_ok, -(NB // 2))

            for p in range(2):
                sp.sem_inc(parts_out[p], 16 * STORES)
            sp.sem_inc(x_free, 1)
            sp.sem_inc(m_free, 1)
            if nbatch > 2:
                with sp.Fori(0, nbatch - 2, 2) as b:
                    for p in range(2):
                        step(b + p, p, False)
            step(nbatch - 2, 0, False)
            step(nbatch - 1, 1, True)
            for p in range(2):
                sp.wait_ge(parts_out[p], 16 * STORES)

        @blk.vector
        def _(v):
            for r in range(2):
                v.memset(vout[:, r, :, :, :, :, DK:32].rearrange("p k g r h c -> p (k g r h) c"), 1.0).then_inc(ones_ok, 1)
            v.wait_ge(ones_ok, 2)
            for r in range(2):
                v.sem_inc(v_out[r], 32)

            def norm(p, first):
                v.wait_ge(x_in[p], 16)
                v.sem_inc(x_in[p], -16)
                for t in range(NB):
                    v.bn_stats(stats[:, t], xin[:, p, t]).then_inc(dve_step, 1)
                v.wait_ge(dve_step, NB)
                for t in range(NB):
                    v.bn_aggr(mv[:, t], stats[:, t]).then_inc(dve_step, 1)
                v.wait_ge(dve_step, 2 * NB)
                v.tensor_scalar(veps[:], mv[:, :, 1], EPS, None, ALU.add).then_inc(var_ok, 1)
                v.wait_ge(rstd_ok, 1)
                v.sem_inc(rstd_ok, -1)
                v.scalar_tensor_tensor(nmr[:], mv[:, :, 0], -1.0, rstd[:], ALU.mult, ALU.mult).then_inc(dve_step, 1)
                v.wait_ge(dve_step, 2 * NB + 1)
                if not first:
                    v.wait_ge(nrm_free, 1)
                    v.sem_inc(nrm_free, -1)
                for t in range(NB):
                    v.tensor_scalar(nrm[:, t], xin[:, p, t], rstd[:, t:t + 1], nmr[:, t:t + 1],
                                    ALU.mult, ALU.add).then_inc(dve_step, 1)
                v.wait_ge(dve_step, 3 * NB + 1)
                v.sem_inc(normed, 1)
                v.sem_inc(x_free, 1)
                v.sem_inc(dve_step, -(3 * NB + 1))

            norm(0, True)

            def step(p, last):
                if not last:
                    norm(1 - p, False)
                for f in range(QK + NC):
                    rows = P if f < QK else H
                    v.wait_ge(part1_ok, f + 1)
                    if f >= 2:
                        v.wait_ge(rest_free, f - 1)
                    col = f % NC * CH
                    first = part1[0:rows, p, f // 2, col:col + CH]
                    if QK // 2 <= f < QK:
                        v.scalar_tensor_tensor(rest[0:rows, f % 2], bank(f)[0:rows, :], w["rk_col"][:, 0:1], first,
                                               ALU.add, ALU.subtract).then_inc(rest_ok, 1)
                    else:
                        v.tensor_tensor(rest[0:rows, f % 2], bank(f)[0:rows, :], first, ALU.subtract).then_inc(rest_ok, 1)
                v.sem_inc(part1_ok, -(QK + NC))
                v.wait_ge(rest_free, QK + NC)
                v.sem_inc(rest_free, -(QK + NC))
                for f in range(NB // 2):
                    v.wait_ge(v_full, f + 1)
                    v.wait_ge(v_out[f % 2], 32)
                    v.sem_inc(v_out[f % 2], -32)
                    src = bank(QK + NC + f)[:, :].rearrange("p (g h d) -> p g h d", g=2 * NG, h=HB)
                    for r in range(2):
                        add = w["rv_bc"][:, r].unsqueeze(1).unsqueeze(1).broadcast_to([P, 2 * NG, HB, DK])
                        to = vout[:, f % 2, :, :, r, :, 0:DK].rearrange("p k g h d -> p (k g) h d")
                        v.tensor_tensor(to, src, add, ALU.add).then_inc(dve_step, 1)
                    v.wait_ge(dve_step, 2 * (f + 1))
                    v.sem_inc(ps_v_free, 1)
                    v.sem_inc(v_ok, 1)
                v.sem_inc(dve_step, -NB)
                v.sem_inc(v_full, -(NB // 2))

            if nbatch > 2:
                with v.Fori(0, nbatch - 2, 2):
                    for p in range(2):
                        step(p, False)
            step(0, False)
            step(1, True)
            for r in range(2):
                v.wait_ge(v_out[r], 32)

        @blk.gpsimd
        def _(pool):
            def root():
                pool.wait_ge(var_ok, 1)
                pool.sem_inc(var_ok, -1)
                pool.tensor_tensor(rstd[:], veps[:], w["mhalf"][:], ALU.pow).then_inc(rstd_ok, 1)

            def step(p, last):
                if not last:
                    root()
                for f in range(QK + NC):
                    rows = P if f < QK else H
                    col = f % NC * CH
                    second = part2[0:rows, p, f // 2, col:col + CH]
                    pool.wait_ge(rest_ok, f + 1)
                    pool.sem_inc(ps_free, 1)
                    pool.tensor_copy(second, rest[0:rows, f % 2]).then_inc(pool_step, 1)
                    pool.wait_ge(pool_step, 2 * f + 1)
                    pool.tensor_tensor(part3[0:rows, p, f // 2, col:col + CH], rest[0:rows, f % 2], second,
                                       ALU.subtract).then_inc(pool_step, 1)
                    pool.wait_ge(pool_step, 2 * f + 2)
                    pool.sem_inc(rest_free, 1)
                    pool.sem_inc(parts_ok, 1)
                pool.sem_inc(rest_ok, -(QK + NC))
                pool.sem_inc(pool_step, -2 * (QK + NC))

            root()
            if nbatch > 2:
                with pool.Fori(0, nbatch - 2, 2):
                    for p in range(2):
                        step(p, False)
            step(0, False)
            step(1, True)

        @blk.scalar
        def _(act):
            def turn(n, p):
                kt, half = n % KT, n // KT
                act.wait_ge(tp_full, n + 1)
                act.activation(hT[:, p, kt, half * CH:(half + 1) * CH], tp[:, :], ACT.Identity,
                               scale=mcol[:, p, KT + kt:KT + kt + 1], bias=mcol[:, p, kt:kt + 1]).then_inc(tp_free, 1)

            def first_use(p):
                act.wait_ge(m_in[p], 16)
                act.sem_inc(m_in[p], -16)

            def split(f, p):
                rows = P if f < QK else H
                col = f % NC * CH
                act.wait_ge(qkc_full, f + 1)
                out, src = part1[0:rows, p, f // 2, col:col + CH], bank(f)[0:rows, :]
                if QK // 2 <= f < QK:
                    act.activation(out, src, ACT.Identity, bias=w["rk_col"][:, 0:1]).then_inc(part1_ok, 1)
                else:
                    act.activation(out, src, ACT.Copy).then_inc(part1_ok, 1)

            def step(p, last):
                act.wait_ge(parts_free, 1)
                act.sem_inc(parts_free, -1)
                if not last:
                    first_use(1 - p)
                for f in range(QK + NC):
                    split(f, p)
                    if f < 2 * KT and not last:
                        turn(f, 1 - p)
                if not last:
                    act.sem_inc(tp_full, -2 * KT)
                act.sem_inc(qkc_full, -(QK + NC))

            first_use(0)
            for n in range(2 * KT):
                turn(n, 0)
            act.sem_inc(tp_full, -2 * KT)
            if nbatch > 2:
                with act.Fori(0, nbatch - 2, 2):
                    for p in range(2):
                        step(p, False)
            step(0, False)
            step(1, True)

        @blk.tensor
        def _(pe):
            def turn(n):
                kt, half = n % KT, n // KT
                if n:
                    pe.wait_ge(tp_free, n)
                for t in range(4):
                    mm = pe.transpose(tp[:, t * P:(t + 1) * P], nrm[:, 4 * half + t, kt * P:(kt + 1) * P], w["ident"][:])
                mm.then_inc(tp_full, 1)

            def fill(f, p):
                if f < QK:
                    m, c = f % (QK // 2) // 2, f % 2
                    wt = w["wqT"] if f < QK // 2 else w["wkT"]
                    for kt in range(KT):
                        mm = pe.matmul(bank(f)[:, :], wt[:, kt, m * P:(m + 1) * P], hT[:, p, kt, c * CH:(c + 1) * CH],
                                       start=(kt == 0), stop=(kt == KT - 1))
                    return mm.then_inc(qkc_full, 1)
                if f < QK + NC:
                    c = f - QK
                    for kt in range(KT):
                        mm = pe.matmul(bank(f)[0:H, :], w["wcT"][:, kt, :], hT[:, p, kt, c * CH:(c + 1) * CH],
                                       start=(kt == 0), stop=(kt == KT - 1))
                    return mm.then_inc(qkc_full, 1)
                for k in range(2):
                    t = 2 * (f - QK - NC) + k
                    for kt in range(KT):
                        mm = pe.matmul(bank(f)[:, k * D:(k + 1) * D], hT[:, p, kt, t * P:(t + 1) * P], w["wvT"][:, kt, :],
                                       start=(kt == 0), stop=(kt == KT - 1))
                return mm.then_inc(v_full, 1)

            for n in range(2 * KT):
                if n == 0:
                    pe.wait_ge(normed, 1)
                turn(n)
            pe.wait_ge(tp_free, 2 * KT)
            pe.sem_inc(tp_free, -2 * KT)
            pe.sem_inc(normed, -1)
            pe.sem_inc(nrm_free, 1)
            pe.sem_inc(m_free, 1)

            def bank_free(f):
                if f == 0:
                    pe.wait_ge(ps_free, QK + NC)
                    pe.sem_inc(ps_free, -(QK + NC))
                elif QK + NC - NP_ <= f < NP_:
                    pe.wait_ge(ps_v_free, f + NP_ - QK - NC + 1)
                    if f == NP_ - 1:
                        pe.sem_inc(ps_v_free, -(NB // 2))
                elif f >= NP_:
                    pe.wait_ge(ps_free, f - NP_ + 1)

            def step(p, last):
                for f in range(FILLS):
                    bank_free(f)
                    fill(f, p)
                    if f < 2 * KT and not last:
                        if f == 0:
                            pe.wait_ge(normed, 1)
                        turn(f)
                if not last:
                    pe.wait_ge(tp_free, 2 * KT)
                    pe.sem_inc(tp_free, -2 * KT)
                    pe.sem_inc(normed, -1)
                    pe.sem_inc(nrm_free, 1)
                    pe.sem_inc(m_free, 1)

            pe.sem_inc(ps_free, QK + NC)
            pe.sem_inc(ps_v_free, NB // 2)
            if nbatch > 2:
                with pe.Fori(0, nbatch - 2, 2):
                    for p in range(2):
                        step(p, False)
            step(0, False)
            step(1, True)



XA = XW - R
TA = XA + P - 1
TB = R + P - 1


def window(jb, c):
    lo, hi = max(jb * P - R, c * CH), min(jb * P + P + R, (c + 1) * CH)
    return (lo, hi) if lo < hi else None


def pieces(jb, c):
    lo, hi, at = c * CH, (c + 1) * CH, jb * P
    found = []
    if lo < at:
        found.append((1, lo, min(hi, at)))
    if hi > at:
        found.append((0, max(lo, at), hi))
    return found


QUADS = [(jb, c) for jb in range(NB) for c in range(NC)]
NQ = len(QUADS)
WIN = [window(jb, c) is not None for jb, c in QUADS]
NWIN = sum(WIN)
NT = NQ * HB
RING = 3
XF = CH // (HB * NB)
DF = XW // XF


def setup_attend(nc, io, dr, w):
    with ExitStack() as ctx:
        def tmp(name, shape, dt=F32):
            return ctx.enter_context(nc.sbuf_tensor(name, shape, dt))
        rkT = tmp("rkT", [DK, NR])
        tab = tmp("tab", [DK, TA + TB])
        tp1, tp2, tp3 = (tmp(f"tabp{i}", [DK, TA + TB], BF16) for i in range(3))
        rvb = tmp("rvb", [P, 2, DK])
        loaded, dve = ctx.enter_context(nc.semaphore("tab_in")), ctx.enter_context(nc.semaphore("tab_step"))
        split, packed = ctx.enter_context(nc.semaphore("tab_split")), ctx.enter_context(nc.semaphore("tab_packed"))
        pool_step = ctx.enter_context(nc.semaphore("const_step"))
        blk = ctx.enter_context(nc.Block())

        @blk.sync
        def _(sp):
            sp.dma_start(rkT[:], io["rel_k"].rearrange("r d -> d r"), allow_slow_non_contiguous=True).then_inc(loaded, 16)
            rv, ext = io["rel_v"], dr["relv"]
            sp.dma_start(rvb[:], bass.AP(rv.tensor, 0, [[0, P], [2 * R * DK, 2], [1, DK]])).then_inc(loaded, 16)
            sp.dma_start(w["rvt"][:].rearrange("p x d -> p (x d)"),
                         bass.AP(ext.tensor, 0, [[DK, P], [1, XW * DK]])).then_inc(loaded, 16)
            sp.wait_ge(split, 1)
            for n, part in enumerate(K_PARTS):
                sp.dma_start(w["rkp"][n * DK:(n + 1) * DK], (tp1, tp2, tp3)[part][:]).then_inc(packed, 16)
            sp.wait_ge(packed, 16 * len(K_PARTS))

        @blk.gpsimd
        def _(pool):
            for b in range(3):
                pool.memset(w["kpk"][ROWS:C_ROWS, b], 1.0).then_inc(pool_step, 1)
            pool.memset(w["spread"][:], 1.0).then_inc(pool_step, 1)
            pool.wait_ge(pool_step, 4)
            pool.affine_select(out=w["spread"][:], in_=w["spread"][:], compare_op=ALU.is_ge, fill=0.0,
                               base=0, pattern=[[1, P]], channel_multiplier=-32).then_inc(pool_step, 1)
            pool.wait_ge(pool_step, 5)
            pool.affine_select(out=w["spread"][:], in_=w["spread"][:], compare_op=ALU.is_ge, fill=0.0,
                               base=31, pattern=[[-1, P]], channel_multiplier=32).then_inc(pool_step, 1)

        @blk.vector
        def _(v):
            steps = 0

            def done(ins):
                nonlocal steps
                steps += 1
                ins.then_inc(dve, 1)
                v.wait_ge(dve, steps)

            v.wait_ge(loaded, 48)
            done(v.memset(tab[:], 0.0))
            far = rkT[:, NR - 1:NR]
            done(v.tensor_scalar(tab[:, P - 1:P - 1 + NR], rkT[:], rkT[:, 0:1], None, ALU.subtract))
            done(v.tensor_scalar(tab[:, P - 1 + NR:TA], rkT[:, NR - 1:NR].broadcast_to([DK, TA - P + 1 - NR]),
                                 rkT[:, 0:1], None, ALU.subtract))
            done(v.tensor_scalar(tab[:, TA:TA + R], rkT[:, R + 1:NR], far, None, ALU.subtract))
            done(v.tensor_copy(tp1[:], tab[:]))
            done(v.tensor_tensor(tab[:], tab[:], tp1[:], ALU.subtract))
            done(v.tensor_copy(tp2[:], tab[:]))
            v.tensor_tensor(tp3[:], tab[:], tp2[:], ALU.subtract).then_inc(split, 1)
            for r, (lo, hi) in enumerate(((0, XA), (XA, XW))):
                done(v.tensor_tensor(w["rvt"][:, lo:hi], w["rvt"][:, lo:hi],
                                     rvb[:, r].unsqueeze(1).broadcast_to([P, hi - lo, DK]), ALU.subtract))
            done(v.tensor_copy(w["identb"][:], w["ident"][:]))


def attend(nc, dr, w, ngroups=B * NG):
    with ExitStack() as ctx:
        def sb(name, shape, dt=F32):
            return ctx.enter_context(nc.sbuf_tensor(name, shape, dt))

        def sem(name):
            return ctx.enter_context(nc.semaphore(name))

        qpk, kpk = w["qpk"], w["kpk"]
        vs = sb("vs", [P, 2, NB, 2, HB * 32])
        dt = sb("dt", [P, 2, HB, NB, XW])
        dh = sb("dh", [P, HB, NB, XW], BF16)
        prob = sb("prob", [P, RING * HB, CH])
        tmax = sb("tmax", [P, HB * NB, NC])
        rmax = sb("rmax", [P, HB * NB])
        m1 = sb("m1", [HB * NB, P], BF16)
        m2 = sb("m2", [HB * NB, P], BF16)
        ctxs = sb("ctxs", [P, S])
        rs = sb("rs", [P, HB * S // P])
        rr = sb("rr", [P, HB * S // P])
        rrow = sb("rrow", [HB, S])
        pp = ctx.enter_context(nc.psum_tensor("pp", [P, 8 * CH], F32))
        bank = lambda n: pp[:, n * CH:(n + 1) * CH]
        ctxT = pp[:, 0:2 * CH]
        S_BANK, ST_BANK, M_BANK = 2, 4, 7
        relvT = pp[:, 4 * CH:6 * CH].rearrange("p (a h i) -> p a h i", h=HB, i=NB)
        bc = pp[:, 6 * CH:8 * CH]
        D_BANKS = (2, 3, 0, 1)

        qk_in = [sem(f"qk_in{i}") for i in range(3)]
        v_in = [sem(f"v_in{i}") for i in range(2)]
        s_full, s_free = sem("s_full"), sem("s_free")
        st_win, st_plain, added = sem("st_win"), sem("st_plain"), sem("added")
        exp_ok = sem("exp_ok")
        pv_win, pv_plain, win_ok = sem("pv_win"), sem("pv_plain"), sem("win_ok")
        pwin_ok, ctx_full = sem("pwin_ok"), sem("ctx_full")
        ctx_pe, ctx_dve, ctx_sp = sem("ctx_pe"), sem("ctx_dve"), sem("ctx_sp")
        ctxs_free, ctx_out = sem("ctxs_free"), sem("ctx_out")
        rmax_ok, mT_full, m_ok, m_in = sem("rmax_ok"), sem("mT_full"), sem("m_ok"), sem("m_in")
        relv_full, relv_free = sem("relv_full"), sem("relv_free")
        rs_in, rr_ok, rrow_in = sem("rs_in"), sem("rr_ok"), sem("rrow_in")
        bc_full, bc_free, ctxn_ok = sem("bc_full"), sem("bc_free"), sem("ctxn_ok")
        d_full, d_out, dh_ok = sem("d_full"), sem("d_out"), sem("dh_ok")
        bufs_free = sem("bufs_free")
        dve_step, pool_step, act_step = sem("dve_step3"), sem("pool_step3"), sem("act_step3")
        blk = ctx.enter_context(nc.Block())
        N_QK = 7

        def load_qk(sp, g, b3):
            def rows(src, to, lo, parts):
                n = len(parts)
                step = parts[1] - parts[0] if n > 1 else 1
                take = src[bass.ds(g, 1), parts[0]:parts[-1] + 1:step].rearrange("o n d t -> (o n) d t")
                sp.dma_start(to[lo:lo + n * DK, b3], take).then_inc(qk_in[b3], 16)
            rows(dr["q"], qpk, 0, Q_PARTS[0:3])
            rows(dr["q"], qpk, 3 * DK, Q_PARTS[3:5])
            rows(dr["q"], qpk, 5 * DK, Q_PARTS[5:6])
            for n in range(3):
                rows(dr["k"], kpk, 2 * n * DK, K_PARTS[2 * n:2 * n + 2])
            sp.dma_start(qpk[ROWS:C_ROWS, b3], dr["c"][bass.ds(g, 1)].rearrange("o r t -> (o r) t")).then_inc(qk_in[b3], 16)

        def load_v(sp, g, b2):
            sp.dma_start(vs[:, b2].rearrange("p j r c -> p j (r c)"),
                         dr["v"][bass.ds(g, 1)].rearrange("o j p c -> p (o j) c")).then_inc(v_in[b2], 16)

        def send_m(sp, b3):
            sp.wait_ge(m_ok, 1)
            sp.sem_inc(m_ok, -1)
            for n, m in enumerate((m1, m2)):
                sp.dma_start(qpk[ROWS + n:ROWS + n + 1, b3], m[:]).then_inc(m_in, 16)

        def run_steps(eng, step):
            n = (ngroups - 4) // 6 * 6
            if n:
                with eng.Fori(0, n // 6) as turn:
                    for i in range(6):
                        step(turn * 6 + i, i, 3)
            for g in range(n, ngroups):
                step(g, g % 6, min(3, ngroups - 1 - g))

        @blk.sync
        def _(sp):
            for g in range(3):
                load_qk(sp, g, g)
            for g in range(2):
                load_v(sp, g, g)
            sp.sem_inc(ctx_out, 16)
            send_m(sp, 0)

            def step(g, i, left):
                sp.wait_ge(ctx_out, 16)
                sp.sem_inc(ctx_out, -16)
                sp.sem_inc(ctxs_free, 1)
                if left >= 1:
                    send_m(sp, (i + 1) % 3)
                sp.wait_ge(ctx_sp, 1)
                sp.sem_inc(ctx_sp, -1)
                sp.dma_start(rs[:], ctxs[DK:P:32, :]).then_inc(rs_in, 16)
                sp.wait_ge(rr_ok, 1)
                sp.sem_inc(rr_ok, -1)
                sp.dma_start(rrow[:], rr[:]).then_inc(rrow_in, 16)
                if left >= 2:
                    sp.wait_ge(bufs_free, 1)
                    sp.sem_inc(bufs_free, -1)
                    if left >= 3:
                        load_qk(sp, g + 3, i % 3)
                    load_v(sp, g + 2, i % 2)
                sp.wait_ge(ctxn_ok, 2)
                sp.sem_inc(ctxn_ok, -2)
                sp.dma_start(dr["ctx"][bass.ds(g, 1)].rearrange("o p t -> (o p) t"), ctxs[:]).then_inc(ctx_out, 16)

            run_steps(sp, step)
            sp.wait_ge(ctx_out, 16)


        @blk.tensor
        def _(pe):
            def tables(b3):
                pe.wait_ge(qk_in[b3], 16 * N_QK)
                pe.sem_inc(qk_in[b3], -16 * N_QK)
                q = qpk[0:ROWS, b3].rearrange("r (h j a) -> r a h j", h=HB, a=P)
                for f in range(DF):
                    if f >= len(D_BANKS):
                        pe.wait_ge(dh_ok, f - len(D_BANKS) + 1)
                    out = bank(D_BANKS[f % len(D_BANKS)]).rearrange("p (x h j) -> p x h j", h=HB, j=NB)
                    for k in range(XF):
                        x = f * XF + k
                        if x < R:
                            at, a, j0, j1, i0 = TA + R - 1 - x, P - R + x, 1, NB, 0
                        elif x < R + P:
                            at, a, j0, j1, i0 = XW - 1 - x, x - R, 0, NB, 0
                        else:
                            at, a, j0, j1, i0 = XW - 1 - x, x - R - P, 0, NB - 1, 1
                        mm = pe.matmul(out[:, k, :, j0:j1], w["rkp"][0:ROWS, at:at + P], q[:, a, :, i0:i0 + j1 - j0],
                                       start=True, stop=True)
                    mm.then_inc(d_full, 1)

            def score_rows(t, b3):
                h, ib, c = t // (NB * NC), t // NC % NB, t % NC
                out = bank(S_BANK + t % 2)
                at = h * S + ib * P
                mms = []
                for j in range(2):
                    lo, hi = (c * CH, min((c + 1) * CH, (ib + 1) * P)) if j == 0 else (max(c * CH, (ib + 1) * P), (c + 1) * CH)
                    rows = (ROWS, C_ROWS)[j]
                    if lo < hi:
                        mms.append((out[:, lo - c * CH:hi - c * CH], qpk[0:rows, b3, at:at + P],
                                    kpk[0:rows, b3, h * S + lo:h * S + hi]))
                if ib // 4 == c:
                    o = ib % 4 * P
                    mms.append((out[:, o:o + P], dh[:, h, ib, R:R + P], w["identb"][:]))
                if ib and (ib - 1) // 4 == c:
                    o = (ib - 1) % 4 * P + P - R
                    mms.append((out[0:R, o:o + R], dh[:, h, ib - 1, R + P:XW], w["identb"][:, P - R:P]))
                if ib < NB - 1 and (ib + 1) // 4 == c:
                    o = (ib + 1) % 4 * P
                    mms.append((out[P - R:P, o:o + R], dh[:, h, ib + 1, 0:R], w["identb"][:, 0:R]))
                for n, (o, l, r) in enumerate(mms):
                    mm = pe.matmul(o, l, r, start=(n == 0), stop=(n == len(mms) - 1), skip_group_check=True)
                mm.then_inc(s_full, 1)

            def score_cols(t, b3):
                (jb, c), h = QUADS[t // HB], t % HB
                out = bank(ST_BANK + t % 3)
                at = h * S + jb * P
                for n, (far, lo, hi) in enumerate(pieces(jb, c)):
                    rows = C_ROWS if far else M_ROWS
                    mm = pe.matmul(out[:, lo - c * CH:hi - c * CH], kpk[0:rows, b3, at:at + P],
                                   qpk[0:rows, b3, h * S + lo:h * S + hi], start=(n == 0), stop=True,
                                   skip_group_check=True)
                mm.then_inc(st_win if WIN[t // HB] else st_plain, 1)

            def values(q, b2):
                jb, c = QUADS[q]
                found = pieces(jb, c)
                for n, (far, lo, hi) in enumerate(found):
                    for h in range(HB):
                        mm = pe.matmul(ctxT[32 * h:32 * h + 32, lo:hi], vs[:, b2, jb, far, 32 * h:32 * h + 32],
                                       prob[:, q % RING * HB + h, lo - c * CH:hi - c * CH],
                                       start=(jb == 0), stop=(jb == NB - 1 and n == len(found) - 1),
                                       skip_group_check=True)
                mm.then_inc(pv_win if WIN[q] else pv_plain, 1)

            def relative_values(b2):
                win = dt[:, b2]
                for a in range(R):
                    for q in range(4):
                        x = R * q + a + R
                        mm = pe.matmul(relvT[32 * q:32 * q + DK, a], w["rvt"][:, XW - 1 - x], win[:, :, :, x],
                                       start=True, stop=(0 < q < 3), skip_group_check=True)
                    x = R + P + a
                    pe.matmul(relvT[0:DK, a, :, 1:NB], w["rvt"][:, XW - 1 - x], win[:, :, 0:NB - 1, x],
                              start=False, stop=True, skip_group_check=True)
                    mm = pe.matmul(relvT[96:96 + DK, a, :, 0:NB - 1], w["rvt"][:, XW - 1 - a], win[:, :, 1:NB, a],
                                   start=False, stop=True, skip_group_check=True)
                mm.then_inc(relv_full, 1)

            def turn_max():
                pe.wait_ge(rmax_ok, 1)
                pe.sem_inc(rmax_ok, -1)
                pe.transpose(bank(M_BANK)[0:HB * NB, 0:P], rmax[:], w["ident"][:]).then_inc(mT_full, 1)

            def spread():
                pe.wait_ge(rrow_in, 16)
                pe.sem_inc(rrow_in, -16)
                for c in range(NC):
                    pe.matmul(bc[:, c * CH:(c + 1) * CH], w["spread"][:], rrow[:, c * CH:(c + 1) * CH],
                              start=True, stop=True).then_inc(bc_full, 1)

            tables(0)
            pe.wait_ge(dh_ok, DF)
            pe.sem_inc(dh_ok, -DF)
            for t in range(NT):
                if t >= 2:
                    pe.wait_ge(s_free, t - 1)
                score_rows(t, 0)
            pe.wait_ge(s_free, NT)
            pe.sem_inc(s_free, -NT)
            turn_max()
            tables(1)
            pe.sem_inc(relv_free, 1)
            pe.sem_inc(bc_free, 1)

            def step(g, i, left):
                b3, n3, b2 = i % 3, (i + 1) % 3, i % 2
                pe.wait_ge(m_in, 32)
                pe.sem_inc(m_in, -32)
                pe.wait_ge(relv_free, 1)
                pe.sem_inc(relv_free, -1)
                pe.wait_ge(bc_free, 1)
                pe.sem_inc(bc_free, -1)
                for t in range(NT):
                    if t >= 3:
                        pe.wait_ge(exp_ok, t - 2)
                    score_cols(t, b3)
                    if left >= 1:
                        if t == 0:
                            pe.wait_ge(dh_ok, DF)
                            pe.sem_inc(dh_ok, -DF)
                        if t >= 2:
                            pe.wait_ge(s_free, t - 1)
                        score_rows(t, n3)
                    if t % HB == HB - 1 and t > HB:
                        if t // HB == 1:
                            pe.wait_ge(v_in[b2], 16)
                            pe.sem_inc(v_in[b2], -16)
                        values(t // HB - 1, b2)
                pe.wait_ge(exp_ok, NT)
                pe.sem_inc(exp_ok, -NT)
                values(NQ - 1, b2)
                if left >= 1:
                    pe.wait_ge(s_free, NT)
                    pe.sem_inc(s_free, -NT)
                    turn_max()
                pe.wait_ge(pwin_ok, 1)
                pe.sem_inc(pwin_ok, -1)
                relative_values(b2)
                pe.wait_ge(ctx_pe, 1)
                pe.sem_inc(ctx_pe, -1)
                if left >= 2:
                    tables((i + 2) % 3)
                spread()

            run_steps(pe, step)


        @blk.scalar
        def _(act):
            def tables_out(b2):
                for f in range(DF):
                    act.wait_ge(d_full, f + 1)
                    x0 = f * XF
                    j0 = 1 if x0 < R else 0
                    j1 = NB - 1 if x0 >= R + P else NB
                    src = bank(D_BANKS[f % len(D_BANKS)]).rearrange("p (x h j) -> p h j x", h=HB, j=NB)
                    act.activation(dt[:, b2, :, j0:j1, x0:x0 + XF], src[:, :, j0:j1, :], ACT.Copy).then_inc(d_out, 1)
                act.sem_inc(d_full, -DF)

            def ring_free(q):
                n = sum(WIN[:q + 1])
                if WIN[q]:
                    act.wait_ge(win_ok, n)
                else:
                    act.wait_ge(pv_plain, q + 1 - n)

            tables_out(0)
            tables_out(1)
            act.sem_inc(win_ok, NWIN)
            act.sem_inc(pv_plain, NQ - NWIN)

            def step(g, i, left):
                act.wait_ge(win_ok, NWIN)
                act.wait_ge(pv_plain, NQ - NWIN)
                act.sem_inc(win_ok, -NWIN)
                act.sem_inc(pv_plain, -(NQ - NWIN))
                n_win = n_plain = 0
                for t in range(NT):
                    q = t // HB
                    if t % HB == 0 and q >= RING:
                        ring_free(q - RING)
                    if WIN[q]:
                        n_win += 1
                        act.wait_ge(added, n_win)
                    else:
                        n_plain += 1
                        act.wait_ge(st_plain, n_plain)
                    act.activation(prob[:, q % RING * HB + t % HB], bank(ST_BANK + t % 3), ACT.Exp,
                                   scale=SCALE).then_inc(exp_ok, 1)
                act.sem_inc(added, -n_win)
                act.sem_inc(st_plain, -n_plain)
                act.wait_ge(ctx_full, 1)
                act.sem_inc(ctx_full, -1)
                act.wait_ge(ctxs_free, 1)
                act.sem_inc(ctxs_free, -1)
                act.activation(ctxs[:], ctxT, ACT.Copy).then_inc(act_step, 1)
                act.wait_ge(act_step, 1)
                act.sem_inc(act_step, -1)
                for s in (ctx_pe, ctx_dve, ctx_sp):
                    act.sem_inc(s, 1)
                if left >= 2:
                    tables_out(i % 2)
                    act.sem_inc(bufs_free, 1)

            run_steps(act, step)


        @blk.vector
        def _(v):
            def round_table(f, b2):
                v.wait_ge(d_out, f + 1)
                x0 = f * XF
                j0 = 1 if x0 < R else 0
                j1 = NB - 1 if x0 >= R + P else NB
                v.tensor_copy(dh[:, :, j0:j1, x0:x0 + XF], dt[:, b2, :, j0:j1, x0:x0 + XF]).then_inc(dh_ok, 1)

            def tile_max(t):
                v.wait_ge(s_full, t + 1)
                v.tensor_reduce(tmax[:, t // NC, t % NC:t % NC + 1], bank(S_BANK + t % 2), AX, ALU.max).then_inc(s_free, 1)

            def row_max():
                v.sem_inc(s_full, -NT)
                v.drain()
                v.tensor_reduce(rmax[:], tmax[:], AX, ALU.max).then_inc(rmax_ok, 1)
                v.wait_ge(mT_full, 1)
                v.sem_inc(mT_full, -1)
                src = bank(M_BANK)[0:HB * NB, 0:P]
                v.tensor_scalar(m1[:], src, -1.0, None, ALU.mult).then_inc(dve_step, 1)
                v.wait_ge(dve_step, 1)
                v.sem_inc(dve_step, -1)
                v.scalar_tensor_tensor(m2[:], src, -1.0, m1[:], ALU.mult, ALU.subtract).then_inc(m_ok, 1)

            for f in range(DF):
                round_table(f, 0)
            v.sem_inc(d_out, -DF)
            for t in range(NT):
                tile_max(t)
            row_max()
            for f in range(DF):
                round_table(f, 1)
            v.sem_inc(d_out, -DF)

            def step(g, i, left):
                b2 = i % 2
                n_win = 0
                for t in range(NT):
                    (jb, c), h = QUADS[t // HB], t % HB
                    if WIN[t // HB]:
                        n_win += 1
                        v.wait_ge(st_win, n_win)
                        lo, hi = window(jb, c)
                        x0 = lo - jb * P + R
                        cols = bank(ST_BANK + t % 3)[:, lo - c * CH:hi - c * CH]
                        v.tensor_tensor(cols, cols, dt[:, b2, h, jb, x0:x0 + hi - lo], ALU.add).then_inc(added, 1)
                    if left >= 1:
                        tile_max(t)
                v.sem_inc(st_win, -n_win)
                if left >= 1:
                    row_max()
                v.wait_ge(rs_in, 16)
                v.sem_inc(rs_in, -16)
                v.reciprocal(rr[:], rs[:]).then_inc(rr_ok, 1)
                v.wait_ge(relv_full, 1)
                v.sem_inc(relv_full, -1)
                v.wait_ge(ctx_dve, 1)
                v.sem_inc(ctx_dve, -1)
                for n in range(4 * HB):
                    if left >= 2 and n < DF:
                        round_table(n, b2)
                    h, q = n // 4, n % 4
                    to = ctxs[32 * h:32 * h + DK].rearrange("p (i a) -> p i a", a=P)[:, :, R * q:R * q + R]
                    part = relvT[32 * q:32 * q + DK, :, h, :].rearrange("p a i -> p i a")
                    v.tensor_tensor(to, part, to, ALU.add).then_inc(dve_step, 1)
                if left >= 2:
                    v.sem_inc(d_out, -DF)
                v.wait_ge(dve_step, 4 * HB)
                v.sem_inc(dve_step, -4 * HB)
                v.sem_inc(relv_free, 1)
                for c in range(NC):
                    v.wait_ge(bc_full, c + 1)
                    v.tensor_tensor(ctxs[:, c * CH:(c + 1) * CH], bc[:, c * CH:(c + 1) * CH],
                                    ctxs[:, c * CH:(c + 1) * CH], ALU.mult).then_inc(dve_step, 1)
                v.sem_inc(bc_full, -NC)
                v.wait_ge(dve_step, NC)
                v.sem_inc(dve_step, -NC)
                v.sem_inc(bc_free, 1)
                v.sem_inc(ctxn_ok, 2)

            run_steps(v, step)


        @blk.gpsimd
        def _(pool):
            def step(g, i, left):
                n = 0
                for q, (jb, c) in enumerate(QUADS):
                    if not WIN[q]:
                        continue
                    n += 1
                    pool.wait_ge(pv_win, n)
                    if q == NQ - 1:
                        pool.sem_inc(ctx_full, 1)
                    lo, hi = window(jb, c)
                    x0, s0 = lo - jb * P + R, q % RING * HB
                    copy = pool.tensor_copy(dt[:, i % 2, :, jb, x0:x0 + hi - lo],
                                            prob[:, s0:s0 + HB, lo - c * CH:hi - c * CH])
                    if q < NQ - 1:
                        copy.then_inc(win_ok, 1)
                    else:
                        copy.then_inc(pool_step, 1)
                        pool.wait_ge(pool_step, 1)
                        pool.sem_inc(pool_step, -1)
                        pool.sem_inc(win_ok, 1)
                        pool.sem_inc(pwin_ok, 1)
                pool.sem_inc(pv_win, -NWIN)

            run_steps(pool, step)




def setup_ffn(nc, io, w):
    with ExitStack() as ctx:
        wop = ctx.enter_context(nc.sbuf_tensor("wop", [P, KT, H, 32], F32))
        pt = [ctx.enter_context(nc.psum_tensor(f"wo_t{i}", [P, CH], F32)) for i in range(2)]
        loaded, const_step = ctx.enter_context(nc.semaphore("ffn_in")), ctx.enter_context(nc.semaphore("ffn_const"))
        wo_zero, turned = ctx.enter_context(nc.semaphore("wo_zero")), ctx.enter_context(nc.semaphore("wo_turned"))
        blk = ctx.enter_context(nc.Block())
        N_WO = 2 * KT

        @blk.sync
        def _(sp):
            sp.wait_ge(wo_zero, 1)
            for t in range(KT):
                sp.dma_start(wop[:, t, :, 0:DK], io["Wo"][t * P:(t + 1) * P, :].rearrange("p (h d) -> p h d", d=DK)
                             ).then_inc(loaded, 16)
                sp.dma_start(wop[:, t, 0, DK:DK + 1], io["b_o"][t * P:(t + 1) * P].rearrange("(p o) -> p o", o=1),
                             allow_slow_non_contiguous=True).then_inc(loaded, 16)
            sp.dma_start(w["w1"][:], io["W1"].rearrange("(t p) f -> p t f", p=P)).then_inc(loaded, 16)
            sp.dma_start(w["w2"][:], io["W2"].rearrange("(t p) f -> p t f", p=P)).then_inc(loaded, 16)
            sp.dma_start(w["b1c"][:], io["b1"].rearrange("(t p) -> p t", p=P), allow_slow_non_contiguous=True
                         ).then_inc(loaded, 16)
            sp.dma_start(w["b2_bc"][:], bass.AP(io["b2"].tensor, 0, [[0, P], [1, D]])).then_inc(loaded, 16)
            sp.dma_start(w["wr"][:], io["w_router"].rearrange("(t p) -> p t", p=P), allow_slow_non_contiguous=True
                         ).then_inc(loaded, 16)

        @blk.gpsimd
        def _(pool):
            pool.memset(w["mhalf2"][:], -0.5).then_inc(const_step, 1)
            pool.memset(w["before"][:], 1.0).then_inc(const_step, 1)
            pool.wait_ge(const_step, 2)
            pool.affine_select(out=w["before"][:], in_=w["before"][:], compare_op=ALU.is_ge, fill=0.0,
                               base=-1, pattern=[[-1, P]], channel_multiplier=1).then_inc(const_step, 1)

        @blk.tensor
        def _(pe):
            pe.wait_ge(loaded, 16 * (N_WO + 5))
            for hg in range(NG):
                for t in range(KT):
                    mm = pe.transpose(pt[hg // 2][:, hg % 2 * D + t * P:hg % 2 * D + (t + 1) * P],
                                      wop[:, t, hg * HB:(hg + 1) * HB].rearrange("p h c -> p (h c)"), w["ident"][:])
            mm.then_inc(turned, 1)

        @blk.vector
        def _(v):
            v.memset(wop[:], 0.0).then_inc(wo_zero, 1)
            v.wait_ge(turned, 1)
            for k in range(2):
                v.tensor_copy(w["woT"][:, 2 * k:2 * k + 2], pt[k][:, :].rearrange("p (g n) -> p g n", g=2))
            for kt in range(KT):
                v.tensor_copy(w["wr_bc"][:, kt], w["wr"][:, kt:kt + 1].broadcast_to([P, P]))


def ffn(nc, io, dr, out, w, nbatch=B):
    with ExitStack() as ctx:
        def sb(name, shape, dt=F32):
            return ctx.enter_context(nc.sbuf_tensor(name, shape, dt))

        def sem(name):
            return ctx.enter_context(nc.semaphore(name))

        cin = sb("cin", [P, NG, S])
        xin = sb("xin2", [P, NB, D])
        mrow = sb("mrow", [P, 2, 4, D])
        t1 = sb("t1", [P, CH])
        x1 = sb("x1", [P, 2, NB, D])
        h2 = sb("h2", [P, NB, D])
        gh = sb("gh", [P, NB, D])
        hT = sb("hT2", [P, KT, S])
        sbc = sb("sbc", [P, S])
        pick = sb("pick", [P, NB, P])
        scol = sb("scol", [P, NB])
        th = sb("th", [P, NB])
        junk = sb("junk", [P, S])
        cnt = sb("cnt", [P, NB, 4])
        rank = sb("rank", [P, NB])
        wm = sb("wm", [P, NB])
        gT = sb("gT", [P, FT, S])
        y = sb("y", [P, NB, D])
        stats = sb("stats2", [P, NB, 6])
        mv = sb("mv2", [P, NB, 2])
        veps, rstd, nmr = sb("veps2", [P, NB]), sb("rstd2", [P, NB]), sb("nmr2", [P, NB])
        bank = [ctx.enter_context(nc.psum_tensor(f"pf{i}", [P, CH], F32)) for i in range(8)]
        UP, PROJ, DOWN = 0, 2, 4
        NF = NB // 2
        NU = NC * FT
        NT_H = KT * NC

        x_in2, c_in = sem("x_in2"), sem("c_in")
        mr_in = [sem(f"mr_in{i}") for i in range(2)]
        x_used, mr_used = sem("x_used"), sem("mr_used")
        up_full, gelu_ok = sem("up_full"), sem("gelu_ok")
        proj_full, proj_free = sem("proj_full"), sem("proj_free")
        h2_ok, h2_used, x1_ok = sem("h2_ok"), sem("h2_used"), sem("x1_ok")
        turn_full, hT_ok = sem("turn_full"), sem("hT_ok")
        sc_full, sbc_ok, sbc_pe, sbc_free = sem("sc_full"), sem("sbc_ok"), sem("sbc_pe"), sem("sbc_free")
        scol_ok, th_ok = sem("scol_ok"), sem("th_ok")
        down_full, down_free = sem("down_full"), sem("down_free")
        y_ok, y_free, o_ok = sem("y_ok"), sem("y_free"), sem("o_ok")
        o_out = [sem(f"o_out{i}") for i in range(2)]
        var_ok, rstd_ok = sem("var_ok2"), sem("rstd_ok2")
        dve_step, act_step, pool_step = sem("dve_step4"), sem("act_step4"), sem("pool_step4")
        blk = ctx.enter_context(nc.Block())

        def run_steps(eng, step):
            if nbatch > 2:
                with eng.Fori(0, (nbatch - 2) // 2) as pair:
                    for p in range(2):
                        step(pair * 2 + p, p, 2)
            step(nbatch - 2, 0, 1)
            step(nbatch - 1, 1, 0)

        @blk.sync
        def _(sp):
            def load(b):
                sp.dma_start(xin[:], io["x"][bass.ds(b, 1)].rearrange("o (t p) d -> p (o t) d", p=P)).then_inc(x_in2, 16)
                sp.dma_start(cin[:], dr["ctx"][bass.ds(b * NG, NG)].rearrange("g p t -> p g t")).then_inc(c_in, 16)

            def load_rows(b, p):
                sp.dma_start(mrow[:, p].rearrange("p f d -> p (f d)"),
                             dr["mod_row"][bass.ds(b, 1)].broadcast_to([P, 4 * D])).then_inc(mr_in[p], 16)

            load(0)
            load_rows(0, 0)
            load_rows(1, 1)
            sp.wait_ge(x_used, 1)
            sp.sem_inc(x_used, -1)
            load(1)

            def step(b, p, left):
                if left >= 2:
                    sp.wait_ge(x_used, 1)
                    sp.sem_inc(x_used, -1)
                    load(b + 2)
                for f in range(NF):
                    sp.wait_ge(o_ok, f + 1)
                    sp.dma_start(out[bass.ds(b, 1), 2 * f * P:(2 * f + 2) * P].rearrange("o (t p) d -> p (o t) d", p=P),
                                 x1[:, p, 2 * f:2 * f + 2]).then_inc(o_out[p], 16)
                sp.sem_inc(o_ok, -NF)
                if left >= 2:
                    sp.wait_ge(mr_used, 1)
                    sp.sem_inc(mr_used, -1)
                    load_rows(b + 2, p)

            run_steps(sp, step)

        @blk.tensor
        def _(pe):
            def project():
                pe.wait_ge(c_in, 16)
                pe.sem_inc(c_in, -16)
                for f in range(NF):
                    if f >= 2:
                        pe.wait_ge(proj_free, f - 1)
                    for k in range(2):
                        at = (2 * f + k) * P
                        for hg in range(NG):
                            mm = pe.matmul(bank[PROJ + f % 2][:, k * D:(k + 1) * D], cin[:, hg, at:at + P],
                                           w["woT"][:, hg], start=(hg == 0), stop=(hg == NG - 1))
                    mm.then_inc(proj_full, 1)

            def turn_and_score():
                pe.wait_ge(h2_ok, 1)
                pe.sem_inc(h2_ok, -1)
                for n in range(NT_H):
                    kt, half = n % KT, n // KT
                    if n >= 2:
                        pe.wait_ge(hT_ok, n - 1)
                    for t in range(4):
                        mm = pe.transpose(bank[UP + n % 2][:, t * P:(t + 1) * P],
                                          h2[:, 4 * half + t, kt * P:(kt + 1) * P], w["ident"][:])
                    mm.then_inc(turn_full, 1)
                pe.wait_ge(proj_free, NF)
                pe.sem_inc(proj_free, -NF)
                pe.wait_ge(hT_ok, NT_H)
                pe.sem_inc(hT_ok, -NT_H)
                for c in range(NC):
                    for kt in range(KT):
                        mm = pe.matmul(bank[PROJ + c][:, :], w["wr_bc"][:, kt], hT[:, kt, c * CH:(c + 1) * CH],
                                       start=(kt == 0), stop=(kt == KT - 1))
                    mm.then_inc(sc_full, 1)

            def up():
                for u in range(NU):
                    c, ft = u // FT, u % FT
                    if u >= 2:
                        pe.wait_ge(gelu_ok, u - 1)
                    for kt in range(KT):
                        mm = pe.matmul(bank[UP + u % 2][:, :], w["w1"][:, kt, ft * P:(ft + 1) * P],
                                       hT[:, kt, c * CH:(c + 1) * CH], start=(kt == 0), stop=(kt == KT - 1))
                    mm.then_inc(up_full, 1)

            def down():
                pe.wait_ge(gelu_ok, NU)
                pe.sem_inc(gelu_ok, -NU)
                pe.wait_ge(down_free, NF)
                pe.sem_inc(down_free, -NF)
                for f in range(NF):
                    for k in range(2):
                        at = (2 * f + k) * P
                        for ft in range(FT):
                            mm = pe.matmul(bank[DOWN + f][:, k * D:(k + 1) * D], gT[:, ft, at:at + P], w["w2"][:, ft],
                                           start=(ft == 0), stop=(ft == FT - 1))
                    mm.then_inc(down_full, 1)

            project()
            turn_and_score()
            pe.sem_inc(down_free, NF)

            def step(b, p, left):
                up()
                pe.wait_ge(sbc_pe, NC)
                pe.sem_inc(sbc_pe, -NC)
                if left >= 1:
                    project()
                down()
                if left >= 1:
                    turn_and_score()

            run_steps(pe, step)

        @blk.scalar
        def _(act):
            def turned():
                for n in range(NT_H):
                    kt, half = n % KT, n // KT
                    act.wait_ge(turn_full, n + 1)
                    act.activation(hT[:, kt, half * CH:(half + 1) * CH], bank[UP + n % 2][:, :], ACT.Copy).then_inc(hT_ok, 1)
                act.sem_inc(turn_full, -NT_H)
                act.wait_ge(sbc_free, 1)
                act.sem_inc(sbc_free, -1)
                for c in range(NC):
                    act.wait_ge(sc_full, c + 1)
                    act.activation(sbc[:, c * CH:(c + 1) * CH], bank[PROJ + c][:, :], ACT.Copy).then_inc(act_step, 1)
                    act.wait_ge(act_step, c + 1)
                    act.sem_inc(sbc_ok, 1)
                    act.sem_inc(sbc_pe, 1)
                act.sem_inc(act_step, -NC)
                act.sem_inc(sc_full, -NC)

            act.sem_inc(sbc_free, 1)
            turned()

            def step(b, p, left):
                for u in range(NU):
                    c, ft = u // FT, u % FT
                    act.wait_ge(up_full, u + 1)
                    act.activation(gT[:, ft, c * CH:(c + 1) * CH], bank[UP + u % 2][:, :], ACT.Gelu_apprx_tanh,
                                   bias=w["b1c"][:, ft:ft + 1]).then_inc(gelu_ok, 1)
                    if u == 3:
                        act.wait_ge(scol_ok, 1)
                        act.sem_inc(scol_ok, -1)
                        act.activation(th[:], scol[:], ACT.Tanh, scale=0.5).then_inc(th_ok, 1)
                act.sem_inc(up_full, -NU)
                if left >= 1:
                    turned()

            run_steps(act, step)

        @blk.vector
        def _(v):
            steps = 0

            def go(ins):
                nonlocal steps
                steps += 1
                return ins.then_inc(dve_step, 1)

            def settle():
                v.wait_ge(dve_step, steps)

            def restart():
                nonlocal steps
                settle()
                v.sem_inc(dve_step, -steps)
                steps = 0

            def ranks():
                v.wait_ge(sbc_ok, NC)
                v.sem_inc(sbc_ok, -NC)
                go(v.tensor_tensor(pick[:], sbc[:].rearrange("p (t u) -> p t u", u=P),
                                   w["ident"][:].unsqueeze(1).broadcast_to([P, NB, P]), ALU.mult))
                settle()
                go(v.tensor_reduce(scol[:], pick[:], AX, ALU.add))
                settle()
                v.sem_inc(scol_ok, 1)
                for t in range(NB):
                    s, lo, hi = scol[:, t:t + 1], t * P, (t + 1) * P
                    if lo:
                        go(v.tensor_scalar(junk[:, 0:lo], sbc[:, 0:lo], s, 0.0, ALU.is_ge, ALU.add,
                                           accum_out=cnt[:, t, 0:1]))
                    if hi < S:
                        go(v.tensor_scalar(junk[:, hi:S], sbc[:, hi:S], s, 0.0, ALU.is_gt, ALU.add,
                                           accum_out=cnt[:, t, 1:2]))
                    go(v.tensor_scalar(junk[:, lo:hi], sbc[:, lo:hi], s, 0.0, ALU.is_gt, ALU.add,
                                       accum_out=cnt[:, t, 2:3]))
                    settle()
                    go(v.scalar_tensor_tensor(junk[:, lo:hi], sbc[:, lo:hi], s, w["before"][:], ALU.is_equal, ALU.mult,
                                              accum_out=cnt[:, t, 3:4]))
                    settle()
                v.sem_inc(sbc_free, 1)
                go(v.tensor_reduce(rank[:], cnt[:], AX, ALU.add))
                settle()
                go(v.tensor_scalar(rank[:], rank[:], float(TOPK), None, ALU.is_lt))
                v.wait_ge(th_ok, 1)
                v.sem_inc(th_ok, -1)
                go(v.tensor_scalar(wm[:], th[:], 0.5, 0.5, ALU.mult, ALU.add))
                settle()
                go(v.tensor_tensor(wm[:], wm[:], rank[:], ALU.mult))
                restart()

            def residual_and_norm(p):
                v.wait_ge(mr_in[p], 16)
                v.sem_inc(mr_in[p], -16)
                v.wait_ge(x_in2, 16)
                v.sem_inc(x_in2, -16)
                v.wait_ge(o_out[p], 16 * NF)
                v.sem_inc(o_out[p], -16 * NF)
                ga, sb_, cb = (mrow[:, p, n].unsqueeze(1) for n in range(3))
                for f in range(NF):
                    v.wait_ge(proj_full, f + 1)
                    go(v.tensor_tensor(t1[:].rearrange("p (t d) -> p t d", d=D),
                                       bank[PROJ + f % 2][:, :].rearrange("p (t d) -> p t d", d=D),
                                       ga.broadcast_to([P, 2, D]), ALU.mult))
                    settle()
                    v.sem_inc(proj_free, 1)
                    go(v.tensor_tensor(x1[:, p, 2 * f:2 * f + 2], t1[:].rearrange("p (t d) -> p t d", d=D),
                                       xin[:, 2 * f:2 * f + 2], ALU.add))
                    settle()
                    for t in (2 * f, 2 * f + 1):
                        go(v.bn_stats(stats[:, t], x1[:, p, t]))
                v.sem_inc(proj_full, -NF)
                v.sem_inc(x_used, 1)
                settle()
                for t in range(NB):
                    go(v.bn_aggr(mv[:, t], stats[:, t]))
                settle()
                v.tensor_scalar(veps[:], mv[:, :, 1], EPS, None, ALU.add).then_inc(var_ok, 1)
                v.wait_ge(rstd_ok, 1)
                v.sem_inc(rstd_ok, -1)
                go(v.scalar_tensor_tensor(nmr[:], mv[:, :, 0], -1.0, rstd[:], ALU.mult, ALU.mult))
                settle()
                v.wait_ge(h2_used, 1)
                v.sem_inc(h2_used, -1)
                for t in range(NB):
                    go(v.tensor_scalar(h2[:, t], x1[:, p, t], rstd[:, t:t + 1], nmr[:, t:t + 1], ALU.mult, ALU.add))
                settle()
                go(v.tensor_tensor(h2[:], h2[:], cb.broadcast_to([P, NB, D]), ALU.mult))
                settle()
                go(v.tensor_tensor(h2[:], h2[:], sb_.broadcast_to([P, NB, D]), ALU.add))
                restart()
                v.sem_inc(h2_ok, 1)
                v.sem_inc(x1_ok, 1)

            def update(p):
                v.wait_ge(y_free, 1)
                v.sem_inc(y_free, -1)
                for f in range(NF):
                    v.wait_ge(down_full, f + 1)
                    go(v.tensor_tensor(y[:, 2 * f:2 * f + 2], bank[DOWN + f][:, :].rearrange("p (t d) -> p t d", d=D),
                                       w["b2_bc"][:].unsqueeze(1).broadcast_to([P, 2, D]), ALU.add))
                    settle()
                    v.sem_inc(down_free, 1)
                    for t in (2 * f, 2 * f + 1):
                        v.scalar_tensor_tensor(y[:, t], y[:, t], wm[:, t:t + 1], mrow[:, p, 3], ALU.mult, ALU.mult
                                               ).then_inc(y_ok, 1)
                v.sem_inc(down_full, -NF)

            for p in range(2):
                v.sem_inc(o_out[p], 16 * NF)
            v.sem_inc(h2_used, 1)
            v.sem_inc(y_free, 1)
            v.memset(cnt[:], 0.0)
            residual_and_norm(0)

            def step(b, p, left):
                ranks()
                if left >= 1:
                    residual_and_norm(1 - p)
                update(p)
                restart()

            run_steps(v, step)
            for p in range(2):
                v.wait_ge(o_out[p], 16 * NF)

        @blk.gpsimd
        def _(pool):
            def root():
                pool.wait_ge(var_ok, 1)
                pool.sem_inc(var_ok, -1)
                pool.tensor_tensor(rstd[:], veps[:], w["mhalf2"][:], ALU.pow).then_inc(rstd_ok, 1)

            root()

            def step(b, p, left):
                pool.wait_ge(x1_ok, 1)
                pool.sem_inc(x1_ok, -1)
                pool.tensor_tensor(gh[:], h2[:], mrow[:, p, 3].unsqueeze(1).broadcast_to([P, NB, D]), ALU.mult
                                   ).then_inc(pool_step, 1)
                pool.wait_ge(pool_step, 1)
                pool.sem_inc(h2_used, 1)
                pool.tensor_tensor(x1[:, p], x1[:, p], gh[:], ALU.add).then_inc(pool_step, 1)
                pool.wait_ge(pool_step, 2)
                if left >= 1:
                    root()
                for f in range(NF):
                    pool.wait_ge(y_ok, 2 * (f + 1))
                    if f == NF - 1:
                        pool.sem_inc(mr_used, 1)
                    pool.tensor_tensor(x1[:, p, 2 * f:2 * f + 2], x1[:, p, 2 * f:2 * f + 2], y[:, 2 * f:2 * f + 2],
                                       ALU.add).then_inc(pool_step, 1)
                    pool.wait_ge(pool_step, 3 + f)
                    pool.sem_inc(o_ok, 1)
                pool.sem_inc(y_free, 1)
                pool.sem_inc(y_ok, -NB)
                pool.sem_inc(pool_step, -(2 + NF))

            run_steps(pool, step)


def build(nc, io, out, nbatch=B):
    dr = scratch(nc)
    with ExitStack() as ctx:
        ident = ctx.enter_context(nc.sbuf_tensor("ident", [P, P], F32))
        with ExitStack() as c1:
            def sb(name, shape, dt=F32):
                return c1.enter_context(nc.sbuf_tensor(name, shape, dt))
            w = dict(ident=ident, mhalf=sb("mhalf", [P, NB]), rk_bc=sb("rk_bc", [P, 2, DK]), rv_bc=sb("rv_bc", [P, 2, DK]),
                     rk_col=sb("rk_col", [P, 1]), wqT=sb("wqT", [P, KT, D]), wkT=sb("wkT", [P, KT, D]),
                     wvT=sb("wvT", [P, KT, D]), wcT=sb("wcT", [P, KT, H]))
            setup_project(nc, io, dr, w)
            project(nc, io, dr, w, nbatch)
        with ExitStack() as c2:
            def sb(name, shape, dt=F32):
                return c2.enter_context(nc.sbuf_tensor(name, shape, dt))
            w = dict(ident=ident, identb=sb("identb", [P, P], BF16), qpk=sb("qpk", [C_ROWS, 3, HB * S], BF16),
                     kpk=sb("kpk", [C_ROWS, 3, HB * S], BF16), rkp=sb("rkp", [ROWS, TA + TB], BF16),
                     rvt=sb("rvt", [P, XW, DK]), spread=sb("spread", [HB, P]))
            setup_attend(nc, io, dr, w)
            attend(nc, dr, w, nbatch * NG)
        with ExitStack() as c3:
            def sb(name, shape, dt=F32):
                return c3.enter_context(nc.sbuf_tensor(name, shape, dt))
            w = dict(ident=ident, mhalf2=sb("mhalf2", [P, NB]), before=sb("before", [P, P]), woT=sb("woT", [P, NG, D]),
                     w1=sb("w1", [P, KT, F]), w2=sb("w2", [P, FT, D]), b1c=sb("b1c", [P, FT]), b2_bc=sb("b2_bc", [P, D]),
                     wr=sb("wr", [P, KT]), wr_bc=sb("wr_bc", [P, KT, P]))
            setup_ffn(nc, io, w)
            ffn(nc, io, dr, out, w, nbatch)


_INS = {"x": "L0_attn_x", "Wq": "L0_attn_Wq", "Wk": "L0_attn_Wk", "Wv": "L0_attn_Wv", "Wo": "L0_attn_Wo",
        "b_o": "L0_attn_b_o", "rel_k": "L0_attn_rel_k_emb", "rel_v": "L0_attn_rel_v_emb",
        "w_router": "L0_ffn_w_router", "W1": "L0_ffn_W1", "b1": "L0_ffn_b1", "W2": "L0_ffn_W2",
        "b2": "L0_ffn_b2", "c": "L0_c", "wmod": "L0_wmod"}


def kernel(**inputs):
    import numpy as _np
    import concourse.bacc as _bacc
    from concourse.bass_utils import run_bass_kernel_spmd as _run

    nc = _bacc.Bacc("TRN2", target_bir_lowering=False, num_devices=1)
    arrays, io = {}, {}
    for short, name in _INS.items():
        a = _np.ascontiguousarray(inputs[name])
        arrays[f"in_{name}_dram"] = a
        io[short] = nc.dram_tensor(f"in_{name}_dram", a.shape, mybir.dt.from_np(a.dtype), kind="ExternalInput").ap()
    out = nc.dram_tensor("out_0_dram", (B, S, D), F32, kind="ExternalOutput").ap()
    build(nc, io, out)
    return _run(nc, [arrays], core_ids=[0]).results[0]["out_0_dram"]
```

```python
from contextlib import ExitStack

import concourse.bass as bass
from concourse import mybir

F32 = mybir.dt.float32
BF16 = mybir.dt.bfloat16
ALU = mybir.AluOpType
ACT = mybir.ActivationFunctionType
AX = mybir.AxisListType.X

P = 128
B, S, D = 16, 1024, 256
H, DK = 16, 16
R = 32
NR = 2 * R + 1
KT = D // P
NB = S // P
HB = 4
NG = H // HB
CH = 512
NC = S // CH
XW = P + 2 * R
F = 1024
FT = F // P
TOPK = S // 2
EPS = 1e-5
SCALE = 1.0 / 4.0
Q_PARTS = (0, 1, 2, 0, 1, 0)
K_PARTS = (0, 1, 0, 1, 0, 2)
ROWS = 6 * DK
M_ROWS = ROWS + 2
C_ROWS = ROWS + 5


def scratch(nc):
    def t(name, shape, dt=F32):
        return nc.dram_tensor(name, shape, dt).ap()
    return dict(
        mod_row=t("mod_row", [B, 4 * D]),
        mod_col=t("mod_col", [B, P, 2 * KT]),
        q=t("q_parts", [B * NG, 3, DK, HB * S], BF16),
        k=t("k_parts", [B * NG, 3, DK, HB * S], BF16),
        c=t("c_parts", [B * NG, 5, HB * S], BF16),
        v=t("v_both", [B * NG, NB, P, DK * 2 * HB]),
        ctx=t("ctx", [B * NG, P, S]),
        relv=t("relv_ext", [XW + P, DK]),
    )




def setup_project(nc, io, dr, w):
    with ExitStack() as ctx:
        def tmp(name, shape, dt=F32):
            return ctx.enter_context(nc.sbuf_tensor(name, shape, dt))

        wnat = tmp("wnat", [P, 3, KT, D])
        cT = tmp("cT", [P, KT, B])
        cth = tmp("cth", [P, KT, B])
        csl = tmp("csl", [P, KT, B])
        wmod = tmp("wmod", [P, KT, 6 * D])
        mod = tmp("mod", [B, 6 * D])
        sgn = tmp("sgn", [B, 2, D])
        modr = tmp("modr", [B, 4, D])
        modc = tmp("modc", [P, B, 2 * KT])
        dl = tmp("dl", [P, DK])
        wcm = tmp("wcm", [P, KT, D])
        zero = tmp("zero", [P, 2 * HB * S], BF16)
        pt = [ctx.enter_context(nc.psum_tensor(f"pt{i}", [P, CH], F32)) for i in range(8)]
        loaded = ctx.enter_context(nc.semaphore("loaded"))
        ident_z = ctx.enter_context(nc.semaphore("ident_z"))
        ident_ok = ctx.enter_context(nc.semaphore("ident_ok"))
        zero_ok = ctx.enter_context(nc.semaphore("zero_ok"))
        tanh_ok = ctx.enter_context(nc.semaphore("tanh_ok"))
        dve = ctx.enter_context(nc.semaphore("dve_step"))
        turned = ctx.enter_context(nc.semaphore("turned"))
        modded = ctx.enter_context(nc.semaphore("modded"))
        stored = ctx.enter_context(nc.semaphore("stored"))
        silu_ok = ctx.enter_context(nc.semaphore("silu_ok"))
        mod_ok = ctx.enter_context(nc.semaphore("mod_ok"))
        blk = ctx.enter_context(nc.Block())
        N_LOADS = 11

        @blk.sync
        def _(sp):
            for n, name in enumerate(("Wq", "Wk", "Wv")):
                sp.dma_start(wnat[:, n], io[name].rearrange("(t p) k -> p t k", p=P)).then_inc(loaded, 16)
            for kt in range(KT):
                sp.dma_start(cT[:, kt], io["c"].rearrange("b (t p) -> t p b", p=P)[kt],
                             allow_slow_non_contiguous=True).then_inc(loaded, 16)
            sp.dma_start(wmod[:], io["wmod"].rearrange("(t p) n -> p t n", p=P)).then_inc(loaded, 16)
            rk, rv = io["rel_k"], io["rel_v"]
            sp.dma_start(w["rk_bc"][:, 0], bass.AP(rk.tensor, 0, [[0, P], [1, DK]])).then_inc(loaded, 16)
            sp.dma_start(w["rk_bc"][:, 1], bass.AP(rk.tensor, 2 * R * DK, [[0, P], [1, DK]])).then_inc(loaded, 16)
            sp.dma_start(w["rv_bc"][:], bass.AP(rv.tensor, 0, [[0, P], [2 * R * DK, 2], [1, DK]])).then_inc(loaded, 16)
            for g in range(2):
                sp.dma_start(w["rk_col"][g * 64:(g + 1) * 64], bass.AP(rk.tensor, 0, [[1, DK], [0, HB], [1, 1]]),
                             allow_slow_non_contiguous=True).then_inc(loaded, 16)
            ext = dr["relv"]
            sp.dma_start(ext[0:P - 1], bass.AP(rv.tensor, 0, [[0, P - 1], [1, DK]])).then_inc(stored, 16)
            sp.dma_start(ext[P - 1:P - 1 + NR], rv[:, :]).then_inc(stored, 16)
            rest = XW + P - (P - 1 + NR)
            sp.dma_start(ext[P - 1 + NR:], bass.AP(rv.tensor, 2 * R * DK, [[0, rest], [1, DK]])).then_inc(stored, 16)
            sp.wait_ge(zero_ok, 2)
            sp.dma_start(dr["c"][:, 0:2, :].rearrange("g r t -> g (r t)"), zero[0:B * NG, :]).then_inc(stored, 16)
            sp.wait_ge(mod_ok, 2)
            sp.dma_start(dr["mod_row"], modr[:].rearrange("b f d -> b (f d)")).then_inc(stored, 16)
            sp.dma_start(dr["mod_col"].rearrange("b p c -> p b c"), modc[:],
                         allow_slow_non_contiguous=True).then_inc(stored, 16)
            sp.wait_ge(stored, 16 * (3 + 1 + 2))

        @blk.gpsimd
        def _(pool):
            pool.memset(w["ident"][:], 0.0).then_inc(ident_z, 1)
            pool.wait_ge(ident_z, 1)
            pool.affine_select(out=w["ident"][:], in_=w["ident"][:], compare_op=ALU.not_equal, fill=1.0,
                               base=0, pattern=[[-1, P]], channel_multiplier=1).then_inc(ident_ok, 1)
            pool.memset(zero[:], 0.0).then_inc(zero_ok, 1)
            pool.memset(w["mhalf"][:], -0.5).then_inc(zero_ok, 1)

        @blk.scalar
        def _(act):
            act.wait_ge(loaded, 16 * N_LOADS)
            act.activation(cth[:], cT[:], ACT.Tanh, scale=0.5).then_inc(tanh_ok, 1)

        @blk.tensor
        def _(pe):
            pe.wait_ge(loaded, 16 * N_LOADS)
            pe.wait_ge(ident_ok, 1)
            for n in range(3):
                for kt in range(KT):
                    for nt in range(KT):
                        mm = pe.transpose(pt[n * KT + kt][:, nt * P:(nt + 1) * P],
                                          wnat[:, n, nt, kt * P:(kt + 1) * P], w["ident"][:])
            mm.then_inc(turned, 1)
            pe.wait_ge(silu_ok, 1)
            for n in range(3):
                for kt in range(KT):
                    mm = pe.matmul(pt[(6, 7, 0)[n]][0:B, :], csl[:, kt], wmod[:, kt, n * CH:(n + 1) * CH],
                                   start=(kt == 0), stop=(kt == KT - 1))
            for n in range(2 * KT):
                for kt in range(KT):
                    mm = pe.matmul(pt[1][:, n * B:(n + 1) * B], wmod[:, kt, n * P:(n + 1) * P], csl[:, kt],
                                   start=(kt == 0), stop=(kt == KT - 1))
            mm.then_inc(modded, 1)

        @blk.vector
        def _(v):
            steps = 0

            def done(ins):
                nonlocal steps
                steps += 1
                ins.then_inc(dve, 1)
                v.wait_ge(dve, steps)

            v.wait_ge(loaded, 16 * N_LOADS)
            done(v.tensor_tensor(dl[:], w["rk_bc"][:, 1], w["rk_bc"][:, 0], ALU.subtract))
            v.wait_ge(turned, 1)
            for n, name in enumerate(("wqT", "wkT")):
                for kt in range(KT):
                    src = pt[n * KT + kt][:, 0:D].rearrange("k (g h d) -> k g d h", g=NG, h=HB)
                    for g in range(NG):
                        done(v.tensor_copy(w[name][:, kt, g * 64:(g + 1) * 64].rearrange("k (d h) -> k d h", h=HB),
                                           src[:, g]))
            for kt in range(KT):
                done(v.tensor_copy(w["wvT"][:, kt], pt[2 * KT + kt][:, 0:D]))
            for kt in range(KT):
                for h in range(H):
                    c0 = h * DK
                    done(v.tensor_tensor(wcm[:, kt, c0:c0 + DK], pt[kt][:, c0:c0 + DK], dl[:], ALU.mult))
                done(v.tensor_reduce(w["wcT"][:, kt], wcm[:, kt].rearrange("k (h d) -> k h d", d=DK), AX, ALU.add))
            v.wait_ge(tanh_ok, 1)
            done(v.tensor_scalar(cth[:], cth[:], 0.5, 0.5, ALU.mult, ALU.add))
            v.tensor_tensor(csl[:], cth[:], cT[:], ALU.mult).then_inc(silu_ok, 1)
            v.wait_ge(modded, 1)
            for n in range(3):
                done(v.tensor_copy(mod[:, n * CH:(n + 1) * CH], pt[(6, 7, 0)[n]][0:B, :]))
            for n, src, dst in ((0, 2, 0), (1, 5, 3)):
                g = mod[:, src * D:(src + 1) * D]
                done(v.tensor_scalar(sgn[:, n], g, 0.0, 2.0, ALU.is_ge, ALU.mult))
                done(v.tensor_scalar(sgn[:, n], sgn[:, n], -1.0, None, ALU.add))
                done(v.tensor_scalar(modr[:, dst], g, -1.0, None, ALU.mult))
                done(v.tensor_tensor(modr[:, dst], modr[:, dst], g, ALU.max))
                done(v.tensor_scalar(modr[:, dst], modr[:, dst], 0.25, None, ALU.max))
                done(v.tensor_tensor(modr[:, dst], modr[:, dst], sgn[:, n], ALU.mult))
            done(v.tensor_copy(modr[:, 1], mod[:, 3 * D:4 * D]))
            v.tensor_scalar(modr[:, 2], mod[:, 4 * D:5 * D], 1.0, None, ALU.add).then_inc(mod_ok, 1)
            mc = pt[1][:, 0:2 * KT * B].rearrange("p (c b) -> p b c", b=B)
            done(v.tensor_copy(modc[:, :, 0:KT], mc[:, :, 0:KT]))
            v.tensor_scalar(modc[:, :, KT:2 * KT], mc[:, :, KT:2 * KT], 1.0, None, ALU.add).then_inc(mod_ok, 1)


def project(nc, io, dr, w, nbatch=B):
    with ExitStack() as ctx:
        def sb(name, shape, dt=F32):
            return ctx.enter_context(nc.sbuf_tensor(name, shape, dt))

        def sem(name):
            return ctx.enter_context(nc.semaphore(name))

        xin = sb("xin", [P, 2, NB, D])
        mcol = sb("mcol", [P, 2, 2 * KT])
        stats = sb("stats", [P, NB, 6])
        mv = sb("mv", [P, NB, 2])
        veps = sb("veps", [P, NB])
        rstd = sb("rstd", [P, NB])
        nmr = sb("nmr", [P, NB])
        nrm = sb("nrm", [P, NB, D])
        hT = sb("hT", [P, 2, KT, S])
        part1 = sb("part1", [P, 2, 5, S], BF16)
        part2 = sb("part2", [P, 2, 5, S], BF16)
        part3 = sb("part3", [P, 2, 5, S], BF16)
        RESTS = 4
        rest = sb("rest", [P, RESTS, CH])
        vout = sb("vout", [P, 2, 2, NG, DK, 2, HB])
        NP_ = 7
        ps = [ctx.enter_context(nc.psum_tensor(f"ps{i}", [P, CH], F32)) for i in range(NP_)]
        tp = ctx.enter_context(nc.psum_tensor("tp", [P, CH], F32))

        x_in = [sem(f"x_in{i}") for i in range(2)]
        m_in = [sem(f"m_in{i}") for i in range(2)]
        x_free, m_free = sem("x_free"), sem("m_free")
        normed, nrm_free = sem("normed"), sem("nrm_free")
        tp_full, tp_free = sem("tp_full"), sem("tp_free")
        qkc_full, v_full, ps_free, ps_v_free = sem("qkc_full"), sem("v_full"), sem("ps_free"), sem("ps_v_free")
        part1_ok, rest_ok, rest_free = sem("part1_ok"), sem("rest_ok"), sem("rest_free")
        part2_ok = sem("part2_ok")
        pool_step, dve_step = sem("pool_step"), sem("dve_step2")
        parts_ok, parts_free = sem("parts_ok"), sem("parts_free")
        parts_out = [sem(f"parts_out{i}") for i in range(2)]
        v_ok = sem("v_ok")
        v_out = [sem(f"v_out{i}") for i in range(2)]
        var_ok, rstd_ok = sem("var_ok"), sem("rstd_ok")
        blk = ctx.enter_context(nc.Block())

        QK = 8
        FILLS = QK + NC + NB // 2
        bank = lambda f: ps[f % NP_]
        STORES = 3 * (QK // 2) + 3
        NORM_AT = 3
        TURN_AT = (7, 9, 11, 13)

        def load(sp, b, p):
            sp.dma_start(xin[:, p], io["x"][bass.ds(b, 1)].rearrange("o (t p) d -> p (o t) d", p=P)).then_inc(x_in[p], 16)
            sp.dma_start(mcol[:, p], dr["mod_col"][bass.ds(b, 1)].rearrange("o p c -> (o p) c")).then_inc(m_in[p], 16)

        @blk.sync
        def _(sp):
            load(sp, 0, 0)

            def step(b, p, last):
                if not last:
                    sp.wait_ge(x_free, 1)
                    sp.wait_ge(m_free, 1)
                    load(sp, b + 1, 1 - p)
                    sp.sem_inc(x_free, -1)
                    sp.sem_inc(m_free, -1)
                sp.wait_ge(parts_out[p], 16 * STORES)
                sp.sem_inc(parts_out[p], -16 * STORES)
                sp.sem_inc(parts_free, 1)
                for m in range(QK // 2):
                    sp.wait_ge(parts_ok, 2 * (m + 1))
                    dst = dr["q"] if m < KT else dr["k"]
                    for n, part in enumerate((part1, part2, part3)):
                        to = dst[bass.ds(b * NG + m % KT * 2, 2), n].rearrange("g d (h t) -> g (d h) t", h=HB)
                        sp.dma_start(to, part[:, p, m]).then_inc(parts_out[p], 16)
                sp.wait_ge(parts_ok, QK + NC)
                for n, part in enumerate((part1, part2, part3)):
                    to = dr["c"][bass.ds(b * NG, NG), 2 + n].rearrange("g (h t) -> g h t", h=HB)
                    sp.dma_start(to, part[0:H, p, 4]).then_inc(parts_out[p], 16)
                sp.sem_inc(parts_ok, -(QK + NC))
                for f in range(NB // 2):
                    sp.wait_ge(v_ok, f + 1)
                    for k in range(2):
                        to = dr["v"][bass.ds(b * NG, NG), 2 * f + k].rearrange("g p c -> p g c")
                        sp.dma_start(to, vout[:, f % 2, k].rearrange("p g d r h -> p g (d r h)")
                                     ).then_inc(v_out[f % 2], 16)
                sp.sem_inc(v_ok, -(NB // 2))

            for p in range(2):
                sp.sem_inc(parts_out[p], 16 * STORES)
            sp.sem_inc(x_free, 1)
            sp.sem_inc(m_free, 1)
            if nbatch > 2:
                with sp.Fori(0, nbatch - 2, 2) as b:
                    for p in range(2):
                        step(b + p, p, False)
            step(nbatch - 2, 0, False)
            step(nbatch - 1, 1, True)
            for p in range(2):
                sp.wait_ge(parts_out[p], 16 * STORES)

        @blk.vector
        def _(v):
            for r in range(2):
                v.sem_inc(v_out[r], 32)

            def norm(p, first):
                v.wait_ge(x_in[p], 16)
                v.sem_inc(x_in[p], -16)
                for t in range(NB):
                    v.bn_stats(stats[:, t], xin[:, p, t]).then_inc(dve_step, 1)
                v.wait_ge(dve_step, NB)
                for t in range(NB):
                    v.bn_aggr(mv[:, t], stats[:, t]).then_inc(dve_step, 1)
                v.wait_ge(dve_step, 2 * NB)
                v.tensor_scalar(veps[:], mv[:, :, 1], EPS, None, ALU.add).then_inc(var_ok, 1)
                v.wait_ge(rstd_ok, 1)
                v.sem_inc(rstd_ok, -1)
                v.scalar_tensor_tensor(nmr[:], mv[:, :, 0], -1.0, rstd[:], ALU.mult, ALU.mult).then_inc(dve_step, 1)
                v.wait_ge(dve_step, 2 * NB + 1)
                if not first:
                    v.wait_ge(nrm_free, 1)
                    v.sem_inc(nrm_free, -1)
                for t in range(NB):
                    v.tensor_scalar(nrm[:, t], xin[:, p, t], rstd[:, t:t + 1], nmr[:, t:t + 1],
                                    ALU.mult, ALU.add).then_inc(dve_step, 1)
                v.wait_ge(dve_step, 3 * NB + 1)
                v.sem_inc(normed, 1)
                v.sem_inc(x_free, 1)
                v.sem_inc(dve_step, -(3 * NB + 1))

            norm(0, True)

            def step(p, last):
                for f in range(QK + NC):
                    rows = P if f < QK else H
                    if f == NORM_AT and not last:
                        norm(1 - p, False)
                    v.wait_ge(part1_ok, f + 1)
                    if f >= RESTS:
                        v.wait_ge(rest_free, f - RESTS + 1)
                    col = f % NC * CH
                    first = part1[0:rows, p, f // 2, col:col + CH]
                    if QK // 2 <= f < QK:
                        v.scalar_tensor_tensor(rest[0:rows, f % RESTS], bank(f)[0:rows, :], w["rk_col"][:, 0:1], first,
                                               ALU.add, ALU.subtract).then_inc(rest_ok, 1)
                    else:
                        v.tensor_tensor(rest[0:rows, f % RESTS], bank(f)[0:rows, :], first, ALU.subtract).then_inc(rest_ok, 1)
                v.sem_inc(part1_ok, -(QK + NC))
                v.wait_ge(rest_free, QK + NC)
                v.sem_inc(rest_free, -(QK + NC))
                for f in range(NB // 2):
                    v.wait_ge(v_full, f + 1)
                    v.wait_ge(v_out[f % 2], 32)
                    v.sem_inc(v_out[f % 2], -32)
                    src = bank(QK + NC + f)[:, :].rearrange("p (g h d) -> p g h d", g=2 * NG, h=HB)
                    for r in range(2):
                        add = w["rv_bc"][:, r].unsqueeze(1).unsqueeze(1).broadcast_to([P, 2 * NG, HB, DK])
                        to = vout[:, f % 2, :, :, :, r].rearrange("p k g d h -> p (k g) h d")
                        v.tensor_tensor(to, src, add, ALU.add).then_inc(dve_step, 1)
                    v.wait_ge(dve_step, 2 * (f + 1))
                    v.sem_inc(ps_v_free, 1)
                    v.sem_inc(v_ok, 1)
                v.sem_inc(dve_step, -NB)
                v.sem_inc(v_full, -(NB // 2))

            if nbatch > 2:
                with v.Fori(0, nbatch - 2, 2):
                    for p in range(2):
                        step(p, False)
            step(0, False)
            step(1, True)
            for r in range(2):
                v.wait_ge(v_out[r], 32)

        @blk.gpsimd
        def _(pool):
            def root():
                pool.wait_ge(var_ok, 1)
                pool.sem_inc(var_ok, -1)
                pool.tensor_tensor(rstd[:], veps[:], w["mhalf"][:], ALU.pow).then_inc(rstd_ok, 1)

            def step(p, last):
                if not last:
                    root()
                for f in range(QK + NC):
                    rows = P if f < QK else H
                    col = f % NC * CH
                    pool.wait_ge(part2_ok, f + 1)
                    pool.tensor_tensor(part3[0:rows, p, f // 2, col:col + CH], rest[0:rows, f % RESTS],
                                       part2[0:rows, p, f // 2, col:col + CH], ALU.subtract).then_inc(pool_step, 1)
                    pool.wait_ge(pool_step, f + 1)
                    pool.sem_inc(rest_free, 1)
                    pool.sem_inc(parts_ok, 1)
                pool.sem_inc(part2_ok, -(QK + NC))
                pool.sem_inc(pool_step, -(QK + NC))

            root()
            if nbatch > 2:
                with pool.Fori(0, nbatch - 2, 2):
                    for p in range(2):
                        step(p, False)
            step(0, False)
            step(1, True)

        @blk.scalar
        def _(act):
            def turn(n, p):
                kt, half = n % KT, n // KT
                act.wait_ge(tp_full, n + 1)
                act.activation(hT[:, p, kt, half * CH:(half + 1) * CH], tp[:, :], ACT.Identity,
                               scale=mcol[:, p, KT + kt:KT + kt + 1], bias=mcol[:, p, kt:kt + 1]).then_inc(tp_free, 1)

            def first_use(p):
                act.wait_ge(m_in[p], 16)
                act.sem_inc(m_in[p], -16)

            def split(f, p):
                rows = P if f < QK else H
                col = f % NC * CH
                act.wait_ge(qkc_full, f + 1)
                out, src = part1[0:rows, p, f // 2, col:col + CH], bank(f)[0:rows, :]
                if QK // 2 <= f < QK:
                    act.activation(out, src, ACT.Identity, bias=w["rk_col"][:, 0:1]).then_inc(part1_ok, 1)
                else:
                    act.activation(out, src, ACT.Copy).then_inc(part1_ok, 1)

            def split_again(f, p):
                rows = P if f < QK else H
                col = f % NC * CH
                act.wait_ge(rest_ok, f + 1)
                act.sem_inc(ps_free, 1)
                act.activation(part2[0:rows, p, f // 2, col:col + CH], rest[0:rows, f % RESTS], ACT.Copy
                               ).then_inc(part2_ok, 1)

            def step(p, last):
                act.wait_ge(parts_free, 1)
                act.sem_inc(parts_free, -1)
                if not last:
                    first_use(1 - p)
                for f in range(QK + NC):
                    split(f, p)
                    if f:
                        split_again(f - 1, p)
                    if f in TURN_AT and not last:
                        turn(TURN_AT.index(f), 1 - p)
                split_again(QK + NC - 1, p)
                if not last:
                    for n, f in enumerate(TURN_AT):
                        if f >= QK + NC:
                            turn(n, 1 - p)
                    act.sem_inc(tp_full, -2 * KT)
                act.sem_inc(rest_ok, -(QK + NC))
                act.sem_inc(qkc_full, -(QK + NC))

            first_use(0)
            for n in range(2 * KT):
                turn(n, 0)
            act.sem_inc(tp_full, -2 * KT)
            if nbatch > 2:
                with act.Fori(0, nbatch - 2, 2):
                    for p in range(2):
                        step(p, False)
            step(0, False)
            step(1, True)

        @blk.tensor
        def _(pe):
            def turn(n):
                kt, half = n % KT, n // KT
                if n:
                    pe.wait_ge(tp_free, n)
                for t in range(4):
                    mm = pe.transpose(tp[:, t * P:(t + 1) * P], nrm[:, 4 * half + t, kt * P:(kt + 1) * P], w["ident"][:])
                mm.then_inc(tp_full, 1)

            def fill(f, p):
                if f < QK:
                    m, c = f % (QK // 2) // 2, f % 2
                    wt = w["wqT"] if f < QK // 2 else w["wkT"]
                    for kt in range(KT):
                        mm = pe.matmul(bank(f)[:, :], wt[:, kt, m * P:(m + 1) * P], hT[:, p, kt, c * CH:(c + 1) * CH],
                                       start=(kt == 0), stop=(kt == KT - 1))
                    return mm.then_inc(qkc_full, 1)
                if f < QK + NC:
                    c = f - QK
                    for kt in range(KT):
                        mm = pe.matmul(bank(f)[0:H, :], w["wcT"][:, kt, :], hT[:, p, kt, c * CH:(c + 1) * CH],
                                       start=(kt == 0), stop=(kt == KT - 1))
                    return mm.then_inc(qkc_full, 1)
                for k in range(2):
                    t = 2 * (f - QK - NC) + k
                    for kt in range(KT):
                        mm = pe.matmul(bank(f)[:, k * D:(k + 1) * D], hT[:, p, kt, t * P:(t + 1) * P], w["wvT"][:, kt, :],
                                       start=(kt == 0), stop=(kt == KT - 1))
                return mm.then_inc(v_full, 1)

            for n in range(2 * KT):
                if n == 0:
                    pe.wait_ge(normed, 1)
                turn(n)
            pe.wait_ge(tp_free, 2 * KT)
            pe.sem_inc(tp_free, -2 * KT)
            pe.sem_inc(normed, -1)
            pe.sem_inc(nrm_free, 1)
            pe.sem_inc(m_free, 1)

            def bank_free(f):
                if f == 0:
                    pe.wait_ge(ps_free, QK + NC)
                    pe.sem_inc(ps_free, -(QK + NC))
                elif QK + NC - NP_ <= f < NP_:
                    pe.wait_ge(ps_v_free, f + NP_ - QK - NC + 1)
                    if f == NP_ - 1:
                        pe.sem_inc(ps_v_free, -(NB // 2))
                elif f >= NP_:
                    pe.wait_ge(ps_free, f - NP_ + 1)

            def step(p, last):
                for f in range(FILLS):
                    bank_free(f)
                    fill(f, p)
                    if f in TURN_AT and not last:
                        if f == TURN_AT[0]:
                            pe.wait_ge(normed, 1)
                        turn(TURN_AT.index(f))
                if not last:
                    pe.wait_ge(tp_free, 2 * KT)
                    pe.sem_inc(tp_free, -2 * KT)
                    pe.sem_inc(normed, -1)
                    pe.sem_inc(nrm_free, 1)
                    pe.sem_inc(m_free, 1)

            pe.sem_inc(ps_free, QK + NC)
            pe.sem_inc(ps_v_free, NB // 2)
            if nbatch > 2:
                with pe.Fori(0, nbatch - 2, 2):
                    for p in range(2):
                        step(p, False)
            step(0, False)
            step(1, True)



XA = XW - R
TA = XA + P - 1
TB = R + P - 1


def window(jb, c):
    lo, hi = max(jb * P - R, c * CH), min(jb * P + P + R, (c + 1) * CH)
    return (lo, hi) if lo < hi else None


def pieces(jb, c):
    lo, hi, at = c * CH, (c + 1) * CH, jb * P
    found = []
    if lo < at:
        found.append((1, lo, min(hi, at)))
    if hi > at:
        found.append((0, max(lo, at), hi))
    return found


NEAR = [(jb, c) for jb in range(NB) for c in range(NC) if window(jb, c)]
FAR = [(jb, c) for jb in range(NB) for c in range(NC) if not window(jb, c)]
QUADS = []
for n, near in enumerate(NEAR):
    QUADS.append(near)
    if n % 3 == 0 and len(FAR) > 2:
        QUADS.append(FAR.pop(0))
QUADS += FAR
NQ = len(QUADS)
WIN = [window(jb, c) is not None for jb, c in QUADS]
FIRST = [q == min(k for k in range(NQ) if QUADS[k][1] == QUADS[q][1]) for q in range(NQ)]
NWIN = sum(WIN)
NT = NQ * HB
RING = 3
XF = CH // (HB * NB)
DF = XW // XF
JOIN_AT, INVERT_AT, SPREAD_AT = 3, 9, (13, 16)
TABLE_AT = {19 + f * 43 // DF: f for f in range(DF)}


def setup_attend(nc, io, dr, w):
    with ExitStack() as ctx:
        def tmp(name, shape, dt=F32):
            return ctx.enter_context(nc.sbuf_tensor(name, shape, dt))
        rkT = tmp("rkT", [DK, NR])
        tab = tmp("tab", [DK, TA + TB])
        tp1, tp2, tp3 = (tmp(f"tabp{i}", [DK, TA + TB], BF16) for i in range(3))
        rvb = tmp("rvb", [P, 2, DK])
        loaded, dve = ctx.enter_context(nc.semaphore("tab_in")), ctx.enter_context(nc.semaphore("tab_step"))
        split, packed = ctx.enter_context(nc.semaphore("tab_split")), ctx.enter_context(nc.semaphore("tab_packed"))
        pool_step = ctx.enter_context(nc.semaphore("const_step"))
        blk = ctx.enter_context(nc.Block())

        @blk.sync
        def _(sp):
            sp.dma_start(rkT[:], io["rel_k"].rearrange("r d -> d r"), allow_slow_non_contiguous=True).then_inc(loaded, 16)
            rv, ext = io["rel_v"], dr["relv"]
            sp.dma_start(rvb[:], bass.AP(rv.tensor, 0, [[0, P], [2 * R * DK, 2], [1, DK]])).then_inc(loaded, 16)
            sp.dma_start(w["rvt"][:].rearrange("p x d -> p (x d)"),
                         bass.AP(ext.tensor, 0, [[DK, P], [1, XW * DK]])).then_inc(loaded, 16)
            sp.wait_ge(split, 1)
            for n, part in enumerate(K_PARTS):
                sp.dma_start(w["rkp"][n * DK:(n + 1) * DK], (tp1, tp2, tp3)[part][:]).then_inc(packed, 16)
            sp.wait_ge(packed, 16 * len(K_PARTS))

        @blk.gpsimd
        def _(pool):
            for b in range(3):
                pool.memset(w["kpk"][ROWS:C_ROWS, b], 1.0).then_inc(pool_step, 1)
            pool.memset(w["spread"][:], 1.0).then_inc(pool_step, 1)
            pool.wait_ge(pool_step, 4)
            pool.affine_select(out=w["spread"][:], in_=w["spread"][:], compare_op=ALU.is_ge, fill=0.0,
                               base=0, pattern=[[1, P]], channel_multiplier=-32).then_inc(pool_step, 1)
            pool.wait_ge(pool_step, 5)
            pool.affine_select(out=w["spread"][:], in_=w["spread"][:], compare_op=ALU.is_ge, fill=0.0,
                               base=31, pattern=[[-1, P]], channel_multiplier=32).then_inc(pool_step, 1)

        @blk.vector
        def _(v):
            steps = 0

            def done(ins):
                nonlocal steps
                steps += 1
                ins.then_inc(dve, 1)
                v.wait_ge(dve, steps)

            v.wait_ge(loaded, 48)
            done(v.memset(tab[:], 0.0))
            far = rkT[:, NR - 1:NR]
            done(v.tensor_scalar(tab[:, P - 1:P - 1 + NR], rkT[:], rkT[:, 0:1], None, ALU.subtract))
            done(v.tensor_scalar(tab[:, P - 1 + NR:TA], rkT[:, NR - 1:NR].broadcast_to([DK, TA - P + 1 - NR]),
                                 rkT[:, 0:1], None, ALU.subtract))
            done(v.tensor_scalar(tab[:, TA:TA + R], rkT[:, R + 1:NR], far, None, ALU.subtract))
            done(v.tensor_copy(tp1[:], tab[:]))
            done(v.tensor_tensor(tab[:], tab[:], tp1[:], ALU.subtract))
            done(v.tensor_copy(tp2[:], tab[:]))
            v.tensor_tensor(tp3[:], tab[:], tp2[:], ALU.subtract).then_inc(split, 1)
            for r, (lo, hi) in enumerate(((0, XA), (XA, XW))):
                done(v.tensor_tensor(w["rvt"][:, lo:hi], w["rvt"][:, lo:hi],
                                     rvb[:, r].unsqueeze(1).broadcast_to([P, hi - lo, DK]), ALU.subtract))
            done(v.tensor_copy(w["identb"][:], w["ident"][:]))


def attend(nc, dr, w, ngroups=B * NG):
    with ExitStack() as ctx:
        def sb(name, shape, dt=F32):
            return ctx.enter_context(nc.sbuf_tensor(name, shape, dt))

        def sem(name):
            return ctx.enter_context(nc.semaphore(name))

        qpk, kpk = w["qpk"], w["kpk"]
        vs = sb("vs", [P, 2, NB, DK + 1, 2 * HB])
        dt = sb("dt", [P, 3, HB, NB, XW])
        dh = sb("dh", [P, 2, HB, NB, XW], BF16)
        prob = sb("prob", [P, RING * HB, CH])
        tmax = sb("tmax", [P, HB * NB, NC])
        rmax = sb("rmax", [P, HB * NB])
        m1 = sb("m1", [HB * NB, P], BF16)
        m2 = sb("m2", [HB * NB, P], BF16)
        ctxs = sb("ctxs", [P, S])
        relvs = sb("relvs", [P, R, HB, NB])
        rs = sb("rs", [P, HB * S // P])
        rr = sb("rr", [P, HB * S // P])
        rrow = sb("rrow", [HB, S])
        pp = ctx.enter_context(nc.psum_tensor("pp", [P, 8 * CH], F32))
        bank = lambda n: pp[:, n * CH:(n + 1) * CH]
        ctxT = pp[:, 0:2 * CH]
        S_BANKS, ST_BANKS, RELV_BANK, SPARE = (2, 3), (6, 4, 5), 4, 7

        qk_in = [sem(f"qk_in{i}") for i in range(3)]
        v_in = [sem(f"v_in{i}") for i in range(2)]
        s_full, s_free = sem("s_full"), sem("s_free")
        st_win, st_plain, added = sem("st_win"), sem("st_plain"), sem("added")
        exp_ok = sem("exp_ok")
        pv_begun, pv_ok, win_ok = sem("pv_begun"), sem("pv_ok"), sem("win_ok")
        pwin_ok = sem("pwin_ok")
        ctx_full, ctx_pe, ctx_sp = sem("ctx_full"), sem("ctx_pe"), sem("ctx_sp")
        ctxs_free, ctx_out = sem("ctxs_free"), sem("ctx_out")
        rmax_ok, mT_full, m_ok, m_in = sem("rmax_ok"), sem("mT_full"), sem("m_ok"), sem("m_in")
        relv_full, relv_free, relvs_ok = sem("relv_full"), sem("relv_free"), sem("relvs_ok")
        rs_in, rr_ok, rrow_in = sem("rs_in"), sem("rr_ok"), sem("rrow_in")
        bc_full, bc_free, ctxn_ok = sem("bc_full"), sem("bc_free"), sem("ctxn_ok")
        d_full, dh_ok = sem("d_full"), sem("dh_ok")
        bufs_free, ones_ok = sem("bufs_free"), sem("ones_ok3")
        dve_step, pool_step, act_step = sem("dve_step3"), sem("pool_step3"), sem("act_step3")
        blk = ctx.enter_context(nc.Block())
        N_QK = 7

        def load_qk(sp, g, b3):
            def rows(src, to, lo, parts):
                n = len(parts)
                step = parts[1] - parts[0] if n > 1 else 1
                take = src[bass.ds(g, 1), parts[0]:parts[-1] + 1:step].rearrange("o n d t -> (o n) d t")
                sp.dma_start(to[lo:lo + n * DK, b3], take).then_inc(qk_in[b3], 16)
            rows(dr["q"], qpk, 0, Q_PARTS[0:3])
            rows(dr["q"], qpk, 3 * DK, Q_PARTS[3:5])
            rows(dr["q"], qpk, 5 * DK, Q_PARTS[5:6])
            for n in range(3):
                rows(dr["k"], kpk, 2 * n * DK, K_PARTS[2 * n:2 * n + 2])
            sp.dma_start(qpk[ROWS:C_ROWS, b3], dr["c"][bass.ds(g, 1)].rearrange("o r t -> (o r) t")).then_inc(qk_in[b3], 16)

        def load_v(sp, g, b2):
            sp.dma_start(vs[:, b2, :, 0:DK].rearrange("p j r c -> p j (r c)"),
                         dr["v"][bass.ds(g, 1)].rearrange("o j p c -> p (o j) c")).then_inc(v_in[b2], 16)

        def send_m(sp, b3):
            sp.wait_ge(m_ok, 1)
            sp.sem_inc(m_ok, -1)
            for n, m in enumerate((m1, m2)):
                sp.dma_start(qpk[ROWS + n:ROWS + n + 1, b3], m[:]).then_inc(m_in, 16)

        def run_steps(eng, step):
            step(0, 0, True, 3)
            n = (ngroups - 4) // 6 * 6
            if n:
                with eng.Fori(0, n // 6) as turn:
                    for k in range(1, 7):
                        step(turn * 6 + k, k % 6, False, 3)
            for g in range(n + 1, ngroups):
                step(g, g % 6, False, min(3, ngroups - 1 - g))

        @blk.sync
        def _(sp):
            for g in range(3):
                load_qk(sp, g, g)
            for g in range(2):
                load_v(sp, g, g)
            send_m(sp, 0)

            def finish(g):
                sp.wait_ge(ctx_sp, 1)
                sp.sem_inc(ctx_sp, -1)
                sp.dma_start(rs[:], ctxs[DK:P:32, :]).then_inc(rs_in, 16)
                sp.wait_ge(rr_ok, 1)
                sp.sem_inc(rr_ok, -1)
                sp.dma_start(rrow[:], rr[:]).then_inc(rrow_in, 16)
                sp.wait_ge(ctxn_ok, NC)
                sp.sem_inc(ctxn_ok, -NC)
                sp.dma_start(dr["ctx"][bass.ds(g, 1)].rearrange("o p t -> (o p) t"), ctxs[:]).then_inc(ctx_out, 16)
                sp.wait_ge(ctx_out, 16)
                sp.sem_inc(ctx_out, -16)

            def step(g, i, first, left):
                if not first:
                    finish(g - 1)
                sp.sem_inc(ctxs_free, 1)
                if left >= 1:
                    send_m(sp, (i + 1) % 3)
                if left >= 2:
                    sp.wait_ge(bufs_free, 1)
                    sp.sem_inc(bufs_free, -1)
                    if left >= 3:
                        load_qk(sp, g + 3, i % 3)
                    load_v(sp, g + 2, i % 2)

            run_steps(sp, step)
            finish(ngroups - 1)


        @blk.tensor
        def _(pe):
            def table(f, b3):
                q = qpk[0:ROWS, b3].rearrange("r (h j a) -> r a h j", h=HB, a=P)
                if f == 0:
                    pe.wait_ge(qk_in[b3], 16 * N_QK)
                    pe.sem_inc(qk_in[b3], -16 * N_QK)
                else:
                    pe.wait_ge(dh_ok, f)
                out = bank(SPARE).rearrange("p (x h j) -> p x h j", h=HB, j=NB)
                for k in range(XF):
                    x = f * XF + k
                    if x < R:
                        at, a, j0, j1, i0 = TA + R - 1 - x, P - R + x, 1, NB, 0
                    elif x < R + P:
                        at, a, j0, j1, i0 = XW - 1 - x, x - R, 0, NB, 0
                    else:
                        at, a, j0, j1, i0 = XW - 1 - x, x - R - P, 0, NB - 1, 1
                    mm = pe.matmul(out[:, k, :, j0:j1], w["rkp"][0:ROWS, at:at + P], q[:, a, :, i0:i0 + j1 - j0],
                                   start=True, stop=True)
                mm.then_inc(d_full, 1)

            def score_rows(t, b3, b2):
                h, ib, c = t // (NB * NC), t // NC % NB, t % NC
                out = bank(S_BANKS[t % 2])
                at = h * S + ib * P
                mms = []
                for j in range(2):
                    lo, hi = (c * CH, min((c + 1) * CH, (ib + 1) * P)) if j == 0 else (max(c * CH, (ib + 1) * P), (c + 1) * CH)
                    rows = (ROWS, C_ROWS)[j]
                    if lo < hi:
                        mms.append((out[:, lo - c * CH:hi - c * CH], qpk[0:rows, b3, at:at + P],
                                    kpk[0:rows, b3, h * S + lo:h * S + hi]))
                if ib // 4 == c:
                    o = ib % 4 * P
                    mms.append((out[:, o:o + P], dh[:, b2, h, ib, R:R + P], w["identb"][:]))
                if ib and (ib - 1) // 4 == c:
                    o = (ib - 1) % 4 * P + P - R
                    mms.append((out[0:R, o:o + R], dh[:, b2, h, ib - 1, R + P:XW], w["identb"][:, P - R:P]))
                if ib < NB - 1 and (ib + 1) // 4 == c:
                    o = (ib + 1) % 4 * P
                    mms.append((out[P - R:P, o:o + R], dh[:, b2, h, ib + 1, 0:R], w["identb"][:, 0:R]))
                for n, (o, l, r) in enumerate(mms):
                    mm = pe.matmul(o, l, r, start=(n == 0), stop=(n == len(mms) - 1), skip_group_check=True)
                mm.then_inc(s_full, 1)

            def score_cols(t, b3):
                (jb, c), h = QUADS[t // HB], t % HB
                out = bank(ST_BANKS[t % 3])
                at = h * S + jb * P
                for n, (far, lo, hi) in enumerate(pieces(jb, c)):
                    rows = C_ROWS if far else M_ROWS
                    mm = pe.matmul(out[:, lo - c * CH:hi - c * CH], kpk[0:rows, b3, at:at + P],
                                   qpk[0:rows, b3, h * S + lo:h * S + hi], start=(n == 0), stop=True,
                                   skip_group_check=True)
                mm.then_inc(st_win if WIN[t // HB] else st_plain, 1)

            def values(q, half, b2):
                jb, c = QUADS[q]
                begin, end = c * CH + half * CH // 2, c * CH + (half + 1) * CH // 2
                for far, lo, hi in pieces(jb, c):
                    lo, hi = max(lo, begin), min(hi, end)
                    for h in range(HB if lo < hi else 0):
                        mm = pe.matmul(ctxT[32 * h:32 * h + DK + 1, lo:hi], vs[:, b2, jb, :, far * HB + h],
                                       prob[:, q % RING * HB + h, lo - c * CH:hi - c * CH],
                                       start=(FIRST[q] and half == 0), stop=False, skip_group_check=True)
                if half == 1:
                    mm.then_inc(pv_ok, 1)
                elif WIN[q]:
                    mm.then_inc(pv_begun, 1)

            def relative_values(lo, hi, b3):
                win = dt[:, b3]
                half = R // 2
                for a in range(lo, hi):
                    out = bank(RELV_BANK + a // half).rearrange("p (a h i) -> p a h i", h=HB, i=NB)[:, a % half]
                    for q in range(4):
                        x = R * q + a + R
                        pe.matmul(out[32 * q:32 * q + DK], w["rvt"][:, XW - 1 - x], win[:, :, :, x],
                                  start=True, stop=(0 < q < 3), skip_group_check=True)
                    x = R + P + a
                    pe.matmul(out[0:DK, :, 1:NB], w["rvt"][:, XW - 1 - x], win[:, :, 0:NB - 1, x],
                              start=False, stop=True, skip_group_check=True)
                    mm = pe.matmul(out[96:96 + DK, :, 0:NB - 1], w["rvt"][:, XW - 1 - a], win[:, :, 1:NB, a],
                                   start=False, stop=True, skip_group_check=True)
                    if a % half == half - 1:
                        mm.then_inc(relv_full, 1)

            def turn_max():
                pe.wait_ge(rmax_ok, 1)
                pe.sem_inc(rmax_ok, -1)
                pe.transpose(bank(SPARE)[0:HB * NB, 0:P], rmax[:], w["ident"][:]).then_inc(mT_full, 1)

            def join():
                pe.wait_ge(relvs_ok, 1)
                pe.sem_inc(relvs_ok, -1)
                for q in range(4):
                    for c in range(NC):
                        for h in range(HB):
                            to = ctxT[32 * h:32 * h + DK, c * CH:(c + 1) * CH].rearrange("p (i a) -> p i a", a=P)
                            mm = pe.matmul(to[:, :, R * q:R * q + R], w["ident"][:, 32 * q:32 * q + DK],
                                           relvs[:, :, h, c * NB // 2:(c + 1) * NB // 2].rearrange("p a i -> p i a"),
                                           start=False, stop=True, skip_group_check=True)
                mm.then_inc(ctx_full, 1)

            def spread(c):
                if c == 0:
                    pe.wait_ge(rrow_in, 16)
                    pe.sem_inc(rrow_in, -16)
                else:
                    pe.wait_ge(bc_free, c)
                pe.matmul(bank(SPARE), w["spread"][:], rrow[:, c * CH:(c + 1) * CH],
                          start=True, stop=True).then_inc(bc_full, 1)

            def spread_taken():
                pe.wait_ge(bc_free, NC)
                pe.sem_inc(bc_free, -NC)

            for f in range(DF):
                table(f, 0)
            pe.wait_ge(dh_ok, DF)
            pe.sem_inc(dh_ok, -DF)
            for t in range(NT):
                if t >= 2:
                    pe.wait_ge(s_free, t - 1)
                score_rows(t, 0, 0)
            pe.wait_ge(s_free, NT)
            pe.sem_inc(s_free, -NT)
            turn_max()
            pe.wait_ge(m_in, 32)
            for f in range(DF):
                table(f, 1)
            pe.wait_ge(ones_ok, 2)
            pe.sem_inc(relv_free, 2)
            pe.sem_inc(ctx_pe, 1)

            def step(g, i, first, left):
                b3, n3, b2 = i % 3, (i + 1) % 3, i % 2
                pe.wait_ge(m_in, 32)
                pe.sem_inc(m_in, -32)
                for t in range(NT):
                    if t >= 3:
                        pe.wait_ge(exp_ok, t - 2)
                    elif t >= 1:
                        pe.wait_ge(relv_free, t)
                    score_cols(t, b3)
                    if left >= 1:
                        if t == 0:
                            pe.wait_ge(dh_ok, DF)
                            pe.sem_inc(dh_ok, -DF)
                        if t >= 2:
                            pe.wait_ge(s_free, t - 1)
                        score_rows(t, n3, 1 - b2)
                    if t % HB == 2 and t > HB:
                        if t // HB == 1:
                            pe.sem_inc(relv_free, -2)
                            pe.wait_ge(v_in[b2], 16)
                            pe.sem_inc(v_in[b2], -16)
                            pe.wait_ge(ctx_pe, 1)
                            pe.sem_inc(ctx_pe, -1)
                        values(t // HB - 1, 0, b2)
                    if t % HB == 0 and t > HB:
                        values(t // HB - 2, 1, b2)
                    if t == JOIN_AT and not first:
                        join()
                    if t in SPREAD_AT and not first:
                        spread(SPREAD_AT.index(t))
                    if t in TABLE_AT and left >= 2:
                        if TABLE_AT[t] == 0 and not first:
                            spread_taken()
                        table(TABLE_AT[t], (i + 2) % 3)
                pe.wait_ge(exp_ok, NT)
                pe.sem_inc(exp_ok, -NT)
                values(NQ - 2, 1, b2)
                values(NQ - 1, 0, b2)
                values(NQ - 1, 1, b2)
                pe.wait_ge(pwin_ok, 1)
                pe.sem_inc(pwin_ok, -1)
                relative_values(0, R // 4, b3)
                if left >= 2:
                    pe.wait_ge(dh_ok, DF)
                else:
                    spread_taken()
                if left >= 1:
                    pe.wait_ge(s_free, NT)
                    pe.sem_inc(s_free, -NT)
                    turn_max()
                relative_values(R // 4, R, b3)

            run_steps(pe, step)
            join()
            for c in range(NC):
                spread(c)


        @blk.scalar
        def _(act):
            def table_out(f, b3, b2):
                act.wait_ge(d_full, f + 1)
                x0 = f * XF
                j0 = 1 if x0 < R else 0
                j1 = NB - 1 if x0 >= R + P else NB
                src = bank(SPARE).rearrange("p (x h j) -> p h j x", h=HB, j=NB)
                act.activation(dt[:, b3, :, j0:j1, x0:x0 + XF], src[:, :, j0:j1, :], ACT.Copy)
                act.activation(dh[:, b2, :, j0:j1, x0:x0 + XF], src[:, :, j0:j1, :], ACT.Copy).then_inc(dh_ok, 1)
                if f == DF - 1:
                    act.sem_inc(d_full, -DF)

            def ring_free(q):
                act.wait_ge(pv_ok, q + 1)
                if WIN[q]:
                    act.wait_ge(win_ok, sum(WIN[:q + 1]))

            for b3 in range(2):
                for f in range(DF):
                    table_out(f, b3, b3)

            def context_out():
                act.wait_ge(ctx_full, 1)
                act.sem_inc(ctx_full, -1)
                act.wait_ge(ctxs_free, 1)
                act.sem_inc(ctxs_free, -1)
                act.activation(ctxs[:], ctxT, ACT.Copy).then_inc(act_step, 1)
                act.wait_ge(act_step, 1)
                act.sem_inc(act_step, -1)
                act.sem_inc(ctx_pe, 1)
                act.sem_inc(ctx_sp, 1)

            def step(g, i, first, left):
                n_win = n_plain = 0
                for t in range(NT):
                    q = t // HB
                    if t % HB == 0 and q >= RING:
                        ring_free(q - RING)
                    if WIN[q]:
                        n_win += 1
                        act.wait_ge(added, n_win)
                    else:
                        n_plain += 1
                        act.wait_ge(st_plain, n_plain)
                    act.activation(prob[:, q % RING * HB + t % HB], bank(ST_BANKS[t % 3]), ACT.Exp,
                                   scale=SCALE).then_inc(exp_ok, 1)
                    if t in TABLE_AT and left >= 2:
                        table_out(TABLE_AT[t], (i + 2) % 3, i % 2)
                    if t == JOIN_AT and not first:
                        context_out()
                act.sem_inc(added, -n_win)
                act.sem_inc(st_plain, -n_plain)
                act.wait_ge(win_ok, NWIN)
                act.wait_ge(pv_ok, NQ)
                act.sem_inc(win_ok, -NWIN)
                act.sem_inc(pv_ok, -NQ)
                if left >= 2:
                    act.sem_inc(bufs_free, 1)
                half = R // 2
                for k in range(2):
                    act.wait_ge(relv_full, k + 1)
                    act.activation(relvs[:, k * half:(k + 1) * half].rearrange("p a h i -> p (a h i)"),
                                   bank(RELV_BANK + k), ACT.Copy).then_inc(act_step, 1)
                    act.wait_ge(act_step, k + 1)
                    act.sem_inc(relv_free, 1)
                act.sem_inc(relvs_ok, 1)
                act.sem_inc(relv_full, -2)
                act.sem_inc(act_step, -2)

            run_steps(act, step)
            context_out()


        @blk.vector
        def _(v):
            def tile_max(t):
                v.wait_ge(s_full, t + 1)
                v.tensor_reduce(tmax[:, t // NC, t % NC:t % NC + 1], bank(S_BANKS[t % 2]), AX, ALU.max).then_inc(s_free, 1)

            def row_max():
                v.sem_inc(s_full, -NT)
                v.drain()
                v.tensor_reduce(rmax[:], tmax[:], AX, ALU.max).then_inc(rmax_ok, 1)
                v.wait_ge(mT_full, 1)
                v.sem_inc(mT_full, -1)
                src = bank(SPARE)[0:HB * NB, 0:P]
                v.tensor_scalar(m1[:], src, -1.0, None, ALU.mult).then_inc(dve_step, 1)
                v.wait_ge(dve_step, 1)
                v.sem_inc(dve_step, -1)
                v.scalar_tensor_tensor(m2[:], src, -1.0, m1[:], ALU.mult, ALU.subtract).then_inc(m_ok, 1)

            def invert():
                v.wait_ge(rs_in, 16)
                v.sem_inc(rs_in, -16)
                v.reciprocal(rr[:], rs[:]).then_inc(rr_ok, 1)

            def normalise(c):
                v.wait_ge(bc_full, 1)
                v.sem_inc(bc_full, -1)
                v.tensor_tensor(ctxs[:, c * CH:(c + 1) * CH], bank(SPARE), ctxs[:, c * CH:(c + 1) * CH],
                                ALU.mult).then_inc(dve_step, 1)
                v.wait_ge(dve_step, 1)
                v.sem_inc(dve_step, -1)
                v.sem_inc(bc_free, 1)
                v.sem_inc(ctxn_ok, 1)

            v.memset(vs[:, :, :, DK], 1.0).then_inc(ones_ok, 1)
            v.memset(ctxT, 0.0).then_inc(ones_ok, 1)
            for t in range(NT):
                tile_max(t)
            row_max()

            def step(g, i, first, left):
                n_win = 0
                for t in range(NT):
                    (jb, c), h = QUADS[t // HB], t % HB
                    if WIN[t // HB]:
                        n_win += 1
                        v.wait_ge(st_win, n_win)
                        lo, hi = window(jb, c)
                        x0 = lo - jb * P + R
                        cols = bank(ST_BANKS[t % 3])[:, lo - c * CH:hi - c * CH]
                        v.tensor_tensor(cols, cols, dt[:, i % 3, h, jb, x0:x0 + hi - lo], ALU.add).then_inc(added, 1)
                    if left >= 1:
                        tile_max(t)
                    if t == INVERT_AT and not first:
                        invert()
                    if t - 1 in SPREAD_AT and not first:
                        normalise(SPREAD_AT.index(t - 1))
                v.sem_inc(st_win, -n_win)
                if left >= 1:
                    row_max()

            run_steps(v, step)
            invert()
            for c in range(NC):
                normalise(c)


        @blk.gpsimd
        def _(pool):
            def copy_window(q, b3):
                jb, c = QUADS[q]
                n = sum(WIN[:q + 1])
                pool.wait_ge(pv_begun, n)
                lo, hi = window(jb, c)
                x0, s0 = lo - jb * P + R, q % RING * HB
                pool.tensor_copy(dt[:, b3, :, jb, x0:x0 + hi - lo],
                                 prob[:, s0:s0 + HB, lo - c * CH:hi - c * CH]).then_inc(pool_step, 1)
                pool.wait_ge(pool_step, n)
                pool.sem_inc(win_ok, 1)
                if n == NWIN:
                    pool.sem_inc(pwin_ok, 1)
                    pool.sem_inc(pv_begun, -NWIN)
                    pool.sem_inc(pool_step, -NWIN)

            def step(g, i, first, left):
                for t in range(NT):
                    q = t // HB - 1
                    if t % HB == HB - 1 and q >= 0 and WIN[q]:
                        copy_window(q, i % 3)

            run_steps(pool, step)




def setup_ffn(nc, io, w):
    with ExitStack() as ctx:
        wop = ctx.enter_context(nc.sbuf_tensor("wop", [P, KT, H, 32], F32))
        pt = [ctx.enter_context(nc.psum_tensor(f"wo_t{i}", [P, CH], F32)) for i in range(2)]
        loaded, const_step = ctx.enter_context(nc.semaphore("ffn_in")), ctx.enter_context(nc.semaphore("ffn_const"))
        wo_zero, turned = ctx.enter_context(nc.semaphore("wo_zero")), ctx.enter_context(nc.semaphore("wo_turned"))
        blk = ctx.enter_context(nc.Block())
        N_WO = 2 * KT

        @blk.sync
        def _(sp):
            sp.wait_ge(wo_zero, 1)
            for t in range(KT):
                sp.dma_start(wop[:, t, :, 0:DK], io["Wo"][t * P:(t + 1) * P, :].rearrange("p (h d) -> p h d", d=DK)
                             ).then_inc(loaded, 16)
                sp.dma_start(wop[:, t, 0, DK:DK + 1], io["b_o"][t * P:(t + 1) * P].rearrange("(p o) -> p o", o=1),
                             allow_slow_non_contiguous=True).then_inc(loaded, 16)
            sp.dma_start(w["w1"][:], io["W1"].rearrange("(t p) f -> p t f", p=P)).then_inc(loaded, 16)
            sp.dma_start(w["w2"][:], io["W2"].rearrange("(t p) f -> p t f", p=P)).then_inc(loaded, 16)
            sp.dma_start(w["b1c"][:], io["b1"].rearrange("(t p) -> p t", p=P), allow_slow_non_contiguous=True
                         ).then_inc(loaded, 16)
            sp.dma_start(w["b2_bc"][:], bass.AP(io["b2"].tensor, 0, [[0, P], [1, D]])).then_inc(loaded, 16)
            sp.dma_start(w["wr"][:], io["w_router"].rearrange("(t p) -> p t", p=P), allow_slow_non_contiguous=True
                         ).then_inc(loaded, 16)

        @blk.gpsimd
        def _(pool):
            pool.memset(w["mhalf2"][:], -0.5).then_inc(const_step, 1)
            pool.memset(w["before"][:], 1.0).then_inc(const_step, 1)
            pool.wait_ge(const_step, 2)
            pool.affine_select(out=w["before"][:], in_=w["before"][:], compare_op=ALU.is_ge, fill=0.0,
                               base=-1, pattern=[[-1, P]], channel_multiplier=1).then_inc(const_step, 1)

        @blk.tensor
        def _(pe):
            pe.wait_ge(loaded, 16 * (N_WO + 5))
            for hg in range(NG):
                for t in range(KT):
                    mm = pe.transpose(pt[hg // 2][:, hg % 2 * D + t * P:hg % 2 * D + (t + 1) * P],
                                      wop[:, t, hg * HB:(hg + 1) * HB].rearrange("p h c -> p (h c)"), w["ident"][:])
            mm.then_inc(turned, 1)

        @blk.vector
        def _(v):
            v.memset(wop[:], 0.0).then_inc(wo_zero, 1)
            v.wait_ge(turned, 1)
            for k in range(2):
                v.tensor_copy(w["woT"][:, 2 * k:2 * k + 2], pt[k][:, :].rearrange("p (g n) -> p g n", g=2))
            for kt in range(KT):
                v.tensor_copy(w["wr_bc"][:, kt], w["wr"][:, kt:kt + 1].broadcast_to([P, P]))


def ffn(nc, io, dr, out, w, nbatch=B):
    with ExitStack() as ctx:
        def sb(name, shape, dt=F32):
            return ctx.enter_context(nc.sbuf_tensor(name, shape, dt))

        def sem(name):
            return ctx.enter_context(nc.semaphore(name))

        cin = sb("cin", [P, NG, S])
        xin = sb("xin2", [P, NB, D])
        mrow = sb("mrow", [P, 2, 4, D])
        t1 = sb("t1", [P, CH])
        x1 = sb("x1", [P, 2, NB, D])
        h2 = sb("h2", [P, NB, D])
        gh = sb("gh", [P, NB, D])
        hT = sb("hT2", [P, KT, S])
        sbc = sb("sbc", [P, S])
        pick = sb("pick", [P, NB, P])
        scol = sb("scol", [P, NB])
        th = sb("th", [P, NB])
        junk = sb("junk", [P, S])
        cnt = sb("cnt", [P, NB, 4])
        rank = sb("rank", [P, NB])
        wm = sb("wm", [P, NB])
        gT = sb("gT", [P, FT, S])
        y = sb("y", [P, NB, D])
        stats = sb("stats2", [P, NB, 6])
        mv = sb("mv2", [P, NB, 2])
        veps, rstd, nmr = sb("veps2", [P, NB]), sb("rstd2", [P, NB]), sb("nmr2", [P, NB])
        bank = [ctx.enter_context(nc.psum_tensor(f"pf{i}", [P, CH], F32)) for i in range(8)]
        UP, PROJ, DOWN = 0, 2, 4
        NF = NB // 2
        NU = NC * FT
        NT_H = KT * NC

        x_in2, c_in = sem("x_in2"), sem("c_in")
        mr_in = [sem(f"mr_in{i}") for i in range(2)]
        x_used, mr_used = sem("x_used"), sem("mr_used")
        up_full, gelu_ok = sem("up_full"), sem("gelu_ok")
        proj_full, proj_free = sem("proj_full"), sem("proj_free")
        h2_ok, h2_used, x1_ok = sem("h2_ok"), sem("h2_used"), sem("x1_ok")
        turn_full, hT_ok = sem("turn_full"), sem("hT_ok")
        sc_full, sbc_ok, sbc_pe, sbc_free = sem("sc_full"), sem("sbc_ok"), sem("sbc_pe"), sem("sbc_free")
        scol_ok, th_ok = sem("scol_ok"), sem("th_ok")
        down_full, down_free = sem("down_full"), sem("down_free")
        y_ok, y_free, o_ok = sem("y_ok"), sem("y_free"), sem("o_ok")
        o_out = [sem(f"o_out{i}") for i in range(2)]
        var_ok, rstd_ok = sem("var_ok2"), sem("rstd_ok2")
        dve_step, act_step, pool_step = sem("dve_step4"), sem("act_step4"), sem("pool_step4")
        blk = ctx.enter_context(nc.Block())

        def run_steps(eng, step):
            if nbatch > 2:
                with eng.Fori(0, (nbatch - 2) // 2) as pair:
                    for p in range(2):
                        step(pair * 2 + p, p, 2)
            step(nbatch - 2, 0, 1)
            step(nbatch - 1, 1, 0)

        @blk.sync
        def _(sp):
            def load(b):
                sp.dma_start(xin[:], io["x"][bass.ds(b, 1)].rearrange("o (t p) d -> p (o t) d", p=P)).then_inc(x_in2, 16)
                sp.dma_start(cin[:], dr["ctx"][bass.ds(b * NG, NG)].rearrange("g p t -> p g t")).then_inc(c_in, 16)

            def load_rows(b, p):
                sp.dma_start(mrow[:, p].rearrange("p f d -> p (f d)"),
                             dr["mod_row"][bass.ds(b, 1)].broadcast_to([P, 4 * D])).then_inc(mr_in[p], 16)

            load(0)
            load_rows(0, 0)
            load_rows(1, 1)
            sp.wait_ge(x_used, 1)
            sp.sem_inc(x_used, -1)
            load(1)

            def step(b, p, left):
                if left >= 2:
                    sp.wait_ge(x_used, 1)
                    sp.sem_inc(x_used, -1)
                    load(b + 2)
                for f in range(NF):
                    sp.wait_ge(o_ok, f + 1)
                    sp.dma_start(out[bass.ds(b, 1), 2 * f * P:(2 * f + 2) * P].rearrange("o (t p) d -> p (o t) d", p=P),
                                 x1[:, p, 2 * f:2 * f + 2]).then_inc(o_out[p], 16)
                sp.sem_inc(o_ok, -NF)
                if left >= 2:
                    sp.wait_ge(mr_used, 1)
                    sp.sem_inc(mr_used, -1)
                    load_rows(b + 2, p)

            run_steps(sp, step)

        @blk.tensor
        def _(pe):
            def project():
                pe.wait_ge(c_in, 16)
                pe.sem_inc(c_in, -16)
                for f in range(NF):
                    if f >= 2:
                        pe.wait_ge(proj_free, f - 1)
                    for k in range(2):
                        at = (2 * f + k) * P
                        for hg in range(NG):
                            mm = pe.matmul(bank[PROJ + f % 2][:, k * D:(k + 1) * D], cin[:, hg, at:at + P],
                                           w["woT"][:, hg], start=(hg == 0), stop=(hg == NG - 1))
                    mm.then_inc(proj_full, 1)

            def turn_and_score():
                pe.wait_ge(h2_ok, 1)
                pe.sem_inc(h2_ok, -1)
                for n in range(NT_H):
                    kt, half = n % KT, n // KT
                    if n >= 2:
                        pe.wait_ge(hT_ok, n - 1)
                    for t in range(4):
                        mm = pe.transpose(bank[UP + n % 2][:, t * P:(t + 1) * P],
                                          h2[:, 4 * half + t, kt * P:(kt + 1) * P], w["ident"][:])
                    mm.then_inc(turn_full, 1)
                pe.wait_ge(proj_free, NF)
                pe.sem_inc(proj_free, -NF)
                pe.wait_ge(hT_ok, NT_H)
                pe.sem_inc(hT_ok, -NT_H)
                for c in range(NC):
                    for kt in range(KT):
                        mm = pe.matmul(bank[PROJ + c][:, :], w["wr_bc"][:, kt], hT[:, kt, c * CH:(c + 1) * CH],
                                       start=(kt == 0), stop=(kt == KT - 1))
                    mm.then_inc(sc_full, 1)

            def up():
                for u in range(NU):
                    c, ft = u // FT, u % FT
                    if u >= 2:
                        pe.wait_ge(gelu_ok, u - 1)
                    for kt in range(KT):
                        mm = pe.matmul(bank[UP + u % 2][:, :], w["w1"][:, kt, ft * P:(ft + 1) * P],
                                       hT[:, kt, c * CH:(c + 1) * CH], start=(kt == 0), stop=(kt == KT - 1))
                    mm.then_inc(up_full, 1)

            def down():
                pe.wait_ge(gelu_ok, NU)
                pe.sem_inc(gelu_ok, -NU)
                pe.wait_ge(down_free, NF)
                pe.sem_inc(down_free, -NF)
                for f in range(NF):
                    for k in range(2):
                        at = (2 * f + k) * P
                        for ft in range(FT):
                            mm = pe.matmul(bank[DOWN + f][:, k * D:(k + 1) * D], gT[:, ft, at:at + P], w["w2"][:, ft],
                                           start=(ft == 0), stop=(ft == FT - 1))
                    mm.then_inc(down_full, 1)

            project()
            turn_and_score()
            pe.sem_inc(down_free, NF)

            def step(b, p, left):
                up()
                pe.wait_ge(sbc_pe, NC)
                pe.sem_inc(sbc_pe, -NC)
                if left >= 1:
                    project()
                down()
                if left >= 1:
                    turn_and_score()

            run_steps(pe, step)

        @blk.scalar
        def _(act):
            def turned():
                for n in range(NT_H):
                    kt, half = n % KT, n // KT
                    act.wait_ge(turn_full, n + 1)
                    act.activation(hT[:, kt, half * CH:(half + 1) * CH], bank[UP + n % 2][:, :], ACT.Copy).then_inc(hT_ok, 1)
                act.sem_inc(turn_full, -NT_H)
                act.wait_ge(sbc_free, 1)
                act.sem_inc(sbc_free, -1)
                for c in range(NC):
                    act.wait_ge(sc_full, c + 1)
                    act.activation(sbc[:, c * CH:(c + 1) * CH], bank[PROJ + c][:, :], ACT.Copy).then_inc(act_step, 1)
                    act.wait_ge(act_step, c + 1)
                    act.sem_inc(sbc_ok, 1)
                    act.sem_inc(sbc_pe, 1)
                act.sem_inc(act_step, -NC)
                act.sem_inc(sc_full, -NC)

            act.sem_inc(sbc_free, 1)
            turned()

            def step(b, p, left):
                for u in range(NU):
                    c, ft = u // FT, u % FT
                    act.wait_ge(up_full, u + 1)
                    act.activation(gT[:, ft, c * CH:(c + 1) * CH], bank[UP + u % 2][:, :], ACT.Gelu_apprx_tanh,
                                   bias=w["b1c"][:, ft:ft + 1]).then_inc(gelu_ok, 1)
                    if u == 3:
                        act.wait_ge(scol_ok, 1)
                        act.sem_inc(scol_ok, -1)
                        act.activation(th[:], scol[:], ACT.Tanh, scale=0.5).then_inc(th_ok, 1)
                act.sem_inc(up_full, -NU)
                if left >= 1:
                    turned()

            run_steps(act, step)

        @blk.vector
        def _(v):
            steps = 0

            def go(ins):
                nonlocal steps
                steps += 1
                return ins.then_inc(dve_step, 1)

            def settle():
                v.wait_ge(dve_step, steps)

            def restart():
                nonlocal steps
                settle()
                v.sem_inc(dve_step, -steps)
                steps = 0

            def ranks():
                v.wait_ge(sbc_ok, NC)
                v.sem_inc(sbc_ok, -NC)
                go(v.tensor_tensor(pick[:], sbc[:].rearrange("p (t u) -> p t u", u=P),
                                   w["ident"][:].unsqueeze(1).broadcast_to([P, NB, P]), ALU.mult))
                settle()
                go(v.tensor_reduce(scol[:], pick[:], AX, ALU.add))
                settle()
                v.sem_inc(scol_ok, 1)
                for t in range(NB):
                    s, lo, hi = scol[:, t:t + 1], t * P, (t + 1) * P
                    if lo:
                        go(v.tensor_scalar(junk[:, 0:lo], sbc[:, 0:lo], s, 0.0, ALU.is_ge, ALU.add,
                                           accum_out=cnt[:, t, 0:1]))
                    if hi < S:
                        go(v.tensor_scalar(junk[:, hi:S], sbc[:, hi:S], s, 0.0, ALU.is_gt, ALU.add,
                                           accum_out=cnt[:, t, 1:2]))
                    go(v.tensor_scalar(junk[:, lo:hi], sbc[:, lo:hi], s, 0.0, ALU.is_gt, ALU.add,
                                       accum_out=cnt[:, t, 2:3]))
                    settle()
                    go(v.scalar_tensor_tensor(junk[:, lo:hi], sbc[:, lo:hi], s, w["before"][:], ALU.is_equal, ALU.mult,
                                              accum_out=cnt[:, t, 3:4]))
                    settle()
                v.sem_inc(sbc_free, 1)
                go(v.tensor_reduce(rank[:], cnt[:], AX, ALU.add))
                settle()
                go(v.tensor_scalar(rank[:], rank[:], float(TOPK), None, ALU.is_lt))
                v.wait_ge(th_ok, 1)
                v.sem_inc(th_ok, -1)
                go(v.tensor_scalar(wm[:], th[:], 0.5, 0.5, ALU.mult, ALU.add))
                settle()
                go(v.tensor_tensor(wm[:], wm[:], rank[:], ALU.mult))
                restart()

            def residual_and_norm(p):
                v.wait_ge(mr_in[p], 16)
                v.sem_inc(mr_in[p], -16)
                v.wait_ge(x_in2, 16)
                v.sem_inc(x_in2, -16)
                v.wait_ge(o_out[p], 16 * NF)
                v.sem_inc(o_out[p], -16 * NF)
                ga, sb_, cb = (mrow[:, p, n].unsqueeze(1) for n in range(3))
                for f in range(NF):
                    v.wait_ge(proj_full, f + 1)
                    go(v.tensor_tensor(t1[:].rearrange("p (t d) -> p t d", d=D),
                                       bank[PROJ + f % 2][:, :].rearrange("p (t d) -> p t d", d=D),
                                       ga.broadcast_to([P, 2, D]), ALU.mult))
                    settle()
                    v.sem_inc(proj_free, 1)
                    go(v.tensor_tensor(x1[:, p, 2 * f:2 * f + 2], t1[:].rearrange("p (t d) -> p t d", d=D),
                                       xin[:, 2 * f:2 * f + 2], ALU.add))
                    settle()
                    for t in (2 * f, 2 * f + 1):
                        go(v.bn_stats(stats[:, t], x1[:, p, t]))
                v.sem_inc(proj_full, -NF)
                v.sem_inc(x_used, 1)
                settle()
                for t in range(NB):
                    go(v.bn_aggr(mv[:, t], stats[:, t]))
                settle()
                v.tensor_scalar(veps[:], mv[:, :, 1], EPS, None, ALU.add).then_inc(var_ok, 1)
                v.wait_ge(rstd_ok, 1)
                v.sem_inc(rstd_ok, -1)
                go(v.scalar_tensor_tensor(nmr[:], mv[:, :, 0], -1.0, rstd[:], ALU.mult, ALU.mult))
                settle()
                v.wait_ge(h2_used, 1)
                v.sem_inc(h2_used, -1)
                for t in range(NB):
                    go(v.tensor_scalar(h2[:, t], x1[:, p, t], rstd[:, t:t + 1], nmr[:, t:t + 1], ALU.mult, ALU.add))
                settle()
                go(v.tensor_tensor(h2[:], h2[:], cb.broadcast_to([P, NB, D]), ALU.mult))
                settle()
                go(v.tensor_tensor(h2[:], h2[:], sb_.broadcast_to([P, NB, D]), ALU.add))
                restart()
                v.sem_inc(h2_ok, 1)
                v.sem_inc(x1_ok, 1)

            def update(p):
                v.wait_ge(y_free, 1)
                v.sem_inc(y_free, -1)
                for f in range(NF):
                    v.wait_ge(down_full, f + 1)
                    go(v.tensor_tensor(y[:, 2 * f:2 * f + 2], bank[DOWN + f][:, :].rearrange("p (t d) -> p t d", d=D),
                                       w["b2_bc"][:].unsqueeze(1).broadcast_to([P, 2, D]), ALU.add))
                    settle()
                    v.sem_inc(down_free, 1)
                    for t in (2 * f, 2 * f + 1):
                        v.scalar_tensor_tensor(y[:, t], y[:, t], wm[:, t:t + 1], mrow[:, p, 3], ALU.mult, ALU.mult
                                               ).then_inc(y_ok, 1)
                v.sem_inc(down_full, -NF)

            for p in range(2):
                v.sem_inc(o_out[p], 16 * NF)
            v.sem_inc(h2_used, 1)
            v.sem_inc(y_free, 1)
            v.memset(cnt[:], 0.0)
            residual_and_norm(0)

            def step(b, p, left):
                ranks()
                if left >= 1:
                    residual_and_norm(1 - p)
                update(p)
                restart()

            run_steps(v, step)
            for p in range(2):
                v.wait_ge(o_out[p], 16 * NF)

        @blk.gpsimd
        def _(pool):
            def root():
                pool.wait_ge(var_ok, 1)
                pool.sem_inc(var_ok, -1)
                pool.tensor_tensor(rstd[:], veps[:], w["mhalf2"][:], ALU.pow).then_inc(rstd_ok, 1)

            root()

            def step(b, p, left):
                pool.wait_ge(x1_ok, 1)
                pool.sem_inc(x1_ok, -1)
                pool.tensor_tensor(gh[:], h2[:], mrow[:, p, 3].unsqueeze(1).broadcast_to([P, NB, D]), ALU.mult
                                   ).then_inc(pool_step, 1)
                pool.wait_ge(pool_step, 1)
                pool.sem_inc(h2_used, 1)
                pool.tensor_tensor(x1[:, p], x1[:, p], gh[:], ALU.add).then_inc(pool_step, 1)
                pool.wait_ge(pool_step, 2)
                if left >= 1:
                    root()
                for f in range(NF):
                    pool.wait_ge(y_ok, 2 * (f + 1))
                    if f == NF - 1:
                        pool.sem_inc(mr_used, 1)
                    pool.tensor_tensor(x1[:, p, 2 * f:2 * f + 2], x1[:, p, 2 * f:2 * f + 2], y[:, 2 * f:2 * f + 2],
                                       ALU.add).then_inc(pool_step, 1)
                    pool.wait_ge(pool_step, 3 + f)
                    pool.sem_inc(o_ok, 1)
                pool.sem_inc(y_free, 1)
                pool.sem_inc(y_ok, -NB)
                pool.sem_inc(pool_step, -(2 + NF))

            run_steps(pool, step)


def build(nc, io, out, nbatch=B):
    dr = scratch(nc)
    with ExitStack() as ctx:
        ident = ctx.enter_context(nc.sbuf_tensor("ident", [P, P], F32))
        with ExitStack() as c1:
            def sb(name, shape, dt=F32):
                return c1.enter_context(nc.sbuf_tensor(name, shape, dt))
            w = dict(ident=ident, mhalf=sb("mhalf", [P, NB]), rk_bc=sb("rk_bc", [P, 2, DK]), rv_bc=sb("rv_bc", [P, 2, DK]),
                     rk_col=sb("rk_col", [P, 1]), wqT=sb("wqT", [P, KT, D]), wkT=sb("wkT", [P, KT, D]),
                     wvT=sb("wvT", [P, KT, D]), wcT=sb("wcT", [P, KT, H]))
            setup_project(nc, io, dr, w)
            project(nc, io, dr, w, nbatch)
        with ExitStack() as c2:
            def sb(name, shape, dt=F32):
                return c2.enter_context(nc.sbuf_tensor(name, shape, dt))
            w = dict(ident=ident, identb=sb("identb", [P, P], BF16), qpk=sb("qpk", [C_ROWS, 3, HB * S], BF16),
                     kpk=sb("kpk", [C_ROWS, 3, HB * S], BF16), rkp=sb("rkp", [ROWS, TA + TB], BF16),
                     rvt=sb("rvt", [P, XW, DK]), spread=sb("spread", [HB, P]))
            setup_attend(nc, io, dr, w)
            attend(nc, dr, w, nbatch * NG)
        with ExitStack() as c3:
            def sb(name, shape, dt=F32):
                return c3.enter_context(nc.sbuf_tensor(name, shape, dt))
            w = dict(ident=ident, mhalf2=sb("mhalf2", [P, NB]), before=sb("before", [P, P]), woT=sb("woT", [P, NG, D]),
                     w1=sb("w1", [P, KT, F]), w2=sb("w2", [P, FT, D]), b1c=sb("b1c", [P, FT]), b2_bc=sb("b2_bc", [P, D]),
                     wr=sb("wr", [P, KT]), wr_bc=sb("wr_bc", [P, KT, P]))
            setup_ffn(nc, io, w)
            ffn(nc, io, dr, out, w, nbatch)


_INS = {"x": "L0_attn_x", "Wq": "L0_attn_Wq", "Wk": "L0_attn_Wk", "Wv": "L0_attn_Wv", "Wo": "L0_attn_Wo",
        "b_o": "L0_attn_b_o", "rel_k": "L0_attn_rel_k_emb", "rel_v": "L0_attn_rel_v_emb",
        "w_router": "L0_ffn_w_router", "W1": "L0_ffn_W1", "b1": "L0_ffn_b1", "W2": "L0_ffn_W2",
        "b2": "L0_ffn_b2", "c": "L0_c", "wmod": "L0_wmod"}


def kernel(**inputs):
    import numpy as _np
    import concourse.bacc as _bacc
    from concourse.bass_utils import run_bass_kernel_spmd as _run

    nc = _bacc.Bacc("TRN2", target_bir_lowering=False, num_devices=1)
    arrays, io = {}, {}
    for short, name in _INS.items():
        a = _np.ascontiguousarray(inputs[name])
        arrays[f"in_{name}_dram"] = a
        io[short] = nc.dram_tensor(f"in_{name}_dram", a.shape, mybir.dt.from_np(a.dtype), kind="ExternalInput").ap()
    out = nc.dram_tensor("out_0_dram", (B, S, D), F32, kind="ExternalOutput").ap()
    build(nc, io, out)
    return _run(nc, [arrays], core_ids=[0]).results[0]["out_0_dram"]
```

```python
from contextlib import ExitStack

import concourse.bass as bass
from concourse import mybir

F32 = mybir.dt.float32
BF16 = mybir.dt.bfloat16
ALU = mybir.AluOpType
ACT = mybir.ActivationFunctionType
AX = mybir.AxisListType.X

P = 128
B, S, D = 16, 1024, 256
H, DK = 16, 16
R = 32
NR = 2 * R + 1
KT = D // P
NB = S // P
HB = 4
NG = H // HB
CH = 512
NC = S // CH
XW = P + 2 * R
F = 1024
FT = F // P
TOPK = S // 2
EPS = 1e-5
SCALE = 1.0 / 4.0
Q_PARTS = (0, 1, 2, 0, 1, 0)
K_PARTS = (0, 1, 0, 1, 0, 2)
ROWS = 6 * DK
M_ROWS = ROWS + 2
C_ROWS = ROWS + 5


def scratch(nc):
    def t(name, shape, dt=F32):
        return nc.dram_tensor(name, shape, dt).ap()
    return dict(
        mod_row=t("mod_row", [B, 4 * D]),
        mod_col=t("mod_col", [B, P, 2 * KT]),
        q=t("q_parts", [B * NG, 3, DK, HB * S], BF16),
        k=t("k_parts", [B * NG, 3, DK, HB * S], BF16),
        c=t("c_parts", [B * NG, 5, HB * S], BF16),
        v=t("v_by_block", [B * NG, NB, P, DK * HB]),
        ctx=t("ctx", [B * NG, P, S]),
        relv=t("relv_ext", [XW + P, DK]),
        sorted=t("h_by_rank", [TOPK, D]),
        ffn_sum=t("ffn_sum_by_rank", [TOPK, D]),
    )




def setup_project(nc, io, dr, w):
    with ExitStack() as ctx:
        def tmp(name, shape, dt=F32):
            return ctx.enter_context(nc.sbuf_tensor(name, shape, dt))

        wnat = tmp("wnat", [P, 3, KT, D])
        cT = tmp("cT", [P, KT, B])
        cth = tmp("cth", [P, KT, B])
        csl = tmp("csl", [P, KT, B])
        wmod = tmp("wmod", [P, KT, 6 * D])
        mod = tmp("mod", [B, 6 * D])
        sgn = tmp("sgn", [B, 2, D])
        modr = tmp("modr", [B, 4, D])
        modc = tmp("modc", [P, B, 2 * KT])
        dl = tmp("dl", [P, DK])
        wcm = tmp("wcm", [P, KT, D])
        zero = tmp("zero", [P, 2 * HB * S], BF16)
        pt = [ctx.enter_context(nc.psum_tensor(f"pt{i}", [P, CH], F32)) for i in range(8)]
        loaded = ctx.enter_context(nc.semaphore("loaded"))
        ident_z = ctx.enter_context(nc.semaphore("ident_z"))
        ident_ok = ctx.enter_context(nc.semaphore("ident_ok"))
        zero_ok = ctx.enter_context(nc.semaphore("zero_ok"))
        tanh_ok = ctx.enter_context(nc.semaphore("tanh_ok"))
        dve = ctx.enter_context(nc.semaphore("dve_step"))
        turned = ctx.enter_context(nc.semaphore("turned"))
        modded = ctx.enter_context(nc.semaphore("modded"))
        stored = ctx.enter_context(nc.semaphore("stored"))
        silu_ok = ctx.enter_context(nc.semaphore("silu_ok"))
        mod_ok = ctx.enter_context(nc.semaphore("mod_ok"))
        blk = ctx.enter_context(nc.Block())
        N_LOADS = 10

        @blk.sync
        def _(sp):
            for n, name in enumerate(("Wq", "Wk", "Wv")):
                sp.dma_start(wnat[:, n], io[name].rearrange("(t p) k -> p t k", p=P)).then_inc(loaded, 16)
            for kt in range(KT):
                sp.dma_start(cT[:, kt], io["c"].rearrange("b (t p) -> t p b", p=P)[kt],
                             allow_slow_non_contiguous=True).then_inc(loaded, 16)
            sp.dma_start(wmod[:], io["wmod"].rearrange("(t p) n -> p t n", p=P)).then_inc(loaded, 16)
            rk, rv = io["rel_k"], io["rel_v"]
            sp.dma_start(w["rk_bc"][:, 0], bass.AP(rk.tensor, 0, [[0, P], [1, DK]])).then_inc(loaded, 16)
            sp.dma_start(w["rk_bc"][:, 1], bass.AP(rk.tensor, 2 * R * DK, [[0, P], [1, DK]])).then_inc(loaded, 16)
            for g in range(2):
                sp.dma_start(w["rk_col"][g * 64:(g + 1) * 64], bass.AP(rk.tensor, 0, [[1, DK], [0, HB], [1, 1]]),
                             allow_slow_non_contiguous=True).then_inc(loaded, 16)
            ext = dr["relv"]
            sp.dma_start(ext[0:P - 1], bass.AP(rv.tensor, 0, [[0, P - 1], [1, DK]])).then_inc(stored, 16)
            sp.dma_start(ext[P - 1:P - 1 + NR], rv[:, :]).then_inc(stored, 16)
            rest = XW + P - (P - 1 + NR)
            sp.dma_start(ext[P - 1 + NR:], bass.AP(rv.tensor, 2 * R * DK, [[0, rest], [1, DK]])).then_inc(stored, 16)
            sp.wait_ge(zero_ok, 2)
            sp.dma_start(dr["c"][:, 0:2, :].rearrange("g r t -> g (r t)"), zero[0:B * NG, :]).then_inc(stored, 16)
            sp.wait_ge(mod_ok, 2)
            sp.dma_start(dr["mod_row"], modr[:].rearrange("b f d -> b (f d)")).then_inc(stored, 16)
            sp.dma_start(dr["mod_col"].rearrange("b p c -> p b c"), modc[:],
                         allow_slow_non_contiguous=True).then_inc(stored, 16)
            sp.wait_ge(stored, 16 * (3 + 1 + 2))

        @blk.gpsimd
        def _(pool):
            pool.memset(w["ident"][:], 0.0).then_inc(ident_z, 1)
            pool.wait_ge(ident_z, 1)
            pool.affine_select(out=w["ident"][:], in_=w["ident"][:], compare_op=ALU.not_equal, fill=1.0,
                               base=0, pattern=[[-1, P]], channel_multiplier=1).then_inc(ident_ok, 1)
            pool.memset(zero[:], 0.0).then_inc(zero_ok, 1)
            pool.memset(w["mhalf"][:], -0.5).then_inc(zero_ok, 1)

        @blk.scalar
        def _(act):
            act.wait_ge(loaded, 16 * N_LOADS)
            act.activation(cth[:], cT[:], ACT.Tanh, scale=0.5).then_inc(tanh_ok, 1)

        @blk.tensor
        def _(pe):
            pe.wait_ge(loaded, 16 * N_LOADS)
            pe.wait_ge(ident_ok, 1)
            for n in range(3):
                for kt in range(KT):
                    for nt in range(KT):
                        mm = pe.transpose(pt[n * KT + kt][:, nt * P:(nt + 1) * P],
                                          wnat[:, n, nt, kt * P:(kt + 1) * P], w["ident"][:])
            mm.then_inc(turned, 1)
            pe.wait_ge(silu_ok, 1)
            for n in range(3):
                for kt in range(KT):
                    mm = pe.matmul(pt[(6, 7, 0)[n]][0:B, :], csl[:, kt], wmod[:, kt, n * CH:(n + 1) * CH],
                                   start=(kt == 0), stop=(kt == KT - 1))
            for n in range(2 * KT):
                for kt in range(KT):
                    mm = pe.matmul(pt[1][:, n * B:(n + 1) * B], wmod[:, kt, n * P:(n + 1) * P], csl[:, kt],
                                   start=(kt == 0), stop=(kt == KT - 1))
            mm.then_inc(modded, 1)

        @blk.vector
        def _(v):
            steps = 0

            def done(ins):
                nonlocal steps
                steps += 1
                ins.then_inc(dve, 1)
                v.wait_ge(dve, steps)

            v.wait_ge(loaded, 16 * N_LOADS)
            done(v.tensor_tensor(dl[:], w["rk_bc"][:, 1], w["rk_bc"][:, 0], ALU.subtract))
            v.wait_ge(turned, 1)
            for n, name in enumerate(("wqT", "wkT")):
                for kt in range(KT):
                    src = pt[n * KT + kt][:, 0:D].rearrange("k (g h d) -> k g d h", g=NG, h=HB)
                    for g in range(NG):
                        done(v.tensor_copy(w[name][:, kt, g * 64:(g + 1) * 64].rearrange("k (d h) -> k d h", h=HB),
                                           src[:, g]))
            for kt in range(KT):
                done(v.tensor_copy(w["wvT"][:, kt], pt[2 * KT + kt][:, 0:D]))
            for kt in range(KT):
                for h in range(H):
                    c0 = h * DK
                    done(v.tensor_tensor(wcm[:, kt, c0:c0 + DK], pt[kt][:, c0:c0 + DK], dl[:], ALU.mult))
                done(v.tensor_reduce(w["wcT"][:, kt], wcm[:, kt].rearrange("k (h d) -> k h d", d=DK), AX, ALU.add))
            v.wait_ge(tanh_ok, 1)
            done(v.tensor_scalar(cth[:], cth[:], 0.5, 0.5, ALU.mult, ALU.add))
            v.tensor_tensor(csl[:], cth[:], cT[:], ALU.mult).then_inc(silu_ok, 1)
            v.wait_ge(modded, 1)
            for n in range(3):
                done(v.tensor_copy(mod[:, n * CH:(n + 1) * CH], pt[(6, 7, 0)[n]][0:B, :]))
            for n, src, dst in ((0, 2, 0), (1, 5, 3)):
                g = mod[:, src * D:(src + 1) * D]
                done(v.tensor_scalar(sgn[:, n], g, 0.0, 2.0, ALU.is_ge, ALU.mult))
                done(v.tensor_scalar(sgn[:, n], sgn[:, n], -1.0, None, ALU.add))
                done(v.tensor_scalar(modr[:, dst], g, -1.0, None, ALU.mult))
                done(v.tensor_tensor(modr[:, dst], modr[:, dst], g, ALU.max))
                done(v.tensor_scalar(modr[:, dst], modr[:, dst], 0.25, None, ALU.max))
                done(v.tensor_tensor(modr[:, dst], modr[:, dst], sgn[:, n], ALU.mult))
            done(v.tensor_copy(modr[:, 1], mod[:, 3 * D:4 * D]))
            v.tensor_scalar(modr[:, 2], mod[:, 4 * D:5 * D], 1.0, None, ALU.add).then_inc(mod_ok, 1)
            mc = pt[1][:, 0:2 * KT * B].rearrange("p (c b) -> p b c", b=B)
            done(v.tensor_copy(modc[:, :, 0:KT], mc[:, :, 0:KT]))
            v.tensor_scalar(modc[:, :, KT:2 * KT], mc[:, :, KT:2 * KT], 1.0, None, ALU.add).then_inc(mod_ok, 1)


def project(nc, io, dr, w, nbatch=B):
    with ExitStack() as ctx:
        def sb(name, shape, dt=F32):
            return ctx.enter_context(nc.sbuf_tensor(name, shape, dt))

        def sem(name):
            return ctx.enter_context(nc.semaphore(name))

        xin = sb("xin", [P, 2, NB, D])
        mcol = sb("mcol", [P, 2, 2 * KT])
        stats = sb("stats", [P, NB, 6])
        mv = sb("mv", [P, NB, 2])
        veps = sb("veps", [P, NB])
        rstd = sb("rstd", [P, NB])
        nmr = sb("nmr", [P, NB])
        nrm = sb("nrm", [P, NB, D])
        hT = sb("hT", [P, 2, KT, S])
        part1 = sb("part1", [P, 2, 5, S], BF16)
        part2 = sb("part2", [P, 2, 5, S], BF16)
        part3 = sb("part3", [P, 2, 5, S], BF16)
        RESTS = 4
        rest = sb("rest", [P, RESTS, CH])
        vout = sb("vout", [P, 2, 2, NG, DK, HB])
        NP_ = 7
        ps = [ctx.enter_context(nc.psum_tensor(f"ps{i}", [P, CH], F32)) for i in range(NP_)]
        tp = ctx.enter_context(nc.psum_tensor("tp", [P, CH], F32))

        x_in = [sem(f"x_in{i}") for i in range(2)]
        m_in = [sem(f"m_in{i}") for i in range(2)]
        x_free, m_free = sem("x_free"), sem("m_free")
        normed, nrm_free = sem("normed"), sem("nrm_free")
        tp_full, tp_free = sem("tp_full"), sem("tp_free")
        qkc_full, v_full, ps_free, ps_v_free = sem("qkc_full"), sem("v_full"), sem("ps_free"), sem("ps_v_free")
        part1_ok, rest_ok, rest_free = sem("part1_ok"), sem("rest_ok"), sem("rest_free")
        part2_ok = sem("part2_ok")
        pool_step, dve_step = sem("pool_step"), sem("dve_step2")
        parts_ok, parts_free = sem("parts_ok"), sem("parts_free")
        parts_out = [sem(f"parts_out{i}") for i in range(2)]
        v_ok = sem("v_ok")
        v_out = [sem(f"v_out{i}") for i in range(2)]
        var_ok, rstd_ok = sem("var_ok"), sem("rstd_ok")
        blk = ctx.enter_context(nc.Block())

        QK = 8
        FILLS = QK + NC + NB // 2
        bank = lambda f: ps[f % NP_]
        STORES = 3 * (QK // 2) + 3
        NORM_AT = 3
        TURN_AT = (7, 9, 11, 13)

        def load(sp, b, p):
            sp.dma_start(xin[:, p], io["x"][bass.ds(b, 1)].rearrange("o (t p) d -> p (o t) d", p=P)).then_inc(x_in[p], 16)
            sp.dma_start(mcol[:, p], dr["mod_col"][bass.ds(b, 1)].rearrange("o p c -> (o p) c")).then_inc(m_in[p], 16)

        @blk.sync
        def _(sp):
            load(sp, 0, 0)

            def step(b, p, last):
                if not last:
                    sp.wait_ge(x_free, 1)
                    sp.wait_ge(m_free, 1)
                    load(sp, b + 1, 1 - p)
                    sp.sem_inc(x_free, -1)
                    sp.sem_inc(m_free, -1)
                sp.wait_ge(parts_out[p], 16 * STORES)
                sp.sem_inc(parts_out[p], -16 * STORES)
                sp.sem_inc(parts_free, 1)
                for m in range(QK // 2):
                    sp.wait_ge(parts_ok, 2 * (m + 1))
                    dst = dr["q"] if m < KT else dr["k"]
                    for n, part in enumerate((part1, part2, part3)):
                        to = dst[bass.ds(b * NG + m % KT * 2, 2), n].rearrange("g d (h t) -> g (d h) t", h=HB)
                        sp.dma_start(to, part[:, p, m]).then_inc(parts_out[p], 16)
                sp.wait_ge(parts_ok, QK + NC)
                for n, part in enumerate((part1, part2, part3)):
                    to = dr["c"][bass.ds(b * NG, NG), 2 + n].rearrange("g (h t) -> g h t", h=HB)
                    sp.dma_start(to, part[0:H, p, 4]).then_inc(parts_out[p], 16)
                sp.sem_inc(parts_ok, -(QK + NC))
                for f in range(NB // 2):
                    sp.wait_ge(v_ok, f + 1)
                    for k in range(2):
                        to = dr["v"][bass.ds(b * NG, NG), 2 * f + k].rearrange("g p c -> p g c")
                        sp.dma_start(to, vout[:, f % 2, k].rearrange("p g d h -> p g (d h)")
                                     ).then_inc(v_out[f % 2], 16)
                sp.sem_inc(v_ok, -(NB // 2))

            for p in range(2):
                sp.sem_inc(parts_out[p], 16 * STORES)
            sp.sem_inc(x_free, 1)
            sp.sem_inc(m_free, 1)
            if nbatch > 2:
                with sp.Fori(0, nbatch - 2, 2) as b:
                    for p in range(2):
                        step(b + p, p, False)
            step(nbatch - 2, 0, False)
            step(nbatch - 1, 1, True)
            for p in range(2):
                sp.wait_ge(parts_out[p], 16 * STORES)

        @blk.vector
        def _(v):
            for r in range(2):
                v.sem_inc(v_out[r], 32)

            def norm(p, first):
                v.wait_ge(x_in[p], 16)
                v.sem_inc(x_in[p], -16)
                for t in range(NB):
                    v.bn_stats(stats[:, t], xin[:, p, t]).then_inc(dve_step, 1)
                v.wait_ge(dve_step, NB)
                for t in range(NB):
                    v.bn_aggr(mv[:, t], stats[:, t]).then_inc(dve_step, 1)
                v.wait_ge(dve_step, 2 * NB)
                v.tensor_scalar(veps[:], mv[:, :, 1], EPS, None, ALU.add).then_inc(var_ok, 1)
                v.wait_ge(rstd_ok, 1)
                v.sem_inc(rstd_ok, -1)
                v.scalar_tensor_tensor(nmr[:], mv[:, :, 0], -1.0, rstd[:], ALU.mult, ALU.mult).then_inc(dve_step, 1)
                v.wait_ge(dve_step, 2 * NB + 1)
                if not first:
                    v.wait_ge(nrm_free, 1)
                    v.sem_inc(nrm_free, -1)
                for t in range(NB):
                    v.tensor_scalar(nrm[:, t], xin[:, p, t], rstd[:, t:t + 1], nmr[:, t:t + 1],
                                    ALU.mult, ALU.add).then_inc(dve_step, 1)
                v.wait_ge(dve_step, 3 * NB + 1)
                v.sem_inc(normed, 1)
                v.sem_inc(x_free, 1)
                v.sem_inc(dve_step, -(3 * NB + 1))

            norm(0, True)

            def step(p, last):
                for f in range(QK + NC):
                    rows = P if f < QK else H
                    if f == NORM_AT and not last:
                        norm(1 - p, False)
                    v.wait_ge(part1_ok, f + 1)
                    if f >= RESTS:
                        v.wait_ge(rest_free, f - RESTS + 1)
                    col = f % NC * CH
                    first = part1[0:rows, p, f // 2, col:col + CH]
                    if QK // 2 <= f < QK:
                        v.scalar_tensor_tensor(rest[0:rows, f % RESTS], bank(f)[0:rows, :], w["rk_col"][:, 0:1], first,
                                               ALU.add, ALU.subtract).then_inc(rest_ok, 1)
                    else:
                        v.tensor_tensor(rest[0:rows, f % RESTS], bank(f)[0:rows, :], first, ALU.subtract).then_inc(rest_ok, 1)
                v.sem_inc(part1_ok, -(QK + NC))
                v.wait_ge(rest_free, QK + NC)
                v.sem_inc(rest_free, -(QK + NC))
                for f in range(NB // 2):
                    v.wait_ge(v_full, f + 1)
                    v.wait_ge(v_out[f % 2], 32)
                    v.sem_inc(v_out[f % 2], -32)
                    src = bank(QK + NC + f)[:, :].rearrange("p (g h d) -> p g h d", g=2 * NG, h=HB)
                    to = vout[:, f % 2].rearrange("p k g d h -> p (k g) h d")
                    v.tensor_copy(to, src).then_inc(dve_step, 1)
                    v.wait_ge(dve_step, f + 1)
                    v.sem_inc(ps_v_free, 1)
                    v.sem_inc(v_ok, 1)
                v.sem_inc(dve_step, -(NB // 2))
                v.sem_inc(v_full, -(NB // 2))

            if nbatch > 2:
                with v.Fori(0, nbatch - 2, 2):
                    for p in range(2):
                        step(p, False)
            step(0, False)
            step(1, True)
            for r in range(2):
                v.wait_ge(v_out[r], 32)

        @blk.gpsimd
        def _(pool):
            def root():
                pool.wait_ge(var_ok, 1)
                pool.sem_inc(var_ok, -1)
                pool.tensor_tensor(rstd[:], veps[:], w["mhalf"][:], ALU.pow).then_inc(rstd_ok, 1)

            def step(p, last):
                if not last:
                    root()
                for f in range(QK + NC):
                    rows = P if f < QK else H
                    col = f % NC * CH
                    pool.wait_ge(part2_ok, f + 1)
                    pool.tensor_tensor(part3[0:rows, p, f // 2, col:col + CH], rest[0:rows, f % RESTS],
                                       part2[0:rows, p, f // 2, col:col + CH], ALU.subtract).then_inc(pool_step, 1)
                    pool.wait_ge(pool_step, f + 1)
                    pool.sem_inc(rest_free, 1)
                    pool.sem_inc(parts_ok, 1)
                pool.sem_inc(part2_ok, -(QK + NC))
                pool.sem_inc(pool_step, -(QK + NC))

            root()
            if nbatch > 2:
                with pool.Fori(0, nbatch - 2, 2):
                    for p in range(2):
                        step(p, False)
            step(0, False)
            step(1, True)

        @blk.scalar
        def _(act):
            def turn(n, p):
                kt, half = n % KT, n // KT
                act.wait_ge(tp_full, n + 1)
                act.activation(hT[:, p, kt, half * CH:(half + 1) * CH], tp[:, :], ACT.Identity,
                               scale=mcol[:, p, KT + kt:KT + kt + 1], bias=mcol[:, p, kt:kt + 1]).then_inc(tp_free, 1)

            def first_use(p):
                act.wait_ge(m_in[p], 16)
                act.sem_inc(m_in[p], -16)

            def split(f, p):
                rows = P if f < QK else H
                col = f % NC * CH
                act.wait_ge(qkc_full, f + 1)
                out, src = part1[0:rows, p, f // 2, col:col + CH], bank(f)[0:rows, :]
                if QK // 2 <= f < QK:
                    act.activation(out, src, ACT.Identity, bias=w["rk_col"][:, 0:1]).then_inc(part1_ok, 1)
                else:
                    act.activation(out, src, ACT.Copy).then_inc(part1_ok, 1)

            def split_again(f, p):
                rows = P if f < QK else H
                col = f % NC * CH
                act.wait_ge(rest_ok, f + 1)
                act.sem_inc(ps_free, 1)
                act.activation(part2[0:rows, p, f // 2, col:col + CH], rest[0:rows, f % RESTS], ACT.Copy
                               ).then_inc(part2_ok, 1)

            def step(p, last):
                act.wait_ge(parts_free, 1)
                act.sem_inc(parts_free, -1)
                for f in range(QK + NC):
                    split(f, p)
                    if f:
                        split_again(f - 1, p)
                    if f in TURN_AT and not last:
                        if f == TURN_AT[0]:
                            first_use(1 - p)
                        turn(TURN_AT.index(f), 1 - p)
                split_again(QK + NC - 1, p)
                if not last:
                    for n, f in enumerate(TURN_AT):
                        if f >= QK + NC:
                            turn(n, 1 - p)
                    act.sem_inc(tp_full, -2 * KT)
                act.sem_inc(rest_ok, -(QK + NC))
                act.sem_inc(qkc_full, -(QK + NC))

            first_use(0)
            for n in range(2 * KT):
                turn(n, 0)
            act.sem_inc(tp_full, -2 * KT)
            if nbatch > 2:
                with act.Fori(0, nbatch - 2, 2):
                    for p in range(2):
                        step(p, False)
            step(0, False)
            step(1, True)

        @blk.tensor
        def _(pe):
            def turn(n):
                kt, half = n % KT, n // KT
                if n:
                    pe.wait_ge(tp_free, n)
                for t in range(4):
                    mm = pe.transpose(tp[:, t * P:(t + 1) * P], nrm[:, 4 * half + t, kt * P:(kt + 1) * P], w["ident"][:])
                mm.then_inc(tp_full, 1)

            def fill(f, p):
                if f < QK:
                    m, c = f % (QK // 2) // 2, f % 2
                    wt = w["wqT"] if f < QK // 2 else w["wkT"]
                    for kt in range(KT):
                        mm = pe.matmul(bank(f)[:, :], wt[:, kt, m * P:(m + 1) * P], hT[:, p, kt, c * CH:(c + 1) * CH],
                                       start=(kt == 0), stop=(kt == KT - 1))
                    return mm.then_inc(qkc_full, 1)
                if f < QK + NC:
                    c = f - QK
                    for kt in range(KT):
                        mm = pe.matmul(bank(f)[0:H, :], w["wcT"][:, kt, :], hT[:, p, kt, c * CH:(c + 1) * CH],
                                       start=(kt == 0), stop=(kt == KT - 1))
                    return mm.then_inc(qkc_full, 1)
                for k in range(2):
                    t = 2 * (f - QK - NC) + k
                    for kt in range(KT):
                        mm = pe.matmul(bank(f)[:, k * D:(k + 1) * D], hT[:, p, kt, t * P:(t + 1) * P], w["wvT"][:, kt, :],
                                       start=(kt == 0), stop=(kt == KT - 1))
                return mm.then_inc(v_full, 1)

            for n in range(2 * KT):
                if n == 0:
                    pe.wait_ge(normed, 1)
                turn(n)
            pe.wait_ge(tp_free, 2 * KT)
            pe.sem_inc(tp_free, -2 * KT)
            pe.sem_inc(normed, -1)
            pe.sem_inc(nrm_free, 1)
            pe.sem_inc(m_free, 1)

            def bank_free(f):
                if f == 0:
                    pe.wait_ge(ps_free, QK + NC)
                    pe.sem_inc(ps_free, -(QK + NC))
                elif QK + NC - NP_ <= f < NP_:
                    pe.wait_ge(ps_v_free, f + NP_ - QK - NC + 1)
                    if f == NP_ - 1:
                        pe.sem_inc(ps_v_free, -(NB // 2))
                elif f >= NP_:
                    pe.wait_ge(ps_free, f - NP_ + 1)

            def step(p, last):
                for f in range(FILLS):
                    bank_free(f)
                    fill(f, p)
                    if f in TURN_AT and not last:
                        if f == TURN_AT[0]:
                            pe.wait_ge(normed, 1)
                        turn(TURN_AT.index(f))
                if not last:
                    pe.wait_ge(tp_free, 2 * KT)
                    pe.sem_inc(tp_free, -2 * KT)
                    pe.sem_inc(normed, -1)
                    pe.sem_inc(nrm_free, 1)
                    pe.sem_inc(m_free, 1)

            pe.sem_inc(ps_free, QK + NC)
            pe.sem_inc(ps_v_free, NB // 2)
            if nbatch > 2:
                with pe.Fori(0, nbatch - 2, 2):
                    for p in range(2):
                        step(p, False)
            step(0, False)
            step(1, True)



XA = XW - R
TA = XA + P - 1
TB = R + P - 1


def window(jb, c):
    lo, hi = max(jb * P - R, c * CH), min(jb * P + P + R, (c + 1) * CH)
    return (lo, hi) if lo < hi else None


def pieces(jb, c):
    lo, hi, at = c * CH, (c + 1) * CH, jb * P
    found = []
    if lo < at:
        found.append((1, lo, min(hi, at)))
    if hi > at:
        found.append((0, max(lo, at), hi))
    return found


NEAR = [(jb, c) for jb in range(NB) for c in range(NC) if window(jb, c)]
FAR = [(jb, c) for jb in range(NB) for c in range(NC) if not window(jb, c)]
QUADS = []
for n, near in enumerate(NEAR):
    QUADS.append(near)
    if n % 3 == 0 and len(FAR) > 2:
        QUADS.append(FAR.pop(0))
QUADS += FAR
NQ = len(QUADS)
WIN = [window(jb, c) is not None for jb, c in QUADS]
FIRST = [q == min(k for k in range(NQ) if QUADS[k][1] == QUADS[q][1]) for q in range(NQ)]
NWIN = sum(WIN)
NT = NQ * HB
RING = 3
XF = CH // (HB * NB)
DF = XW // XF
JOIN_AT, INVERT_AT, SPREAD_AT = 3, 8, (13, 16)
TABLE_AT = {19 + f * 43 // DF: f for f in range(DF)}
FIRST_TABLE_AT = {1 + f * (NT - 2) // DF: f for f in range(DF)}


def setup_attend(nc, io, dr, w):
    with ExitStack() as ctx:
        def tmp(name, shape, dt=F32):
            return ctx.enter_context(nc.sbuf_tensor(name, shape, dt))
        rkT = tmp("rkT", [DK, NR])
        tab = tmp("tab", [DK, TA + TB])
        tp1, tp2, tp3 = (tmp(f"tabp{i}", [DK, TA + TB], BF16) for i in range(3))
        rvb = w["rvb"]
        loaded, dve = ctx.enter_context(nc.semaphore("tab_in")), ctx.enter_context(nc.semaphore("tab_step"))
        split, packed = ctx.enter_context(nc.semaphore("tab_split")), ctx.enter_context(nc.semaphore("tab_packed"))
        pool_step = ctx.enter_context(nc.semaphore("const_step"))
        blk = ctx.enter_context(nc.Block())

        @blk.sync
        def _(sp):
            sp.dma_start(rkT[:], io["rel_k"].rearrange("r d -> d r"), allow_slow_non_contiguous=True).then_inc(loaded, 16)
            rv, ext = io["rel_v"], dr["relv"]
            sp.dma_start(rvb[:], bass.AP(rv.tensor, 0, [[0, P], [2 * R * DK, 2], [1, DK]])).then_inc(loaded, 16)
            sp.dma_start(w["rvt"][:].rearrange("p x d -> p (x d)"),
                         bass.AP(ext.tensor, 0, [[DK, P], [1, XW * DK]])).then_inc(loaded, 16)
            sp.wait_ge(split, 1)
            for n, part in enumerate(K_PARTS):
                sp.dma_start(w["rkp"][n * DK:(n + 1) * DK], (tp1, tp2, tp3)[part][:]).then_inc(packed, 16)
            sp.wait_ge(packed, 16 * len(K_PARTS))

        @blk.gpsimd
        def _(pool):
            for b in range(3):
                pool.memset(w["kpk"][ROWS:C_ROWS, b], 1.0).then_inc(pool_step, 1)
            pool.memset(w["spread"][:], 1.0).then_inc(pool_step, 1)
            pool.wait_ge(pool_step, 4)
            pool.affine_select(out=w["spread"][:], in_=w["spread"][:], compare_op=ALU.is_ge, fill=0.0,
                               base=0, pattern=[[1, P]], channel_multiplier=-32).then_inc(pool_step, 1)
            pool.wait_ge(pool_step, 5)
            pool.affine_select(out=w["spread"][:], in_=w["spread"][:], compare_op=ALU.is_ge, fill=0.0,
                               base=31, pattern=[[-1, P]], channel_multiplier=32).then_inc(pool_step, 1)

        @blk.vector
        def _(v):
            steps = 0

            def done(ins):
                nonlocal steps
                steps += 1
                ins.then_inc(dve, 1)
                v.wait_ge(dve, steps)

            v.wait_ge(loaded, 48)
            done(v.memset(tab[:], 0.0))
            far = rkT[:, NR - 1:NR]
            done(v.tensor_scalar(tab[:, P - 1:P - 1 + NR], rkT[:], rkT[:, 0:1], None, ALU.subtract))
            done(v.tensor_scalar(tab[:, P - 1 + NR:TA], rkT[:, NR - 1:NR].broadcast_to([DK, TA - P + 1 - NR]),
                                 rkT[:, 0:1], None, ALU.subtract))
            done(v.tensor_scalar(tab[:, TA:TA + R], rkT[:, R + 1:NR], far, None, ALU.subtract))
            done(v.tensor_copy(tp1[:], tab[:]))
            done(v.tensor_tensor(tab[:], tab[:], tp1[:], ALU.subtract))
            done(v.tensor_copy(tp2[:], tab[:]))
            v.tensor_tensor(tp3[:], tab[:], tp2[:], ALU.subtract).then_inc(split, 1)
            for r, (lo, hi) in enumerate(((0, XA), (XA, XW))):
                done(v.tensor_tensor(w["rvt"][:, lo:hi], w["rvt"][:, lo:hi],
                                     rvb[:, r].unsqueeze(1).broadcast_to([P, hi - lo, DK]), ALU.subtract))
            done(v.tensor_copy(w["identb"][:], w["ident"][:]))


def attend(nc, dr, w, ngroups=B * NG):
    with ExitStack() as ctx:
        def sb(name, shape, dt=F32):
            return ctx.enter_context(nc.sbuf_tensor(name, shape, dt))

        def sem(name):
            return ctx.enter_context(nc.semaphore(name))

        qpk, kpk = w["qpk"], w["kpk"]
        vs = sb("vs", [P, 2, NB, DK + 1, 2 * HB])
        vraw = sb("vraw", [P, NB, DK * HB])
        dt = sb("dt", [P, 3, HB, NB, XW])
        dh = sb("dh", [P, 2, HB, NB, XW], BF16)
        prob = sb("prob", [P, RING * HB, CH])
        tmax = sb("tmax", [P, HB * NB, NC])
        rmax = sb("rmax", [P, HB * NB])
        m1 = sb("m1", [HB * NB, P], BF16)
        m2 = sb("m2", [HB * NB, P], BF16)
        ctxs = sb("ctxs", [P, S])
        relvs = sb("relvs", [P, R, HB, NB])
        rs = sb("rs", [P, HB * S // P])
        rr = sb("rr", [P, HB * S // P])
        rrow = sb("rrow", [HB, S])
        pp = ctx.enter_context(nc.psum_tensor("pp", [P, 8 * CH], F32))
        bank = lambda n: pp[:, n * CH:(n + 1) * CH]
        ctxT = pp[:, 0:2 * CH]
        S_BANKS, ST_BANKS, RELV_BANK, SPARE = (2, 3), (6, 4, 5), 4, 7

        qk_in = [sem(f"qk_in{i}") for i in range(3)]
        v_in, vraw_free = sem("v_in"), sem("vraw_free")
        v_ok = [sem(f"v_both{i}") for i in range(2)]
        s_full, s_free = sem("s_full"), sem("s_free")
        st_win, st_plain, added = sem("st_win"), sem("st_plain"), sem("added")
        exp_ok = sem("exp_ok")
        pv_begun, pv_ok, win_ok = sem("pv_begun"), sem("pv_ok"), sem("win_ok")
        pwin_ok = sem("pwin_ok")
        ctx_full, ctx_pe, ctx_sp = sem("ctx_full"), sem("ctx_pe"), sem("ctx_sp")
        ctxs_free, ctx_out = sem("ctxs_free"), sem("ctx_out")
        rmax_ok, mT_full, m_ok, m_in = sem("rmax_ok"), sem("mT_full"), sem("m_ok"), sem("m_in")
        relv_full, relv_free, relvs_ok = sem("relv_full"), sem("relv_free"), sem("relvs_ok")
        rs_in, rr_ok, rrow_in = sem("rs_in"), sem("rr_ok"), sem("rrow_in")
        bc_full, bc_free, ctxn_ok = sem("bc_full"), sem("bc_free"), sem("ctxn_ok")
        d_full, dh_ok, pool_base = sem("d_full"), sem("dh_ok"), sem("pool_base")
        bufs_free, ones_ok = sem("bufs_free"), sem("ones_ok3")
        dve_step, pool_step, act_step = sem("dve_step3"), sem("pool_step3"), sem("act_step3")
        blk = ctx.enter_context(nc.Block())
        N_QK = 7

        def load_qk(sp, g, b3):
            def rows(src, to, lo, parts):
                n = len(parts)
                step = parts[1] - parts[0] if n > 1 else 1
                take = src[bass.ds(g, 1), parts[0]:parts[-1] + 1:step].rearrange("o n d t -> (o n) d t")
                sp.dma_start(to[lo:lo + n * DK, b3], take).then_inc(qk_in[b3], 16)
            rows(dr["q"], qpk, 0, Q_PARTS[0:3])
            rows(dr["q"], qpk, 3 * DK, Q_PARTS[3:5])
            rows(dr["q"], qpk, 5 * DK, Q_PARTS[5:6])
            for n in range(3):
                rows(dr["k"], kpk, 2 * n * DK, K_PARTS[2 * n:2 * n + 2])
            sp.dma_start(qpk[ROWS:C_ROWS, b3], dr["c"][bass.ds(g, 1)].rearrange("o r t -> (o r) t")).then_inc(qk_in[b3], 16)

        def load_v(sp, g):
            sp.wait_ge(vraw_free, 1)
            sp.sem_inc(vraw_free, -1)
            sp.dma_start(vraw[:], dr["v"][bass.ds(g, 1)].rearrange("o j p c -> p (o j) c")).then_inc(v_in, 16)

        def send_m(sp, b3):
            sp.wait_ge(m_ok, 1)
            sp.sem_inc(m_ok, -1)
            for n, m in enumerate((m1, m2)):
                sp.dma_start(qpk[ROWS + n:ROWS + n + 1, b3], m[:]).then_inc(m_in, 16)

        def run_steps(eng, step):
            step(0, 0, True, 3)
            n = (ngroups - 4) // 6 * 6
            if n:
                with eng.Fori(0, n // 6) as turn:
                    for k in range(1, 7):
                        step(turn * 6 + k, k % 6, False, 3)
            for g in range(n + 1, ngroups):
                step(g, g % 6, False, min(3, ngroups - 1 - g))

        @blk.sync
        def _(sp):
            for g in range(3):
                load_qk(sp, g, g)
            sp.sem_inc(vraw_free, 1)
            for g in range(2):
                load_v(sp, g)
            send_m(sp, 0)

            def finish(g):
                sp.wait_ge(ctx_sp, 1)
                sp.sem_inc(ctx_sp, -1)
                sp.dma_start(rs[:], ctxs[DK:P:32, :]).then_inc(rs_in, 16)
                sp.wait_ge(rr_ok, 1)
                sp.sem_inc(rr_ok, -1)
                sp.dma_start(rrow[:], rr[:]).then_inc(rrow_in, 16)
                sp.wait_ge(ctxn_ok, NC)
                sp.sem_inc(ctxn_ok, -NC)
                sp.dma_start(dr["ctx"][bass.ds(g, 1)].rearrange("o p t -> (o p) t"), ctxs[:]).then_inc(ctx_out, 16)
                sp.wait_ge(ctx_out, 16)
                sp.sem_inc(ctx_out, -16)

            def step(g, i, first, left):
                if not first:
                    finish(g - 1)
                sp.sem_inc(ctxs_free, 1)
                if left >= 1:
                    send_m(sp, (i + 1) % 3)
                if left >= 2:
                    sp.wait_ge(bufs_free, 1)
                    sp.sem_inc(bufs_free, -1)
                    if left >= 3:
                        load_qk(sp, g + 3, i % 3)
                    load_v(sp, g + 2)

            run_steps(sp, step)
            finish(ngroups - 1)


        @blk.tensor
        def _(pe):
            def table(f, b3):
                q = qpk[0:ROWS, b3].rearrange("r (h j a) -> r a h j", h=HB, a=P)
                if f == 0:
                    pe.wait_ge(qk_in[b3], 16 * N_QK)
                    pe.sem_inc(qk_in[b3], -16 * N_QK)
                else:
                    pe.wait_ge(dh_ok, f)
                out = bank(SPARE).rearrange("p (x h j) -> p x h j", h=HB, j=NB)
                for k in range(XF):
                    x = f * XF + k
                    if x < R:
                        at, a, j0, j1, i0 = TA + R - 1 - x, P - R + x, 1, NB, 0
                    elif x < R + P:
                        at, a, j0, j1, i0 = XW - 1 - x, x - R, 0, NB, 0
                    else:
                        at, a, j0, j1, i0 = XW - 1 - x, x - R - P, 0, NB - 1, 1
                    mm = pe.matmul(out[:, k, :, j0:j1], w["rkp"][0:ROWS, at:at + P], q[:, a, :, i0:i0 + j1 - j0],
                                   start=True, stop=True)
                mm.then_inc(d_full, 1)

            def score_rows(t, b3, b2):
                h, ib, c = t // (NB * NC), t // NC % NB, t % NC
                out = bank(S_BANKS[t % 2])
                at = h * S + ib * P
                mms = []
                for j in range(2):
                    lo, hi = (c * CH, min((c + 1) * CH, (ib + 1) * P)) if j == 0 else (max(c * CH, (ib + 1) * P), (c + 1) * CH)
                    rows = (ROWS, C_ROWS)[j]
                    if lo < hi:
                        mms.append((out[:, lo - c * CH:hi - c * CH], qpk[0:rows, b3, at:at + P],
                                    kpk[0:rows, b3, h * S + lo:h * S + hi]))
                if ib // 4 == c:
                    o = ib % 4 * P
                    mms.append((out[:, o:o + P], dh[:, b2, h, ib, R:R + P], w["identb"][:]))
                if ib and (ib - 1) // 4 == c:
                    o = (ib - 1) % 4 * P + P - R
                    mms.append((out[0:R, o:o + R], dh[:, b2, h, ib - 1, R + P:XW], w["identb"][:, P - R:P]))
                if ib < NB - 1 and (ib + 1) // 4 == c:
                    o = (ib + 1) % 4 * P
                    mms.append((out[P - R:P, o:o + R], dh[:, b2, h, ib + 1, 0:R], w["identb"][:, 0:R]))
                for n, (o, l, r) in enumerate(mms):
                    mm = pe.matmul(o, l, r, start=(n == 0), stop=(n == len(mms) - 1), skip_group_check=True)
                mm.then_inc(s_full, 1)

            def score_cols(t, b3):
                (jb, c), h = QUADS[t // HB], t % HB
                out = bank(ST_BANKS[t % 3])
                at = h * S + jb * P
                for n, (far, lo, hi) in enumerate(pieces(jb, c)):
                    rows = C_ROWS if far else M_ROWS
                    mm = pe.matmul(out[:, lo - c * CH:hi - c * CH], kpk[0:rows, b3, at:at + P],
                                   qpk[0:rows, b3, h * S + lo:h * S + hi], start=(n == 0), stop=True,
                                   skip_group_check=True)
                mm.then_inc(st_win if WIN[t // HB] else st_plain, 1)

            def values(q, half, b2):
                jb, c = QUADS[q]
                begin, end = c * CH + half * CH // 2, c * CH + (half + 1) * CH // 2
                for far, lo, hi in pieces(jb, c):
                    lo, hi = max(lo, begin), min(hi, end)
                    for h in range(HB if lo < hi else 0):
                        mm = pe.matmul(ctxT[32 * h:32 * h + DK + 1, lo:hi], vs[:, b2, jb, :, far * HB + h],
                                       prob[:, q % RING * HB + h, lo - c * CH:hi - c * CH],
                                       start=(FIRST[q] and half == 0), stop=False, skip_group_check=True)
                if half == 1:
                    mm.then_inc(pv_ok, 1)
                elif WIN[q]:
                    mm.then_inc(pv_begun, 1)

            def relative_values(lo, hi, b3):
                win = dt[:, b3]
                half = R // 2
                for a in range(lo, hi):
                    out = bank(RELV_BANK + a // half).rearrange("p (a h i) -> p a h i", h=HB, i=NB)[:, a % half]
                    for q in range(4):
                        x = R * q + a + R
                        pe.matmul(out[32 * q:32 * q + DK], w["rvt"][:, XW - 1 - x], win[:, :, :, x],
                                  start=True, stop=(0 < q < 3), skip_group_check=True)
                    x = R + P + a
                    pe.matmul(out[0:DK, :, 1:NB], w["rvt"][:, XW - 1 - x], win[:, :, 0:NB - 1, x],
                              start=False, stop=True, skip_group_check=True)
                    mm = pe.matmul(out[96:96 + DK, :, 0:NB - 1], w["rvt"][:, XW - 1 - a], win[:, :, 1:NB, a],
                                   start=False, stop=True, skip_group_check=True)
                    if a % half == half - 1:
                        mm.then_inc(relv_full, 1)

            def turn_max():
                pe.wait_ge(rmax_ok, 1)
                pe.sem_inc(rmax_ok, -1)
                pe.transpose(bank(SPARE)[0:HB * NB, 0:P], rmax[:], w["ident"][:]).then_inc(mT_full, 1)

            def join():
                pe.wait_ge(relvs_ok, 1)
                pe.sem_inc(relvs_ok, -1)
                for q in range(4):
                    for c in range(NC):
                        for h in range(HB):
                            to = ctxT[32 * h:32 * h + DK, c * CH:(c + 1) * CH].rearrange("p (i a) -> p i a", a=P)
                            mm = pe.matmul(to[:, :, R * q:R * q + R], w["ident"][:, 32 * q:32 * q + DK],
                                           relvs[:, :, h, c * NB // 2:(c + 1) * NB // 2].rearrange("p a i -> p i a"),
                                           start=False, stop=True, skip_group_check=True)
                mm.then_inc(ctx_full, 1)

            def spread(c):
                if c == 0:
                    pe.wait_ge(rrow_in, 16)
                    pe.sem_inc(rrow_in, -16)
                else:
                    pe.wait_ge(bc_free, c)
                pe.matmul(bank(SPARE), w["spread"][:], rrow[:, c * CH:(c + 1) * CH],
                          start=True, stop=True).then_inc(bc_full, 1)

            def spread_taken():
                pe.wait_ge(bc_free, NC)
                pe.sem_inc(bc_free, -NC)

            for f in range(DF):
                table(f, 0)
            pe.wait_ge(dh_ok, DF)
            pe.sem_inc(dh_ok, -DF)
            for t in range(NT):
                if t >= 2:
                    pe.wait_ge(s_free, t - 1)
                score_rows(t, 0, 0)
                if t in FIRST_TABLE_AT:
                    table(FIRST_TABLE_AT[t], 1)
            pe.wait_ge(dh_ok, DF)
            pe.wait_ge(s_free, NT)
            pe.sem_inc(s_free, -NT)
            turn_max()
            pe.wait_ge(ones_ok, 2)
            pe.sem_inc(relv_free, 2)
            pe.sem_inc(ctx_pe, 1)

            def step(g, i, first, left):
                b3, n3, b2 = i % 3, (i + 1) % 3, i % 2
                pe.wait_ge(m_in, 32)
                pe.sem_inc(m_in, -32)
                for t in range(NT):
                    if t >= 3:
                        pe.wait_ge(exp_ok, t - 2)
                    elif t >= 1:
                        pe.wait_ge(relv_free, t)
                    score_cols(t, b3)
                    if left >= 1:
                        if t == 0:
                            pe.wait_ge(dh_ok, DF)
                            pe.sem_inc(dh_ok, -DF)
                        if t >= 2:
                            pe.wait_ge(s_free, t - 1)
                        score_rows(t, n3, 1 - b2)
                    if t % HB == 2 and t > HB:
                        if t // HB == 1:
                            pe.sem_inc(relv_free, -2)
                            pe.wait_ge(v_ok[b2], 1)
                            pe.sem_inc(v_ok[b2], -1)
                            pe.wait_ge(ctx_pe, 1)
                            pe.sem_inc(ctx_pe, -1)
                        values(t // HB - 1, 0, b2)
                    if t % HB == 0 and t > HB:
                        values(t // HB - 2, 1, b2)
                    if t == JOIN_AT and not first:
                        join()
                    if t in SPREAD_AT and not first:
                        spread(SPREAD_AT.index(t))
                    if t in TABLE_AT and left >= 2:
                        if TABLE_AT[t] == 0 and not first:
                            spread_taken()
                        table(TABLE_AT[t], (i + 2) % 3)
                pe.wait_ge(exp_ok, NT)
                pe.sem_inc(exp_ok, -NT)
                values(NQ - 2, 1, b2)
                values(NQ - 1, 0, b2)
                values(NQ - 1, 1, b2)
                pe.wait_ge(pwin_ok, 1)
                pe.sem_inc(pwin_ok, -1)
                relative_values(0, R // 4, b3)
                if left >= 2:
                    pe.wait_ge(dh_ok, DF)
                else:
                    spread_taken()
                if left >= 1:
                    pe.wait_ge(s_free, NT)
                    pe.sem_inc(s_free, -NT)
                    turn_max()
                relative_values(R // 4, R, b3)

            run_steps(pe, step)
            join()
            for c in range(NC):
                spread(c)


        @blk.scalar
        def _(act):
            def table_out(f, b3, b2):
                act.wait_ge(d_full, f + 1)
                x0 = f * XF
                j0 = 1 if x0 < R else 0
                j1 = NB - 1 if x0 >= R + P else NB
                src = bank(SPARE).rearrange("p (x h j) -> p h j x", h=HB, j=NB)
                act.activation(dt[:, b3, :, j0:j1, x0:x0 + XF], src[:, :, j0:j1, :], ACT.Copy)
                act.activation(dh[:, b2, :, j0:j1, x0:x0 + XF], src[:, :, j0:j1, :], ACT.Copy).then_inc(dh_ok, 1)
                if f == DF - 1:
                    act.sem_inc(d_full, -DF)

            def ring_free(q):
                act.wait_ge(pv_ok, q + 1)
                if WIN[q]:
                    act.wait_ge(win_ok, sum(WIN[:q + 1]))

            for b3 in range(2):
                for f in range(DF):
                    table_out(f, b3, b3)

            def context_out():
                act.wait_ge(ctx_full, 1)
                act.sem_inc(ctx_full, -1)
                act.wait_ge(ctxs_free, 1)
                act.sem_inc(ctxs_free, -1)
                act.activation(ctxs[:], ctxT, ACT.Copy).then_inc(act_step, 1)
                act.wait_ge(act_step, 1)
                act.sem_inc(act_step, -1)
                act.sem_inc(ctx_pe, 1)
                act.sem_inc(ctx_sp, 1)

            def step(g, i, first, left):
                n_win = n_plain = 0
                for t in range(NT):
                    q = t // HB
                    if t % HB == 0 and q >= RING:
                        ring_free(q - RING)
                    if WIN[q]:
                        n_win += 1
                        act.wait_ge(added, n_win)
                    else:
                        n_plain += 1
                        act.wait_ge(st_plain, n_plain)
                    act.activation(prob[:, q % RING * HB + t % HB], bank(ST_BANKS[t % 3]), ACT.Exp,
                                   scale=SCALE).then_inc(exp_ok, 1)
                    if t in TABLE_AT and left >= 2:
                        table_out(TABLE_AT[t], (i + 2) % 3, i % 2)
                    if t == JOIN_AT and not first:
                        context_out()
                act.sem_inc(added, -n_win)
                act.sem_inc(st_plain, -n_plain)
                act.wait_ge(win_ok, NWIN)
                act.wait_ge(pv_ok, NQ)
                act.sem_inc(win_ok, -NWIN)
                act.sem_inc(pv_ok, -NQ)
                if left >= 2:
                    act.sem_inc(bufs_free, 1)
                half = R // 2
                for k in range(2):
                    act.wait_ge(relv_full, k + 1)
                    act.activation(relvs[:, k * half:(k + 1) * half].rearrange("p a h i -> p (a h i)"),
                                   bank(RELV_BANK + k), ACT.Copy).then_inc(act_step, 1)
                    act.wait_ge(act_step, k + 1)
                    act.sem_inc(relv_free, 1)
                act.sem_inc(relvs_ok, 1)
                act.sem_inc(relv_full, -2)
                act.sem_inc(act_step, -2)

            run_steps(act, step)
            context_out()


        @blk.vector
        def _(v):
            def tile_max(t):
                v.wait_ge(s_full, t + 1)
                v.tensor_reduce(tmax[:, t // NC, t % NC:t % NC + 1], bank(S_BANKS[t % 2]), AX, ALU.max).then_inc(s_free, 1)

            def row_max():
                v.sem_inc(s_full, -NT)
                v.drain()
                v.tensor_reduce(rmax[:], tmax[:], AX, ALU.max).then_inc(rmax_ok, 1)
                v.wait_ge(mT_full, 1)
                v.sem_inc(mT_full, -1)
                src = bank(SPARE)[0:HB * NB, 0:P]
                v.tensor_scalar(m1[:], src, -1.0, None, ALU.mult).then_inc(dve_step, 1)
                v.wait_ge(dve_step, 1)
                v.sem_inc(dve_step, -1)
                v.scalar_tensor_tensor(m2[:], src, -1.0, m1[:], ALU.mult, ALU.subtract).then_inc(m_ok, 1)

            def invert():
                v.wait_ge(rs_in, 16)
                v.sem_inc(rs_in, -16)
                v.reciprocal(rr[:], rs[:]).then_inc(rr_ok, 1)

            def normalise(c):
                v.wait_ge(bc_full, 1)
                v.sem_inc(bc_full, -1)
                v.tensor_tensor(ctxs[:, c * CH:(c + 1) * CH], bank(SPARE), ctxs[:, c * CH:(c + 1) * CH],
                                ALU.mult).then_inc(dve_step, 1)
                v.wait_ge(dve_step, 1)
                v.sem_inc(dve_step, -1)
                v.sem_inc(bc_free, 1)
                v.sem_inc(ctxn_ok, 1)

            v.memset(vs[:, :, :, DK], 1.0).then_inc(ones_ok, 1)
            v.memset(ctxT, 0.0).then_inc(ones_ok, 1)
            for t in range(NT):
                tile_max(t)
            row_max()

            def step(g, i, first, left):
                n_win = 0
                for t in range(NT):
                    (jb, c), h = QUADS[t // HB], t % HB
                    if WIN[t // HB]:
                        n_win += 1
                        v.wait_ge(st_win, n_win)
                        lo, hi = window(jb, c)
                        x0 = lo - jb * P + R
                        cols = bank(ST_BANKS[t % 3])[:, lo - c * CH:hi - c * CH]
                        v.tensor_tensor(cols, cols, dt[:, i % 3, h, jb, x0:x0 + hi - lo], ALU.add).then_inc(added, 1)
                    if left >= 1:
                        tile_max(t)
                    if t == INVERT_AT and not first:
                        invert()
                    if t - 1 in SPREAD_AT and not first:
                        normalise(SPREAD_AT.index(t - 1))
                v.sem_inc(st_win, -n_win)
                if left >= 1:
                    row_max()

            run_steps(v, step)
            invert()
            for c in range(NC):
                normalise(c)


        @blk.gpsimd
        def _(pool):
            def both_values(b2):
                pool.wait_ge(v_in, 16)
                pool.sem_inc(v_in, -16)
                for r in range(2):
                    add = w["rvb"][:, r].unsqueeze(1).unsqueeze(3).broadcast_to([P, NB, DK, HB])
                    pool.tensor_tensor(vs[:, b2, :, 0:DK, r * HB:(r + 1) * HB],
                                       vraw[:].rearrange("p j (d h) -> p j d h", h=HB), add, ALU.add
                                       ).then_inc(pool_base, 1)
                    pool.wait_ge(pool_base, r + 1)
                pool.sem_inc(pool_base, -2)
                pool.sem_inc(vraw_free, 1)
                pool.sem_inc(v_ok[b2], 1)

            for b2 in range(2):
                both_values(b2)

            def copy_window(q, b3):
                jb, c = QUADS[q]
                n = sum(WIN[:q + 1])
                pool.wait_ge(pv_begun, n)
                lo, hi = window(jb, c)
                x0, s0 = lo - jb * P + R, q % RING * HB
                pool.tensor_copy(dt[:, b3, :, jb, x0:x0 + hi - lo],
                                 prob[:, s0:s0 + HB, lo - c * CH:hi - c * CH]).then_inc(pool_step, 1)
                pool.wait_ge(pool_step, n)
                pool.sem_inc(win_ok, 1)
                if n == NWIN:
                    pool.sem_inc(pwin_ok, 1)
                    pool.sem_inc(pv_begun, -NWIN)
                    pool.sem_inc(pool_step, -NWIN)

            def step(g, i, first, left):
                for q in range(NQ):
                    if q == RING and not first and left >= 1:
                        both_values((i + 1) % 2)
                    if WIN[q]:
                        copy_window(q, i % 3)

            run_steps(pool, step)




def setup_ffn(nc, io, w):
    with ExitStack() as ctx:
        wop = ctx.enter_context(nc.sbuf_tensor("wop", [P, KT, H, 32], F32))
        pt = [ctx.enter_context(nc.psum_tensor(f"wo_t{i}", [P, CH], F32)) for i in range(2)]
        loaded, const_step = ctx.enter_context(nc.semaphore("ffn_in")), ctx.enter_context(nc.semaphore("ffn_const"))
        wo_zero, turned = ctx.enter_context(nc.semaphore("wo_zero")), ctx.enter_context(nc.semaphore("wo_turned"))
        blk = ctx.enter_context(nc.Block())
        N_WO = 2 * KT

        @blk.sync
        def _(sp):
            sp.wait_ge(wo_zero, 1)
            for t in range(KT):
                sp.dma_start(wop[:, t, :, 0:DK], io["Wo"][t * P:(t + 1) * P, :].rearrange("p (h d) -> p h d", d=DK)
                             ).then_inc(loaded, 16)
                sp.dma_start(wop[:, t, 0, DK:DK + 1], io["b_o"][t * P:(t + 1) * P].rearrange("(p o) -> p o", o=1),
                             allow_slow_non_contiguous=True).then_inc(loaded, 16)
            sp.dma_start(w["w1"][:], io["W1"].rearrange("(t p) f -> p t f", p=P)).then_inc(loaded, 16)
            sp.dma_start(w["w2"][:], io["W2"].rearrange("(t p) f -> p t f", p=P)).then_inc(loaded, 16)
            sp.dma_start(w["b1c"][:], io["b1"].rearrange("(t p) -> p t", p=P), allow_slow_non_contiguous=True
                         ).then_inc(loaded, 16)
            sp.dma_start(w["b2_row"][:], io["b2"].rearrange("(o d) -> o d", o=1)).then_inc(loaded, 16)
            sp.dma_start(w["wr"][:], io["w_router"].rearrange("(t p) -> p t", p=P), allow_slow_non_contiguous=True
                         ).then_inc(loaded, 16)

        @blk.gpsimd
        def _(pool):
            pool.memset(w["mhalf2"][:], -0.5).then_inc(const_step, 1)
            pool.memset(w["one_row"][:], 1.0).then_inc(const_step, 1)
            pool.memset(w["before"][:], 1.0).then_inc(const_step, 1)
            pool.wait_ge(const_step, 3)
            pool.affine_select(out=w["before"][:], in_=w["before"][:], compare_op=ALU.is_ge, fill=0.0,
                               base=-1, pattern=[[-1, P]], channel_multiplier=1).then_inc(const_step, 1)

        @blk.tensor
        def _(pe):
            pe.wait_ge(loaded, 16 * (N_WO + 5))
            for hg in range(NG):
                for t in range(KT):
                    mm = pe.transpose(pt[hg // 2][:, hg % 2 * D + t * P:hg % 2 * D + (t + 1) * P],
                                      wop[:, t, hg * HB:(hg + 1) * HB].rearrange("p h c -> p (h c)"), w["ident"][:])
            mm.then_inc(turned, 1)

        @blk.vector
        def _(v):
            v.memset(wop[:], 0.0).then_inc(wo_zero, 1)
            v.wait_ge(turned, 1)
            for k in range(2):
                v.tensor_copy(w["woT"][:, 2 * k:2 * k + 2], pt[k][:, :].rearrange("p (g n) -> p g n", g=2))
            for kt in range(KT):
                v.tensor_copy(w["wr_bc"][:, kt], w["wr"][:, kt:kt + 1].broadcast_to([P, P]))


def ffn(nc, io, dr, out, w, nbatch=B):
    with ExitStack() as ctx:
        def sb(name, shape, dt=F32):
            return ctx.enter_context(nc.sbuf_tensor(name, shape, dt))

        def sem(name):
            return ctx.enter_context(nc.semaphore(name))

        RINGS = 4
        KB = TOPK // P
        cin = sb("cin", [P, NG, S])
        xin = sb("xin2", [P, NB, D])
        mrow = sb("mrow", [P, RINGS, 4, D])
        t1 = sb("t1", [P, CH])
        x1 = sb("x1", [P, RINGS, NB, D])
        h2 = sb("h2", [P, 2, NB, D])
        gh = sb("gh", [P, NB, D])
        hT = sb("hT2", [P, KT, S])
        sbc = sb("sbc", [P, S])
        pick = sb("pick", [P, NB, P])
        scol = sb("scol", [P, NB])
        th = sb("th", [P, NB])
        junk = sb("junk", [P, 2, 2, S])
        cnt = sb("cnt", [P, NB, 4])
        rank = sb("rank", [P, NB])
        near = sb("near", [P, NB])
        to_row = sb("to_row", [P, RINGS, NB], mybir.dt.uint32)
        from_row = sb("from_row", [P, RINGS, NB], mybir.dt.uint32)
        wm = sb("wm", [P, RINGS, NB])
        hs = sb("hs", [P, KB, D])
        hsT = sb("hsT", [P, KT, TOPK])
        gT = sb("gT", [P, FT, TOPK])
        ys = sb("ys", [P, KB, D])
        y = sb("y", [P, NB, D])
        stats = sb("stats2", [P, NB, 6])
        mv = sb("mv2", [P, NB, 2])
        veps, rstd, nmr = sb("veps2", [P, NB]), sb("rstd2", [P, NB]), sb("nmr2", [P, NB])
        bank = [ctx.enter_context(nc.psum_tensor(f"pf{i}", [P, CH], F32)) for i in range(8)]
        UP, DOWN = (0, 1), (4, 5)
        PROJ, TURN, SCORE = (2, 3, 6, 7), (6, 7), (2, 3)
        NF = NB // 2
        NT_H = KT * NC
        N_IDX = 16 * NB

        x_in2, c_in = sem("x_in2"), sem("c_in")
        mr_in = [sem(f"mr_in{i}") for i in range(RINGS)]
        x_used = sem("x_used")
        up_full, gelu_ok = sem("up_full"), sem("gelu_ok")
        proj_full, proj_free = sem("proj_full"), sem("proj_free")
        h2_ok, h2_used, x1_ok = sem("h2_ok"), sem("h2_used"), sem("x1_ok")
        turn_full, hT_ok = sem("turn_full"), sem("hT_ok")
        sc_full, sbc_ok, sbc_pe, sbc_free = sem("sc_full"), sem("sbc_ok"), sem("sbc_pe"), sem("sbc_free")
        scol_ok, th_ok, rank_ok = sem("scol_ok"), sem("th_ok"), sem("rank_ok")
        h_sorted, hs_in, hs_full, hsT_ok = sem("h_sorted"), sem("hs_in"), sem("hs_full"), sem("hsT_ok")
        down_full, down_free, ys_ok, ys_free = sem("down_full"), sem("down_free"), sem("ys_ok"), sem("ys_free")
        ys_out, y_in = sem("ys_out"), sem("y_in")
        y_ok, o_ok = sem("y_ok"), sem("o_ok")
        o_out = [sem(f"o_out{i}") for i in range(RINGS)]
        var_ok, rstd_ok = sem("var_ok2"), sem("rstd_ok2")
        dve_step, act_step, pool_step = sem("dve_step4"), sem("act_step4"), sem("pool_step4")
        blk = ctx.enter_context(nc.Block())

        def run_periods(eng, period):
            def known(k):
                period(k, k % RINGS, lambda n: 0 <= k - n < nbatch)
            for k in range(RINGS - 1):
                known(k)
            n = (nbatch - RINGS) // RINGS
            if n > 0:
                with eng.Fori(0, n) as turn:
                    for j in range(RINGS):
                        k = turn * RINGS + (RINGS - 1 + j)
                        period(k, (RINGS - 1 + j) % RINGS, lambda n: True)
            for k in range(RINGS - 1 + n * RINGS, nbatch + RINGS - 1):
                known(k)

        @blk.sync
        def _(sp):
            def load(b):
                sp.dma_start(xin[:], io["x"][bass.ds(b, 1)].rearrange("o (t p) d -> p (o t) d", p=P)).then_inc(x_in2, 16)
                sp.dma_start(cin[:], dr["ctx"][bass.ds(b * NG, NG)].rearrange("g p t -> p g t")).then_inc(c_in, 16)

            def load_rows(b, i):
                sp.dma_start(mrow[:, i].rearrange("p f d -> p (f d)"),
                             dr["mod_row"][bass.ds(b, 1)].broadcast_to([P, 4 * D])).then_inc(mr_in[i], 16)

            load(0)
            for b in range(RINGS):
                load_rows(b, b)

            def period(k, i, has):
                if has(1):
                    sp.wait_ge(h_sorted, k * N_IDX)
                    sp.sem_inc(h2_used, 1)
                    sp.dma_start(hs[:], dr["sorted"].rearrange("(t p) d -> p t d", p=P)).then_inc(hs_in, 16)
                if has(0) and has(-1):
                    sp.wait_ge(x_used, 1)
                    sp.sem_inc(x_used, -1)
                    load(k + 1)
                if has(3):
                    sp.wait_ge(o_ok, 1)
                    sp.sem_inc(o_ok, -1)
                    j = (i + 1) % RINGS
                    sp.dma_start(out[bass.ds(k - 3, 1)].rearrange("o (t p) d -> p (o t) d", p=P), x1[:, j]
                                 ).then_inc(o_out[j], 16)
                    if has(-1):
                        load_rows(k + 1, j)
                if has(2):
                    sp.wait_ge(ys_ok, 1)
                    sp.sem_inc(ys_ok, -1)
                    sp.dma_start(dr["ffn_sum"].rearrange("(t p) d -> p t d", p=P), ys[:]).then_inc(ys_out, 16)

            run_periods(sp, period)

        @blk.tensor
        def _(pe):
            def project():
                pe.wait_ge(c_in, 16)
                pe.sem_inc(c_in, -16)
                pe.wait_ge(sbc_pe, NC)
                pe.sem_inc(sbc_pe, -NC)
                for f in range(NF):
                    for k in range(2):
                        at = (2 * f + k) * P
                        for hg in range(NG):
                            mm = pe.matmul(bank[PROJ[f]][:, k * D:(k + 1) * D], cin[:, hg, at:at + P],
                                           w["woT"][:, hg], start=(hg == 0), stop=(hg == NG - 1))
                    mm.then_inc(proj_full, 1)

            def turn_and_score(b2):
                pe.wait_ge(h2_ok, 1)
                pe.sem_inc(h2_ok, -1)
                pe.wait_ge(proj_free, NF)
                pe.sem_inc(proj_free, -NF)
                for n in range(NT_H):
                    kt, half = n % KT, n // KT
                    if n >= 2:
                        pe.wait_ge(hT_ok, n - 1)
                    for t in range(4):
                        mm = pe.transpose(bank[TURN[n % 2]][:, t * P:(t + 1) * P],
                                          h2[:, b2, 4 * half + t, kt * P:(kt + 1) * P], w["ident"][:])
                    mm.then_inc(turn_full, 1)
                pe.wait_ge(hT_ok, NT_H)
                pe.sem_inc(hT_ok, -NT_H)
                for c in range(NC):
                    for kt in range(KT):
                        mm = pe.matmul(bank[SCORE[c]][:, :], w["wr_bc"][:, kt], hT[:, kt, c * CH:(c + 1) * CH],
                                       start=(kt == 0), stop=(kt == KT - 1))
                    mm.then_inc(sc_full, 1)

            def up():
                pe.wait_ge(hs_in, 16)
                pe.sem_inc(hs_in, -16)
                for kt in range(KT):
                    for t in range(KB):
                        mm = pe.transpose(bank[UP[kt]][:, t * P:(t + 1) * P], hs[:, t, kt * P:(kt + 1) * P],
                                          w["ident"][:])
                    mm.then_inc(hs_full, 1)
                pe.wait_ge(hsT_ok, KT)
                pe.sem_inc(hsT_ok, -KT)
                for ft in range(FT):
                    if ft >= 2:
                        pe.wait_ge(gelu_ok, ft - 1)
                    for kt in range(KT):
                        mm = pe.matmul(bank[UP[ft % 2]][:, :], w["w1"][:, kt, ft * P:(ft + 1) * P], hsT[:, kt],
                                       start=(kt == 0), stop=(kt == KT - 1))
                    mm.then_inc(up_full, 1)

            def down():
                pe.wait_ge(gelu_ok, FT)
                pe.sem_inc(gelu_ok, -FT)
                pe.wait_ge(down_free, KB // 2)
                pe.sem_inc(down_free, -(KB // 2))
                for f in range(KB // 2):
                    for k in range(2):
                        at, to = (2 * f + k) * P, bank[DOWN[f]][:, k * D:(k + 1) * D]
                        pe.matmul(to, w["one_row"][:], w["b2_row"][:], start=True, stop=False)
                        for ft in range(FT):
                            mm = pe.matmul(to, gT[:, ft, at:at + P], w["w2"][:, ft], start=False, stop=(ft == FT - 1))
                    mm.then_inc(down_full, 1)

            pe.sem_inc(down_free, KB // 2)
            pe.sem_inc(sbc_pe, NC)

            def period(k, i, has):
                if has(0):
                    project()
                if has(2):
                    down()
                if has(1):
                    up()
                if has(0):
                    turn_and_score(i % 2)

            run_periods(pe, period)

        @blk.scalar
        def _(act):
            def turned():
                for n in range(NT_H):
                    kt, half = n % KT, n // KT
                    act.wait_ge(turn_full, n + 1)
                    act.activation(hT[:, kt, half * CH:(half + 1) * CH], bank[TURN[n % 2]][:, :], ACT.Copy).then_inc(hT_ok, 1)
                act.sem_inc(turn_full, -NT_H)
                act.wait_ge(sbc_free, 1)
                act.sem_inc(sbc_free, -1)
                for c in range(NC):
                    act.wait_ge(sc_full, c + 1)
                    act.activation(sbc[:, c * CH:(c + 1) * CH], bank[SCORE[c]][:, :], ACT.Copy).then_inc(act_step, 1)
                    act.wait_ge(act_step, c + 1)
                    act.sem_inc(sbc_ok, 1)
                    act.sem_inc(sbc_pe, 1)
                act.sem_inc(act_step, -NC)
                act.sem_inc(sc_full, -NC)

            def sums_out():
                act.wait_ge(ys_free, 1)
                act.sem_inc(ys_free, -1)
                for f in range(KB // 2):
                    act.wait_ge(down_full, f + 1)
                    act.activation(ys[:, 2 * f:2 * f + 2].rearrange("p t d -> p (t d)"), bank[DOWN[f]][:, :], ACT.Copy
                                   ).then_inc(act_step, 1)
                    act.wait_ge(act_step, f + 1)
                    act.sem_inc(down_free, 1)
                act.sem_inc(down_full, -(KB // 2))
                act.sem_inc(act_step, -(KB // 2))
                act.sem_inc(ys_ok, 1)

            def gelus():
                for kt in range(KT):
                    act.wait_ge(hs_full, kt + 1)
                    act.activation(hsT[:, kt], bank[UP[kt]][:, :], ACT.Copy).then_inc(hsT_ok, 1)
                act.sem_inc(hs_full, -KT)
                for ft in range(FT):
                    act.wait_ge(up_full, ft + 1)
                    act.activation(gT[:, ft], bank[UP[ft % 2]][:, :], ACT.Gelu_apprx_tanh,
                                   bias=w["b1c"][:, ft:ft + 1]).then_inc(gelu_ok, 1)
                act.sem_inc(up_full, -FT)

            act.sem_inc(sbc_free, 1)
            act.sem_inc(ys_free, 1)

            def period(k, i, has):
                if has(1):
                    act.wait_ge(scol_ok, 1)
                    act.sem_inc(scol_ok, -1)
                    act.activation(th[:], scol[:], ACT.Tanh, scale=0.5).then_inc(th_ok, 1)
                if has(2):
                    sums_out()
                if has(1):
                    gelus()
                if has(0):
                    turned()

            run_periods(act, period)

        @blk.vector
        def _(v):
            steps = 0

            def go(ins):
                nonlocal steps
                steps += 1
                return ins.then_inc(dve_step, 1)

            def settle():
                v.wait_ge(dve_step, steps)

            def restart():
                nonlocal steps
                settle()
                v.sem_inc(dve_step, -steps)
                steps = 0

            def ranks(i):
                v.wait_ge(sbc_ok, NC)
                v.sem_inc(sbc_ok, -NC)
                go(v.tensor_tensor(pick[:], sbc[:].rearrange("p (t u) -> p t u", u=P),
                                   w["ident"][:].unsqueeze(1).broadcast_to([P, NB, P]), ALU.mult))
                settle()
                go(v.tensor_reduce(scol[:], pick[:], AX, ALU.add))
                settle()
                v.sem_inc(scol_ok, 1)
                done_before = [steps, steps]
                for t in range(NB):
                    s, lo, hi = scol[:, t:t + 1], t * P, (t + 1) * P
                    v.wait_ge(dve_step, done_before[t % 2])
                    a, b = junk[:, t % 2, 0], junk[:, t % 2, 1]
                    if lo:
                        go(v.tensor_scalar(a[:, 0:lo], sbc[:, 0:lo], s, 0.0, ALU.is_ge, ALU.add, accum_out=cnt[:, t, 0:1]))
                    if hi < S:
                        go(v.tensor_scalar(a[:, hi:S], sbc[:, hi:S], s, 0.0, ALU.is_gt, ALU.add, accum_out=cnt[:, t, 1:2]))
                    go(v.tensor_scalar(a[:, lo:hi], sbc[:, lo:hi], s, 0.0, ALU.is_gt, ALU.add, accum_out=cnt[:, t, 2:3]))
                    go(v.scalar_tensor_tensor(b[:, lo:hi], sbc[:, lo:hi], s, w["before"][:], ALU.is_equal, ALU.mult,
                                              accum_out=cnt[:, t, 3:4]))
                    done_before[t % 2] = steps
                settle()
                v.sem_inc(sbc_free, 1)
                go(v.tensor_reduce(rank[:], cnt[:], AX, ALU.add))
                settle()
                go(v.tensor_copy(to_row[:, i], rank[:]))
                go(v.tensor_scalar(near[:], rank[:], float(TOPK - 1), None, ALU.min))
                settle()
                go(v.tensor_copy(from_row[:, i], near[:]))
                go(v.tensor_scalar(rank[:], rank[:], float(TOPK), None, ALU.is_lt))
                settle()
                v.sem_inc(rank_ok, 1)
                v.wait_ge(th_ok, 1)
                v.sem_inc(th_ok, -1)
                go(v.tensor_scalar(wm[:, i], th[:], 0.5, 0.5, ALU.mult, ALU.add))
                settle()
                go(v.tensor_tensor(wm[:, i], wm[:, i], rank[:], ALU.mult))
                restart()

            def residual_and_norm(i):
                b2 = i % 2
                v.wait_ge(mr_in[i], 16)
                v.sem_inc(mr_in[i], -16)
                v.wait_ge(x_in2, 16)
                v.sem_inc(x_in2, -16)
                v.wait_ge(o_out[i], 16)
                v.sem_inc(o_out[i], -16)
                ga, sb_, cb = (mrow[:, i, n].unsqueeze(1) for n in range(3))
                for f in range(NF):
                    v.wait_ge(proj_full, f + 1)
                    go(v.tensor_tensor(t1[:].rearrange("p (t d) -> p t d", d=D),
                                       bank[PROJ[f]][:, :].rearrange("p (t d) -> p t d", d=D),
                                       ga.broadcast_to([P, 2, D]), ALU.mult))
                    settle()
                    v.sem_inc(proj_free, 1)
                    go(v.tensor_tensor(x1[:, i, 2 * f:2 * f + 2], t1[:].rearrange("p (t d) -> p t d", d=D),
                                       xin[:, 2 * f:2 * f + 2], ALU.add))
                    settle()
                    for t in (2 * f, 2 * f + 1):
                        go(v.bn_stats(stats[:, t], x1[:, i, t]))
                v.sem_inc(proj_full, -NF)
                v.sem_inc(x_used, 1)
                settle()
                for t in range(NB):
                    go(v.bn_aggr(mv[:, t], stats[:, t]))
                settle()
                v.tensor_scalar(veps[:], mv[:, :, 1], EPS, None, ALU.add).then_inc(var_ok, 1)
                v.wait_ge(rstd_ok, 1)
                v.sem_inc(rstd_ok, -1)
                go(v.scalar_tensor_tensor(nmr[:], mv[:, :, 0], -1.0, rstd[:], ALU.mult, ALU.mult))
                settle()
                v.wait_ge(h2_used, 1)
                v.sem_inc(h2_used, -1)
                for t in range(NB):
                    go(v.tensor_scalar(h2[:, b2, t], x1[:, i, t], rstd[:, t:t + 1], nmr[:, t:t + 1], ALU.mult, ALU.add))
                settle()
                go(v.tensor_tensor(h2[:, b2], h2[:, b2], cb.broadcast_to([P, NB, D]), ALU.mult))
                settle()
                go(v.tensor_tensor(h2[:, b2], h2[:, b2], sb_.broadcast_to([P, NB, D]), ALU.add))
                restart()
                v.sem_inc(h2_ok, 1)
                v.sem_inc(x1_ok, 1)

            def update(k, i):
                v.wait_ge(y_in, (k - 2) * N_IDX)
                for t in range(NB):
                    v.scalar_tensor_tensor(y[:, t], y[:, t], wm[:, i, t:t + 1], mrow[:, i, 3], ALU.mult, ALU.mult
                                           ).then_inc(y_ok, 1)

            for i in range(RINGS):
                v.sem_inc(o_out[i], 16)
            v.sem_inc(h2_used, 2)
            go(v.memset(cnt[:], 0.0))
            restart()

            def period(k, i, has):
                if has(1):
                    ranks((i - 1) % RINGS)
                if has(3):
                    update(k, (i - 3) % RINGS)
                if has(0):
                    residual_and_norm(i)

            run_periods(v, period)
            for i in range(RINGS):
                v.wait_ge(o_out[i], 16)

        @blk.gpsimd
        def _(pool):
            def residual(i):
                pool.wait_ge(x1_ok, 1)
                pool.sem_inc(x1_ok, -1)
                pool.tensor_tensor(gh[:], h2[:, i % 2], mrow[:, i, 3].unsqueeze(1).broadcast_to([P, NB, D]), ALU.mult
                                   ).then_inc(pool_step, 1)
                pool.wait_ge(pool_step, 1)
                pool.tensor_tensor(x1[:, i], x1[:, i], gh[:], ALU.add).then_inc(pool_step, 1)
                pool.wait_ge(pool_step, 2)
                pool.sem_inc(pool_step, -2)

            def scatter(i):
                pool.wait_ge(rank_ok, 1)
                pool.sem_inc(rank_ok, -1)
                for t in range(NB):
                    pool.indirect_dma_start(dr["sorted"], bass.IndirectOffsetOnAxis(ap=to_row[:, i, t:t + 1], axis=0),
                                            h2[:, i % 2, t], None, bounds_check=TOPK - 1, oob_is_err=False
                                            ).then_inc(h_sorted, 16)

            def root():
                pool.wait_ge(var_ok, 1)
                pool.sem_inc(var_ok, -1)
                pool.tensor_tensor(rstd[:], veps[:], w["mhalf2"][:], ALU.pow).then_inc(rstd_ok, 1)

            def result(i):
                pool.wait_ge(y_ok, NB)
                pool.sem_inc(y_ok, -NB)
                pool.tensor_tensor(x1[:, i], x1[:, i], y[:], ALU.add).then_inc(pool_step, 1)
                pool.wait_ge(pool_step, 1)
                pool.sem_inc(pool_step, -1)
                pool.sem_inc(o_ok, 1)

            def fetch(i):
                pool.wait_ge(ys_out, 16)
                pool.sem_inc(ys_out, -16)
                pool.sem_inc(ys_free, 1)
                for t in range(NB):
                    pool.indirect_dma_start(y[:, t], None, dr["ffn_sum"],
                                            bass.IndirectOffsetOnAxis(ap=from_row[:, i, t:t + 1], axis=0)
                                            ).then_inc(y_in, 16)

            def period(k, i, has):
                if has(1):
                    residual((i - 1) % RINGS)
                    scatter((i - 1) % RINGS)
                if has(0):
                    root()
                if has(3):
                    result((i - 3) % RINGS)
                if has(2):
                    fetch((i - 2) % RINGS)

            run_periods(pool, period)


def build(nc, io, out, nbatch=B):
    dr = scratch(nc)
    with ExitStack() as ctx:
        ident = ctx.enter_context(nc.sbuf_tensor("ident", [P, P], F32))
        with ExitStack() as c1:
            def sb(name, shape, dt=F32):
                return c1.enter_context(nc.sbuf_tensor(name, shape, dt))
            w = dict(ident=ident, mhalf=sb("mhalf", [P, NB]), rk_bc=sb("rk_bc", [P, 2, DK]), 
                     rk_col=sb("rk_col", [P, 1]), wqT=sb("wqT", [P, KT, D]), wkT=sb("wkT", [P, KT, D]),
                     wvT=sb("wvT", [P, KT, D]), wcT=sb("wcT", [P, KT, H]))
            setup_project(nc, io, dr, w)
            project(nc, io, dr, w, nbatch)
        with ExitStack() as c2:
            def sb(name, shape, dt=F32):
                return c2.enter_context(nc.sbuf_tensor(name, shape, dt))
            w = dict(ident=ident, identb=sb("identb", [P, P], BF16), qpk=sb("qpk", [C_ROWS, 3, HB * S], BF16),
                     kpk=sb("kpk", [C_ROWS, 3, HB * S], BF16), rkp=sb("rkp", [ROWS, TA + TB], BF16),
                     rvt=sb("rvt", [P, XW, DK]), rvb=sb("rvb", [P, 2, DK]), spread=sb("spread", [HB, P]))
            setup_attend(nc, io, dr, w)
            attend(nc, dr, w, nbatch * NG)
        with ExitStack() as c3:
            def sb(name, shape, dt=F32):
                return c3.enter_context(nc.sbuf_tensor(name, shape, dt))
            w = dict(ident=ident, mhalf2=sb("mhalf2", [P, NB]), before=sb("before", [P, P]), woT=sb("woT", [P, NG, D]),
                     w1=sb("w1", [P, KT, F]), w2=sb("w2", [P, FT, D]), b1c=sb("b1c", [P, FT]), b2_row=sb("b2_row", [1, D]),
                     one_row=sb("one_row", [1, P]),
                     wr=sb("wr", [P, KT]), wr_bc=sb("wr_bc", [P, KT, P]))
            setup_ffn(nc, io, w)
            ffn(nc, io, dr, out, w, nbatch)


_INS = {"x": "L0_attn_x", "Wq": "L0_attn_Wq", "Wk": "L0_attn_Wk", "Wv": "L0_attn_Wv", "Wo": "L0_attn_Wo",
        "b_o": "L0_attn_b_o", "rel_k": "L0_attn_rel_k_emb", "rel_v": "L0_attn_rel_v_emb",
        "w_router": "L0_ffn_w_router", "W1": "L0_ffn_W1", "b1": "L0_ffn_b1", "W2": "L0_ffn_W2",
        "b2": "L0_ffn_b2", "c": "L0_c", "wmod": "L0_wmod"}


def kernel(**inputs):
    import numpy as _np
    import concourse.bacc as _bacc
    from concourse.bass_utils import run_bass_kernel_spmd as _run

    nc = _bacc.Bacc("TRN2", target_bir_lowering=False, num_devices=1)
    arrays, io = {}, {}
    for short, name in _INS.items():
        a = _np.ascontiguousarray(inputs[name])
        arrays[f"in_{name}_dram"] = a
        io[short] = nc.dram_tensor(f"in_{name}_dram", a.shape, mybir.dt.from_np(a.dtype), kind="ExternalInput").ap()
    out = nc.dram_tensor("out_0_dram", (B, S, D), F32, kind="ExternalOutput").ap()
    build(nc, io, out)
    return _run(nc, [arrays], core_ids=[0]).results[0]["out_0_dram"]
```
